# Optimizing a Trainium2 kernel written in Bass

```python
import numpy as np
import jax
import jax.numpy as jnp

def _softmax(x, axis=-1):
    return jax.nn.softmax(x, axis=axis)

def _gelu(x):
    return jax.nn.gelu(x, approximate=True)

def _silu(x):
    return jax.nn.silu(x)

def _sigmoid(x):
    return jax.nn.sigmoid(x)

def _layernorm(x, axis=-1, eps=1e-05):
    m = jnp.mean(x, axis=axis, keepdims=True)
    v = jnp.var(x, axis=axis, keepdims=True)
    return (x - m) / jnp.sqrt(v + eps)

def _scatter_add(tgt, idx, src, axis=0):
    return tgt.at[idx].add(src)

def _segment_sum(src, seg, n):
    return jax.ops.segment_sum(src, seg, n)
kernel_name = 'mk_gps_d2_gnn_r16_e8c618'

def setup_inputs(seed: int=0):
    np.random.seed(seed)
    _w = jnp.asarray

    def _rec_inputs():
        import jax
        import jax.numpy as jnp
        _gk = jax.random.key(seed)
        x = -0.0003713 + 1 * jax.random.normal(jax.random.fold_in(_gk, 1), (3125, 256), jnp.float32)
        src = jax.random.randint(jax.random.fold_in(_gk, 2), (100000,), 0, 3125, jnp.int32)
        dst = jnp.minimum((3125 * jax.random.uniform(jax.random.fold_in(_gk, 3), (100000,)) ** 2.0).astype(jnp.int32), 49999)
        _o = jnp.argsort(dst, stable=True)
        src = src[_o]
        dst = dst[_o]
        edge_type_64 = jax.random.randint(jax.random.fold_in(_gk, 13), (100000,), 0, 64, jnp.int32)
        edge_weight = jax.random.uniform(jax.random.fold_in(_gk, 14), (100000,), jnp.float32, 0.0, 0.999998)
        edge_weight_n2 = jax.random.uniform(jax.random.fold_in(_gk, 15), (100000,), jnp.float32, 0.0, 0.999998)
        return (x, src, dst, edge_type_64, edge_weight, edge_weight_n2)
    x, src, dst, edge_type_64, edge_weight, edge_weight_n2 = _rec_inputs()

    def _L0_gnn_setup():
        import jax, jax.numpy as jnp
        import numpy as np
        N_NODES = 3125
        N_EDGES = 31250
        IN_DIM = 256
        HID = 64
        HEADS = 4
        N_REL = 64
        key = jax.random.key(seed)
        ks = jax.random.split(key, 16)
        s = 0.02
        return {'node_features': jax.random.normal(ks[0], (N_NODES, IN_DIM), jnp.float32), 'edge_index': jax.random.randint(ks[1], (2, N_EDGES), 0, N_NODES, jnp.int32), 'edge_relations': jax.random.randint(ks[2], (N_EDGES,), 0, N_REL, jnp.int32), 'query_emb': jax.random.normal(ks[3], (IN_DIM,), jnp.float32), 'Wq': jax.random.normal(ks[4], (IN_DIM, HID * HEADS), jnp.float32) * s, 'bq': jnp.zeros((HID * HEADS,), jnp.float32), 'Wk': jax.random.normal(ks[5], (IN_DIM, HID * HEADS), jnp.float32) * s, 'bk': jnp.zeros((HID * HEADS,), jnp.float32), 'Wv': jax.random.normal(ks[6], (IN_DIM, HID * HEADS), jnp.float32) * s, 'bv': jnp.zeros((HID * HEADS,), jnp.float32), 'rel_w': jax.random.normal(ks[7], (N_REL, HID), jnp.float32) * s, 'Wo': jax.random.normal(ks[8], (HID * HEADS, IN_DIM), jnp.float32) * s, 'bo': jnp.zeros((IN_DIM,), jnp.float32), 'gamma': jnp.ones((IN_DIM,), jnp.float32), 'beta': jnp.zeros((IN_DIM,), jnp.float32)}
    _L0_gnn_all = _L0_gnn_setup()
    _L0_gnn_in = {k: v for k, v in _L0_gnn_all.items() if k in ('query_emb', 'Wq', 'bq', 'Wk', 'bk', 'Wv', 'bv', 'rel_w', 'Wo', 'bo', 'gamma', 'beta')}
    del _L0_gnn_all

    def _L0_mix_setup():
        import jax, jax.numpy as jnp
        import numpy as np
        EMB, HEADS, DEPTH, SEQ, BATCH = (256, 8, 4, 512, 4)
        DH = EMB // HEADS
        FF = 4 * EMB
        EPS = 1e-05

        def _layernorm(x, g, b):
            mu = x.mean(-1, keepdims=True)
            var = ((x - mu) ** 2).mean(-1, keepdims=True)
            return (x - mu) * jax.lax.rsqrt(var + EPS) * g + b

        def _linear_attn(x, Wq, Wk, Wv, Wo, bo):
            b, n, dm = x.shape
            split = lambda t: t.reshape(b, n, HEADS, DH).transpose(0, 2, 1, 3)
            scale = DH ** (-0.25)
            q = jax.nn.softmax(split(x @ Wq) * scale, axis=-1)
            k = jax.nn.softmax(split(x @ Wk) * scale, axis=-2)
            v = split(x @ Wv)
            context = jnp.einsum('bhnd,bhne->bhde', k, v)
            out = jnp.einsum('bhnd,bhde->bhne', q, context)
            out = out.transpose(0, 2, 1, 3).reshape(b, n, dm)
            return out @ Wo + bo

        def _forward(x, Wq, Wk, Wv, Wo, bo, ln1_g, ln1_b, W1, b1, W2, b2, ln2_g, ln2_b):
            for i in range(DEPTH):
                h = _layernorm(x, ln1_g[i], ln1_b[i])
                x = x + _linear_attn(h, Wq[i], Wk[i], Wv[i], Wo[i], bo[i])
                h = _layernorm(x, ln2_g[i], ln2_b[i])
                x = x + (jax.nn.gelu(h @ W1[i] + b1[i], approximate=False) @ W2[i] + b2[i])
            return x
        key = jax.random.key(seed)
        ks = jax.random.split(key, 8)
        w = lambda k, shape: jax.random.normal(k, shape, dtype=jnp.float32) * 0.02
        D = DEPTH
        return {'x': jax.random.normal(ks[0], (BATCH, SEQ, EMB), dtype=jnp.float32), 'Wq': w(ks[1], (D, EMB, EMB)), 'Wk': w(ks[2], (D, EMB, EMB)), 'Wv': w(ks[3], (D, EMB, EMB)), 'Wo': w(ks[4], (D, EMB, EMB)), 'bo': jnp.zeros((D, EMB), jnp.float32), 'ln1_g': jnp.ones((D, EMB), jnp.float32), 'ln1_b': jnp.zeros((D, EMB), jnp.float32), 'W1': w(ks[5], (D, EMB, FF)), 'b1': jnp.zeros((D, FF), jnp.float32), 'W2': w(ks[6], (D, FF, EMB)), 'b2': jnp.zeros((D, EMB), jnp.float32), 'ln2_g': jnp.ones((D, EMB), jnp.float32), 'ln2_b': jnp.zeros((D, EMB), jnp.float32)}
    _L0_mix_all = _L0_mix_setup()
    _L0_mix_in = {k: v for k, v in _L0_mix_all.items() if k in ('Wq', 'Wk', 'Wv', 'Wo', 'bo', 'ln1_g', 'ln1_b', 'W1', 'b1', 'W2', 'b2', 'ln2_g', 'ln2_b')}
    del _L0_mix_all

    def _L0_ffn_setup():
        import jax, jax.numpy as jnp
        import numpy as np
        D_MODEL = 256
        N_EXPERTS = 16
        HIDDEN = 512
        SCALE = 0.02
        key = jax.random.key(seed)
        ks = jax.random.split(key, 5)
        x = jax.random.normal(ks[0], (4, 512, D_MODEL), dtype=jnp.float32)
        gate_w = jax.random.normal(ks[1], (D_MODEL, N_EXPERTS), dtype=jnp.float32) * SCALE
        gate_b = jnp.zeros((N_EXPERTS,), dtype=jnp.float32)
        w1 = jax.random.normal(ks[2], (N_EXPERTS, D_MODEL, HIDDEN), dtype=jnp.float32) * SCALE
        w2 = jax.random.normal(ks[3], (N_EXPERTS, D_MODEL, HIDDEN), dtype=jnp.float32) * SCALE
        w3 = jax.random.normal(ks[4], (N_EXPERTS, HIDDEN, D_MODEL), dtype=jnp.float32) * SCALE
        return {'x': x, 'gate_w': gate_w, 'gate_b': gate_b, 'w1': w1, 'w2': w2, 'w3': w3}
    _L0_ffn_all = _L0_ffn_setup()
    _L0_ffn_in = {k: v for k, v in _L0_ffn_all.items() if k in ('gate_w', 'gate_b', 'w1', 'w2', 'w3')}
    del _L0_ffn_all

    def _L1_gnn_setup():
        import jax, jax.numpy as jnp
        import numpy as np
        N_NODES = 6250
        N_EDGES = 50000
        DIM = 256
        EPS = 1e-05
        key = jax.random.key(seed)
        ks = jax.random.split(key, 12)
        H = DIM
        s = 1.0 / np.sqrt(H)
        s2 = 1.0 / np.sqrt(2 * H)
        return {'feat': jax.random.normal(ks[0], (N_NODES, DIM), dtype=jnp.float32), 'src': jax.random.randint(ks[1], (N_EDGES,), 0, N_NODES, dtype=jnp.int32), 'dst': jax.random.randint(ks[2], (N_EDGES,), 0, N_NODES, dtype=jnp.int32), 'iw': jax.random.uniform(ks[3], (N_EDGES,), dtype=jnp.float32), 'ow': jax.random.uniform(ks[4], (N_EDGES,), dtype=jnp.float32), 'gamma': jnp.ones((DIM,), jnp.float32), 'beta': jnp.zeros((DIM,), jnp.float32), 'W_in': jax.random.uniform(ks[5], (H, H), jnp.float32, -s, s), 'b_in': jax.random.uniform(ks[6], (H,), jnp.float32, -s, s), 'W_out': jax.random.uniform(ks[7], (H, H), jnp.float32, -s, s), 'b_out': jax.random.uniform(ks[8], (H,), jnp.float32, -s, s), 'W_x2i': jax.random.uniform(ks[9], (2 * H, 2 * H), jnp.float32, -s2, s2), 'b_x2i': jax.random.uniform(ks[10], (2 * H,), jnp.float32, -s2, s2), 'W_h2h': jax.random.uniform(ks[11], (H, 2 * H), jnp.float32, -s, s)}
    _L1_gnn_all = _L1_gnn_setup()
    _L1_gnn_in = {k: v for k, v in _L1_gnn_all.items() if k in ('gamma', 'beta', 'W_in', 'b_in', 'W_out', 'b_out', 'W_x2i', 'b_x2i', 'W_h2h')}
    del _L1_gnn_all

    def _L1_mix_setup():
        import jax, jax.numpy as jnp
        import numpy as np
        HEADS = 8
        DIM_HEAD = 64
        EPS = 1e-05

        def _inst_norm_lastdim(t):
            mu = jnp.mean(t, axis=-1, keepdims=True)
            var = jnp.mean(jnp.square(t - mu), axis=-1, keepdims=True)
            return (t - mu) * jax.lax.rsqrt(var + EPS)
        key = jax.random.key(seed)
        k1, k2, k3, k4 = jax.random.split(key, 4)
        b, n, dim = (4, 512, 256)
        inner = HEADS * DIM_HEAD
        x = jax.random.normal(k1, (b, n, dim), dtype=jnp.float32)
        Wqkv = jax.random.normal(k2, (3 * inner, dim), dtype=jnp.float32) * (1.0 / np.sqrt(dim))
        Wout = jax.random.normal(k3, (dim, inner), dtype=jnp.float32) * (1.0 / np.sqrt(inner))
        bout = jax.random.normal(k4, (dim,), dtype=jnp.float32) * 0.01
        return {'x': x, 'Wqkv': Wqkv, 'Wout': Wout, 'bout': bout}
    _L1_mix_all = _L1_mix_setup()
    _L1_mix_in = {k: v for k, v in _L1_mix_all.items() if k in ('Wqkv', 'Wout', 'bout')}
    del _L1_mix_all

    def _L1_ffn_setup():
        import jax, jax.numpy as jnp
        import numpy as np
        B, S, D = (8, 256, 256)
        H = 4 * D
        CAPACITY = 0.5
        key = jax.random.key(seed)
        ks = jax.random.split(key, 6)
        x = jax.random.normal(ks[0], (B, S, D), dtype=jnp.float32)
        attention_mask = jnp.zeros((B, 1, 1, S), dtype=jnp.float32)
        wr = jax.random.normal(ks[1], (D, 1), dtype=jnp.float32) * 0.02
        br = jnp.zeros((1,), dtype=jnp.float32)
        w1 = jax.random.normal(ks[2], (D, H), dtype=jnp.float32) * 0.02
        b1 = jnp.zeros((H,), dtype=jnp.float32)
        w2 = jax.random.normal(ks[3], (H, D), dtype=jnp.float32) * 0.02
        b2 = jnp.zeros((D,), dtype=jnp.float32)
        return {'x': x, 'attention_mask': attention_mask, 'wr': wr, 'br': br, 'w1': w1, 'b1': b1, 'w2': w2, 'b2': b2}
    _L1_ffn_all = _L1_ffn_setup()
    _L1_ffn_in = {k: v for k, v in _L1_ffn_all.items() if k in ('attention_mask', 'wr', 'br', 'w1', 'b1', 'w2', 'b2')}
    del _L1_ffn_all
    return {'x': x, 'src': src, 'dst': dst, 'edge_type_64': edge_type_64, 'edge_weight': edge_weight, 'edge_weight_n2': edge_weight_n2, 'L0_gnn_query_emb': _L0_gnn_in['query_emb'], 'L0_gnn_Wq': _L0_gnn_in['Wq'], 'L0_gnn_bq': _L0_gnn_in['bq'], 'L0_gnn_Wk': _L0_gnn_in['Wk'], 'L0_gnn_bk': _L0_gnn_in['bk'], 'L0_gnn_Wv': _L0_gnn_in['Wv'], 'L0_gnn_bv': _L0_gnn_in['bv'], 'L0_gnn_rel_w': _L0_gnn_in['rel_w'], 'L0_gnn_Wo': _L0_gnn_in['Wo'], 'L0_gnn_bo': _L0_gnn_in['bo'], 'L0_gnn_gamma': _L0_gnn_in['gamma'], 'L0_gnn_beta': _L0_gnn_in['beta'], 'L0_mix_Wq': _L0_mix_in['Wq'], 'L0_mix_Wk': _L0_mix_in['Wk'], 'L0_mix_Wv': _L0_mix_in['Wv'], 'L0_mix_Wo': _L0_mix_in['Wo'], 'L0_mix_bo': _L0_mix_in['bo'], 'L0_mix_ln1_g': _L0_mix_in['ln1_g'], 'L0_mix_ln1_b': _L0_mix_in['ln1_b'], 'L0_mix_W1': _L0_mix_in['W1'], 'L0_mix_b1': _L0_mix_in['b1'], 'L0_mix_W2': _L0_mix_in['W2'], 'L0_mix_b2': _L0_mix_in['b2'], 'L0_mix_ln2_g': _L0_mix_in['ln2_g'], 'L0_mix_ln2_b': _L0_mix_in['ln2_b'], 'L0_ffn_gate_w': _L0_ffn_in['gate_w'], 'L0_ffn_gate_b': _L0_ffn_in['gate_b'], 'L0_ffn_w1': _L0_ffn_in['w1'], 'L0_ffn_w2': _L0_ffn_in['w2'], 'L0_ffn_w3': _L0_ffn_in['w3'], 'L1_gnn_gamma': _L1_gnn_in['gamma'], 'L1_gnn_beta': _L1_gnn_in['beta'], 'L1_gnn_W_in': _L1_gnn_in['W_in'], 'L1_gnn_b_in': _L1_gnn_in['b_in'], 'L1_gnn_W_out': _L1_gnn_in['W_out'], 'L1_gnn_b_out': _L1_gnn_in['b_out'], 'L1_gnn_W_x2i': _L1_gnn_in['W_x2i'], 'L1_gnn_b_x2i': _L1_gnn_in['b_x2i'], 'L1_gnn_W_h2h': _L1_gnn_in['W_h2h'], 'L1_mix_Wqkv': _L1_mix_in['Wqkv'], 'L1_mix_Wout': _L1_mix_in['Wout'], 'L1_mix_bout': _L1_mix_in['bout'], 'L1_ffn_attention_mask': _L1_ffn_in['attention_mask'], 'L1_ffn_wr': _L1_ffn_in['wr'], 'L1_ffn_br': _L1_ffn_in['br'], 'L1_ffn_w1': _L1_ffn_in['w1'], 'L1_ffn_b1': _L1_ffn_in['b1'], 'L1_ffn_w2': _L1_ffn_in['w2'], 'L1_ffn_b2': _L1_ffn_in['b2']}

def reference(x, src, dst, edge_type_64, edge_weight, edge_weight_n2, L0_gnn_query_emb, L0_gnn_Wq, L0_gnn_bq, L0_gnn_Wk, L0_gnn_bk, L0_gnn_Wv, L0_gnn_bv, L0_gnn_rel_w, L0_gnn_Wo, L0_gnn_bo, L0_gnn_gamma, L0_gnn_beta, L0_mix_Wq, L0_mix_Wk, L0_mix_Wv, L0_mix_Wo, L0_mix_bo, L0_mix_ln1_g, L0_mix_ln1_b, L0_mix_W1, L0_mix_b1, L0_mix_W2, L0_mix_b2, L0_mix_ln2_g, L0_mix_ln2_b, L0_ffn_gate_w, L0_ffn_gate_b, L0_ffn_w1, L0_ffn_w2, L0_ffn_w3, L1_gnn_gamma, L1_gnn_beta, L1_gnn_W_in, L1_gnn_b_in, L1_gnn_W_out, L1_gnn_b_out, L1_gnn_W_x2i, L1_gnn_b_x2i, L1_gnn_W_h2h, L1_mix_Wqkv, L1_mix_Wout, L1_mix_bout, L1_ffn_attention_mask, L1_ffn_wr, L1_ffn_br, L1_ffn_w1, L1_ffn_b1, L1_ffn_w2, L1_ffn_b2):
    import jax
    import jax.numpy as jnp

    def _L0_gnn_ref(node_features, edge_index, edge_relations, query_emb, Wq, bq, Wk, bk, Wv, bv, rel_w, Wo, bo, gamma, beta):
        import jax, jax.numpy as jnp
        import numpy as np
        N_NODES = 3125
        N_EDGES = 31250
        IN_DIM = 256
        HID = 64
        HEADS = 4
        N_REL = 64
        N = node_features.shape[0]
        D = rel_w.shape[1]
        H = Wq.shape[1] // D
        enh = node_features + 0.1 * query_emb[None, :]
        Q = (enh @ Wq + bq).reshape(N, H, D)
        K = (enh @ Wk + bk).reshape(N, H, D)
        V = (enh @ Wv + bv).reshape(N, H, D)
        src, dst = (edge_index[0], edge_index[1])
        rel = rel_w[edge_relations]
        mod_k = K[src] + 0.2 * rel[:, None, :]
        scores = jnp.einsum('ehd,ehd->eh', Q[dst], mod_k) / D ** 0.5
        seg_max = jax.ops.segment_max(scores, dst, num_segments=N)
        ex = jnp.exp(scores - seg_max[dst])
        denom = jax.ops.segment_sum(ex, dst, num_segments=N)
        w = ex / denom[dst]
        agg = jax.ops.segment_sum(w[:, :, None] * V[src], dst, num_segments=N)
        deg = jax.ops.segment_sum(jnp.ones((src.shape[0],), jnp.float32), dst, num_segments=N)
        msgs = jnp.where(deg[:, None, None] > 0, agg, V)
        out = msgs.reshape(N, H * D) @ Wo + bo
        x = out + node_features
        mu = jnp.mean(x, axis=-1, keepdims=True)
        var = jnp.var(x, axis=-1, keepdims=True)
        return (x - mu) / jnp.sqrt(var + 1e-05) * gamma + beta

    def _L0_mix_ref(x, Wq, Wk, Wv, Wo, bo, ln1_g, ln1_b, W1, b1, W2, b2, ln2_g, ln2_b):
        import jax, jax.numpy as jnp
        import numpy as np
        EMB, HEADS, DEPTH, SEQ, BATCH = (256, 8, 4, 512, 4)
        DH = EMB // HEADS
        FF = 4 * EMB
        EPS = 1e-05

        def _layernorm(x, g, b):
            mu = x.mean(-1, keepdims=True)
            var = ((x - mu) ** 2).mean(-1, keepdims=True)
            return (x - mu) * jax.lax.rsqrt(var + EPS) * g + b

        def _linear_attn(x, Wq, Wk, Wv, Wo, bo):
            b, n, dm = x.shape
            split = lambda t: t.reshape(b, n, HEADS, DH).transpose(0, 2, 1, 3)
            scale = DH ** (-0.25)
            q = jax.nn.softmax(split(x @ Wq) * scale, axis=-1)
            k = jax.nn.softmax(split(x @ Wk) * scale, axis=-2)
            v = split(x @ Wv)
            context = jnp.einsum('bhnd,bhne->bhde', k, v)
            out = jnp.einsum('bhnd,bhde->bhne', q, context)
            out = out.transpose(0, 2, 1, 3).reshape(b, n, dm)
            return out @ Wo + bo

        def _forward(x, Wq, Wk, Wv, Wo, bo, ln1_g, ln1_b, W1, b1, W2, b2, ln2_g, ln2_b):
            for i in range(DEPTH):
                h = _layernorm(x, ln1_g[i], ln1_b[i])
                x = x + _linear_attn(h, Wq[i], Wk[i], Wv[i], Wo[i], bo[i])
                h = _layernorm(x, ln2_g[i], ln2_b[i])
                x = x + (jax.nn.gelu(h @ W1[i] + b1[i], approximate=False) @ W2[i] + b2[i])
            return x
        return _forward(x, Wq, Wk, Wv, Wo, bo, ln1_g, ln1_b, W1, b1, W2, b2, ln2_g, ln2_b)

    def _L0_ffn_ref(x, gate_w, gate_b, w1, w2, w3):
        import jax, jax.numpy as jnp
        import numpy as np
        D_MODEL = 256
        N_EXPERTS = 16
        HIDDEN = 512
        SCALE = 0.02
        n_experts = w1.shape[0]
        logits = jnp.einsum('bsd,de->bse', x, gate_w) + gate_b
        probs = jax.nn.softmax(logits, axis=-1)
        top_probs, top_idx = jax.lax.top_k(probs, 2)
        top_probs = top_probs / jnp.sum(top_probs, axis=-1, keepdims=True)
        dispatch = jnp.sum(jax.nn.one_hot(top_idx, n_experts, dtype=x.dtype) * top_probs[..., None], axis=-2)
        h1 = jnp.einsum('bsd,edh->bseh', x, w1)
        h2 = jnp.einsum('bsd,edh->bseh', x, w2)
        hidden = jax.nn.silu(h1) * h2
        expert_out = jnp.einsum('bseh,eho->bseo', hidden, w3)
        return jnp.einsum('bseo,bse->bso', expert_out, dispatch)

    def _L1_gnn_ref(feat, src, dst, iw, ow, gamma, beta, W_in, b_in, W_out, b_out, W_x2i, b_x2i, W_h2h):
        import jax, jax.numpy as jnp
        import numpy as np
        N_NODES = 6250
        N_EDGES = 50000
        DIM = 256
        EPS = 1e-05
        N = feat.shape[0]
        num_steps = 1
        mean = jnp.mean(feat, axis=0)
        var = jnp.var(feat, axis=0)
        h = (feat - mean) * jax.lax.rsqrt(var + EPS) * gamma + beta
        for _ in range(num_steps):
            feat_in = h @ W_in + b_in
            feat_out = h @ W_out + b_out
            a_in = jax.ops.segment_sum(feat_in[src] * iw[:, None], dst, num_segments=N)
            a_out = jax.ops.segment_sum(feat_out[dst] * ow[:, None], src, num_segments=N)
            a = jnp.concatenate((a_in, a_out), axis=1)
            xi = a @ W_x2i + b_x2i
            hh = h @ W_h2h
            i_i, i_n = jnp.split(xi, 2, axis=1)
            h_i, h_n = jnp.split(hh, 2, axis=1)
            input_gate = jax.nn.sigmoid(i_i + h_i)
            new_gate = jnp.tanh(i_n + h_n)
            h = new_gate + input_gate * (h - new_gate)
        return h

    def _L1_mix_ref(x, Wqkv, Wout, bout):
        import jax, jax.numpy as jnp
        import numpy as np
        HEADS = 8
        DIM_HEAD = 64
        EPS = 1e-05

        def _inst_norm_lastdim(t):
            mu = jnp.mean(t, axis=-1, keepdims=True)
            var = jnp.mean(jnp.square(t - mu), axis=-1, keepdims=True)
            return (t - mu) * jax.lax.rsqrt(var + EPS)
        b, n, dim = x.shape
        qkv = jnp.einsum('bnc,fc->bnf', x, Wqkv)
        q, k, v = jnp.split(qkv, 3, axis=-1)

        def to_heads(t):
            return t.reshape(b, n, HEADS, DIM_HEAD).transpose(0, 2, 1, 3)
        q, k, v = (to_heads(q), to_heads(k), to_heads(v))
        k = _inst_norm_lastdim(k)
        v = _inst_norm_lastdim(v)
        dots = jnp.einsum('bhnd,bhne->bhde', k, v)
        out = jnp.einsum('bhnd,bhde->bhne', q, dots) / n
        out = out.transpose(0, 2, 1, 3).reshape(b, n, HEADS * DIM_HEAD)
        return jnp.einsum('bnf,cf->bnc', out, Wout) + bout

    def _L1_ffn_ref(x, attention_mask, wr, br, w1, b1, w2, b2):
        import jax, jax.numpy as jnp
        import numpy as np
        B, S, D = (8, 256, 256)
        H = 4 * D
        CAPACITY = 0.5
        b, s, d = x.shape
        weights = (jnp.einsum('bsd,do->bso', x, wr) + br)[..., 0]
        k = max(1, int(CAPACITY * s))
        kk = k - 1 if k > 1 else 1
        _, idx = jax.lax.top_k(weights, k)
        sel_idx = idx[:, :kk]
        sel = jnp.take_along_axis(x, sel_idx[:, :, None], axis=1)
        h = jax.nn.gelu(jnp.einsum('bkd,dh->bkh', sel, w1) + b1)
        y = jnp.einsum('bkh,hd->bkd', h, w2) + b2
        w_sel = jnp.take_along_axis(weights, sel_idx, axis=1)
        y = y * w_sel[..., None]
        batch_idx = jnp.arange(b)[:, None]
        processed = jnp.zeros_like(x).at[batch_idx, sel_idx].set(y)
        return processed + x
    edge_index = jnp.stack([src, dst])
    xn = _layernorm(x, axis=-1)
    x = x + _L0_gnn_ref(xn, edge_index, edge_type_64, L0_gnn_query_emb, L0_gnn_Wq, L0_gnn_bq, L0_gnn_Wk, L0_gnn_bk, L0_gnn_Wv, L0_gnn_bv, L0_gnn_rel_w, L0_gnn_Wo, L0_gnn_bo, L0_gnn_gamma, L0_gnn_beta) + _L0_mix_ref(xn[None], L0_mix_Wq, L0_mix_Wk, L0_mix_Wv, L0_mix_Wo, L0_mix_bo, L0_mix_ln1_g, L0_mix_ln1_b, L0_mix_W1, L0_mix_b1, L0_mix_W2, L0_mix_b2, L0_mix_ln2_g, L0_mix_ln2_b)[0]
    x = x + _L0_ffn_ref(_layernorm(x, axis=-1)[None], L0_ffn_gate_w, L0_ffn_gate_b, L0_ffn_w1, L0_ffn_w2, L0_ffn_w3)[0]
    xn = _layernorm(x, axis=-1)
    x = x + _L1_gnn_ref(xn, src, dst, edge_weight, edge_weight_n2, L1_gnn_gamma, L1_gnn_beta, L1_gnn_W_in, L1_gnn_b_in, L1_gnn_W_out, L1_gnn_b_out, L1_gnn_W_x2i, L1_gnn_b_x2i, L1_gnn_W_h2h) + _L1_mix_ref(xn[None], L1_mix_Wqkv, L1_mix_Wout, L1_mix_bout)[0]
    x = x + _L1_ffn_ref(_layernorm(x, axis=-1)[None], L1_ffn_attention_mask, L1_ffn_wr, L1_ffn_br, L1_ffn_w1, L1_ffn_b1, L1_ffn_w2, L1_ffn_b2)[0]
    return x

_drawn_inputs = setup_inputs


def setup_inputs(seed=0):
    import zlib

    import numpy as np

    out = dict(_drawn_inputs(seed))
    spreads = {'L0_gnn_bq': (0.0, 0.8),
     'L0_gnn_bk': (0.0, 2.0),
     'L0_gnn_bv': (0.0, 0.8),
     'L0_gnn_bo': (0.0, 0.273),
     'L0_gnn_gamma': (1.0, 0.2),
     'L0_gnn_beta': (0.0, 0.1),
     'L0_mix_bo': (0.0, 0.1),
     'L0_mix_ln1_g': (1.0, 0.6),
     'L0_mix_ln1_b': (0.0, 0.8),
     'L0_mix_b1': (0.0, 0.341),
     'L0_mix_b2': (0.0, 0.1),
     'L0_mix_ln2_g': (1.0, 0.6),
     'L0_mix_ln2_b': (0.0, 0.8),
     'L0_ffn_gate_b': (0.0, 0.8),
     'L1_gnn_gamma': (1.0, 0.6),
     'L1_gnn_beta': (0.0, 0.278),
     'L1_ffn_b1': (0.0, 0.8),
     'L1_ffn_b2': (0.0, 0.8)}
    factors = {'L0_gnn_query_emb': 8.0,
     'L0_gnn_Wq': 8.0,
     'L0_gnn_Wk': 8.0,
     'L0_gnn_Wv': 7.311,
     'L0_gnn_rel_w': 8.0,
     'L0_gnn_Wo': 4.606,
     'L0_mix_Wq': 8.0,
     'L0_mix_Wk': 8.0,
     'L0_mix_Wv': 4.6,
     'L0_mix_Wo': 4.258,
     'L0_ffn_gate_w': 8.0,
     'L0_ffn_w1': 8.0,
     'L0_ffn_w2': 8.0,
     'L0_ffn_w3': 8.0,
     'L1_gnn_b_x2i': 40.049,
     'L1_mix_bout': 64.0,
     'L1_ffn_wr': 8.0,
     'L1_ffn_w1': 8.0,
     'L1_ffn_w2': 8.0,
     'edge_weight': 3.332,
     'edge_weight_n2': 2.902,
     'L1_gnn_b_in': 4.449,
     'L1_gnn_b_out': 4.315}
    for name, (base, spread) in spreads.items():
        noise = np.random.default_rng([zlib.crc32(name.encode()), seed]).standard_normal(out[name].shape)
        drawn = base * np.exp(spread * noise) if base else spread * noise
        out[name] = jnp.asarray(drawn.astype(out[name].dtype))
    for name, factor in factors.items():
        out[name] = (out[name] * factor).astype(out[name].dtype)
    return out
```

```python
import concourse.bass as bass
from concourse import mybir
from contextlib import ExitStack

F32 = mybir.dt.float32
BF16 = mybir.dt.bfloat16
I32 = mybir.dt.int32
ALU = mybir.AluOpType
ACT = mybir.ActivationFunctionType
AX = mybir.AxisListType
ds = bass.ds

N = 3125
D = 256
P = 128
NT = -(-N // P)
TAIL = N - (NT - 1) * P
NU = 4
E = 100000
EP = 125
EC = E // EP
U = 8
NTL = -(-(E // P + 1 + NT) // U) * U
PEEL = 4
LAYERS = 4
BESIDE = 18, (EC // U - PEEL) // LAYERS
HEADS, HD, NREL = 4, 64, 64
NX, HX, TOP = 16, 512, 2
XT = (TOP * N + NX * (P - 1)) // P
BIG = 1e30
EPS = 1e-5


def need(eng, sem, value):
    if not isinstance(value, int) or value > 0:
        eng.wait_ge(sem, value)


def steps(eng, count, unroll, lag, step):
    for u in range(unroll):
        step(0, u)
    with eng.Fori(1, count // unroll) as i:
        for u in range(unroll):
            step(i, u)
    for u in range(count % unroll + lag):
        step(count // unroll, u)


def tile(i, u, k, unroll, count):
    t, r = i * unroll + (u - k), (u - k) % unroll
    return not isinstance(t, int) or 0 <= t < count, t, r


def uses(i, u, k, unroll, ring):
    v = u - k
    return (i + v // unroll) * (unroll // ring) + (v % unroll) // ring


def at(t):
    return ds(t, 1)


class Kernel:
    def __init__(self, nc, a):
        self.nc, self.a = nc, a
        self.ctx = ExitStack()
        self.sems, self.live = None, []
        self.placing = []

    def sb(self, ctx, name, shape, dt=F32):
        return ctx.enter_context(self.nc.sbuf_tensor(name, shape, dt))

    def pb(self, ctx, name, shape, dt=F32):
        return ctx.enter_context(self.nc.psum_tensor(name, shape, dt))

    def sem(self, name):
        s = self.sems.enter_context(self.nc.semaphore(name))
        self.live.append(s)
        return s

    def soft_sems(self, name, n):
        return [self.ctx.enter_context(self.nc.semaphore(f"{name}{i}")) for i in range(n)]

    def stage(self, build, *args):
        with ExitStack() as self.sems:
            self.live = []
            build(*args)
            with self.nc.Block() as block:

                @block.gpsimd
                def _(pool):
                    for s in self.live:
                        pool.sem_clear(s)

    def dram(self, name, shape, dt=F32):
        return self.nc.dram_tensor(name, shape, dt, kind="Internal").ap()

    def constants(self):
        nc, c = self.nc, self.ctx
        self.identf = identf = self.sb(c, "identf", [P, P])
        self.identb = identb = self.sb(c, "identb", [P, P], BF16)
        self.ones = ones = self.sb(c, "ones", [P, P])
        self.lower = lower = self.sb(c, "lower", [P, P])
        self.iota_t = iota_t = self.sb(c, "iota_t", [P, NTL])
        self.eps = eps = self.sb(c, "eps", [P, 1])
        self.zeros = self.sb(c, "zeros", [P, P])
        scratch = ExitStack()
        iota_i = self.sb(scratch, "iota_i", [P, NTL], I32)
        c_set, c_io = self.sem("c_set"), self.sem("c_io")
        with scratch, nc.Block() as block:

            @block.gpsimd
            def _(pool):
                pool.iota(iota_i[:, :], pattern=[[1, NTL]], base=0, channel_multiplier=0).then_inc(c_io, 1)
                pool.memset(identf[:, :], 0.0)
                pool.memset(ones[:, :], 1.0)
                pool.memset(eps[:, :], EPS)
                pool.drain()
                pool.affine_select(out=identf[:, :], in_=identf[:, :], compare_op=ALU.not_equal, fill=1.0,
                                   base=0, pattern=[[-1, P]], channel_multiplier=1).then_inc(c_set, 1)
                pool.affine_select(out=lower[:, :], in_=ones[:, :], compare_op=ALU.is_gt, fill=0.0,
                                   base=0, pattern=[[1, P]], channel_multiplier=-1)

            @block.vector
            def _(dve):
                dve.wait_ge(c_io, 1)
                dve.tensor_copy(iota_t[:, :], iota_i[:, :])
                dve.wait_ge(c_set, 1)
                dve.tensor_copy(identb[:, :], identf[:, :])
                dve.memset(self.zeros[:, :], 0.0)

    def finish_stats(self, dve, st, mean, var, n):
        dve.tensor_tensor(mean, st[:, 0:n, 1], st[:, 0:n, 4], ALU.subtract)
        dve.tensor_tensor(var, st[:, 0:n, 2], st[:, 0:n, 5], ALU.add)
        dve.drain()
        dve.tensor_tensor(mean, mean, mean, ALU.mult)
        dve.tensor_scalar(var, var, 1.0 / D, None, ALU.mult)
        dve.drain()
        dve.scalar_tensor_tensor(out=var, in0=mean, scalar=0.25, in1=var, op0=ALU.mult, op1=ALU.add)
        dve.drain()
        dve.tensor_tensor(mean, st[:, 0:n, 1], st[:, 0:n, 4], ALU.add)
        dve.drain()
        return dve.tensor_scalar(mean, mean, 0.5, None, ALU.mult)

    def split3(self, dve, parts, x, rest):
        dve.tensor_copy(parts[0], x)
        dve.drain()
        dve.tensor_tensor(rest, x, parts[0], ALU.subtract)
        dve.drain()
        dve.tensor_copy(parts[1], rest)
        dve.drain()
        dve.tensor_tensor(parts[2], rest, parts[1], ALU.subtract)

    def norm_x(self):
        nc, a, XN, RES = self.nc, self.a, self.XN, self.RES
        z_tail, s_in, s_st, s_sd, s_xn = (self.sem(f"x_{x}") for x in ("z", "in", "st", "sd", "xn"))
        with ExitStack() as c:
            X = self.sb(c, "x_X", [P, NT, D])
            st = self.sb(c, "x_stats", [P, NT, 6])
            mean, rstd = self.sb(c, "x_mean", [P, NT]), self.sb(c, "x_rstd", [P, NT])
            with nc.Block() as block:

                @block.sync
                def _(sp):
                    sp.wait_ge(z_tail, 1)
                    sp.dma_start(X[:, 0:NT - 1, :], a["x"][0:(NT - 1) * P, :].rearrange("(t p) d -> p t d", p=P)).then_inc(s_in, 16)
                    sp.dma_start(X[0:TAIL, NT - 1, :], a["x"][(NT - 1) * P:N, :]).then_inc(s_in, 16)

                @block.vector
                def _(dve):
                    dve.memset(X[:, NT - 1, :], 0.0).then_inc(z_tail, 1)
                    dve.wait_ge(s_in, 32)
                    with dve.Fori(0, NT) as t:
                        dve.bn_stats(st[:, at(t), :], X[:, at(t), :])
                    dve.drain()
                    self.finish_stats(dve, st, mean[:, :], rstd[:, :], NT).then_inc(s_st, 1)
                    dve.wait_ge(s_sd, 1)
                    dve.reciprocal(rstd[:, :], rstd[:, :])
                    dve.drain()
                    with dve.Fori(0, NT) as t:
                        dve.tensor_scalar(XN[:, at(t), :], X[:, at(t), :], mean[:, at(t)], rstd[:, at(t)],
                                          ALU.subtract, ALU.mult).then_inc(s_xn, 1)

                @block.scalar
                def _(act):
                    act.wait_ge(s_st, 1)
                    act.activation(rstd[:, :], rstd[:, :], ACT.Sqrt, bias=self.eps[:, :]).then_inc(s_sd, 1)
                    act.wait_ge(s_xn, NT)
                    act.activation(RES[:, :, :], XN[:, :, :], ACT.Copy)

    def bucket(self, keep, which, key, other, cols, table, blocks):
        nc, a = self.nc, self.a
        n = self.sem
        s_in, s_c, s_pf, s_fill, s_ok = (n(f"{which}_{x}") for x in ("in", "cnt", "pref", "fill", "ok"))
        s_sc = self.soft_sems(f"{which}_sc", U)
        REC, IDX = self.sb(keep, f"{which}_rec", [EP, EC, 4]), self.sb(keep, f"{which}_idx", [EP, EC], I32)
        idx_r, rec_r = self.sb(keep, f"{which}_idx_r", [EP, 2, U // 2], I32), self.sb(keep, f"{which}_rec_r", [EP, 2, U // 2, 4])
        s_cp, s_turn = (self.ctx.enter_context(nc.semaphore(f"{which}_{x}")) for x in ("cp", "turn"))
        edges = (REC, IDX, idx_r, rec_r, s_sc, s_cp, s_turn, table)
        self.placing.append(edges)
        with ExitStack() as c:
            sb = lambda name, shape, dt=F32: self.sb(c, f"{which}_{name}", shape, dt)
            KI, OI = sb("ki", [EP, EC], I32), sb("oi", [EP, EC], I32)
            CI = sb("ci", [EP, 2, EC], I32)
            BL, MK, SC, POS = sb("bl", [EP, EC]), sb("mk", [EP, EC]), sb("scn", [EP, EC]), sb("pos", [EP, EC])
            ZERO = sb("zero", [EP, EC])
            CNT = sb("cnt", [EP, NT])
            TI, TT, CUM, CUME, BASE = sb("ti", [P, NT], I32), sb("tt", [P, NT]), sb("cum", [P, NT]), sb("cume", [P, NT]), sb("base", [P, NT])
            FILL = sb("fillb", [P, NTL, 4])
            bl1 = sb("bl1", [1, NTL])
            pp = self.pb(c, f"{which}_pp", [P, 2, NT])
            with nc.Block() as block:

                @block.sync
                def _(sp):
                    sp.dma_start(KI[:, :], key.rearrange("(p e) -> p e", p=EP)).then_inc(s_in, 16)
                    sp.dma_start(OI[:, :], other.rearrange("(p e) -> p e", p=EP)).then_inc(s_in, 16)
                    for j, x in enumerate(cols):
                        dst = CI[:, j, :] if x.dtype == I32 else CI[:, j, :].bitcast(F32)
                        sp.dma_start(dst, x.rearrange("(p e) -> p e", p=EP)).then_inc(s_in, 16)
                    sp.wait_ge(s_fill, 1)
                    sp.dma_start(table.rearrange("(p t) c -> p t c", p=P), FILL[:, :, :]).then_inc(s_fill, 16)

                @block.vector
                def _(dve):
                    dve.memset(FILL[:, :, :], 0.0)
                    dve.memset(ZERO[:, :], 0.0)
                    dve.memset(POS[:, :], 0.0)
                    dve.memset(bl1[:, :], 0.0)
                    dve.memset(blocks[:, :], 0)
                    dve.drain()
                    dve.memset(FILL[:, :, 1:2], -1.0).then_inc(s_fill, 1)
                    dve.wait_ge(s_in, 16 * (2 + len(cols)))
                    dve.tensor_copy(SC[:, :], KI[:, :])
                    dve.tensor_scalar(IDX[:, :], KI[:, :], 7, None, ALU.arith_shift_right)
                    dve.drain()
                    dve.tensor_copy(BL[:, :], IDX[:, :])
                    dve.tensor_copy(REC[:, :, 0], OI[:, :])
                    for j, x in enumerate(cols):
                        dve.tensor_copy(REC[:, :, 2 + j], CI[:, j, :] if x.dtype == I32 else CI[:, j, :].bitcast(F32))
                    if len(cols) == 1:
                        dve.tensor_copy(REC[:, :, 3], ZERO[:, :])
                    dve.drain()
                    dve.scalar_tensor_tensor(out=REC[:, :, 1], in0=BL[:, :], scalar=-float(P), in1=SC[:, :], op0=ALU.mult, op1=ALU.add)
                    for b in range(NT):
                        dve.tensor_scalar(MK[:, :], BL[:, :], float(b), None, ALU.is_equal, ALU.add, accum_out=CNT[:, b:b + 1])
                        dve.drain()
                    dve.tensor_copy(CNT[:, :], CNT[:, :]).then_inc(s_c, 1)
                    dve.wait_ge(s_pf, 1)
                    dve.tensor_scalar(TT[:, :], pp[:, 1, :], float(P - 1), None, ALU.add)
                    dve.drain()
                    dve.tensor_copy(TI[:, :], TT[:, :])
                    dve.drain()
                    dve.tensor_scalar(TI[:, :], TI[:, :], 7, None, ALU.arith_shift_right)
                    dve.drain()
                    dve.tensor_copy(TT[:, :], TI[:, :])
                    dve.drain()
                    dve.tensor_tensor_scan(CUM[:, :], TT[:, :], self.zeros[:, 0:NT], 0.0, ALU.add, ALU.add)
                    dve.drain()
                    dve.tensor_tensor(CUME[:, :], CUM[:, :], TT[:, :], ALU.subtract)
                    dve.drain()
                    dve.scalar_tensor_tensor(out=BASE[:, :], in0=CUME[:, :], scalar=float(P), in1=pp[:, 0, :], op0=ALU.mult, op1=ALU.add)
                    dve.drain()
                    dve.tensor_scalar(BASE[:, :], BASE[:, :], -1.0, None, ALU.add)
                    dve.drain()
                    for b in range(1, NT):
                        dve.scalar_tensor_tensor(out=bl1[:, :], in0=self.iota_t[0:1, :], scalar=CUME[0:1, b:b + 1], in1=bl1[:, :],
                                                 op0=ALU.is_ge, op1=ALU.add)
                        dve.drain()
                    dve.tensor_copy(blocks[:, U:U + NTL], bl1[:, :])
                    with dve.Fori(0, NT) as b:
                        dve.tensor_scalar(MK[:, :], BL[:, :], self.iota_t[0:EP, at(b)], None, ALU.is_equal)
                        dve.drain()
                        dve.tensor_tensor_scan(SC[:, :], MK[:, :], ZERO[:, :], 0.0, ALU.add, ALU.add)
                        dve.drain()
                        dve.scalar_tensor_tensor(out=SC[:, :], in0=SC[:, :], scalar=BASE[0:EP, at(b)], in1=MK[:, :], op0=ALU.add, op1=ALU.mult)
                        dve.drain()
                        dve.tensor_tensor(POS[:, :], POS[:, :], SC[:, :], ALU.add)
                        dve.drain()
                    dve.tensor_copy(IDX[:, :], POS[:, :])
                    dve.drain()
                    dve.tensor_scalar(KI[:, :], IDX[:, :], P - 1, None, ALU.bitwise_and)
                    dve.tensor_scalar(IDX[:, :], IDX[:, :], 7, None, ALU.arith_shift_right)
                    dve.drain()
                    dve.scalar_tensor_tensor(out=IDX[:, :], in0=KI[:, :], scalar=float(NTL), in1=IDX[:, :], op0=ALU.mult, op1=ALU.add).then_inc(s_ok, 1)

                @block.tensor
                def _(pe):
                    pe.wait_ge(s_c, 1)
                    pe.matmul(pp[:, 0, :], self.lower[0:EP, :], CNT[:, :], start=True, stop=True)
                    pe.matmul(pp[:, 1, :], self.ones[0:EP, :], CNT[:, :], start=True, stop=True).then_inc(s_pf, 1)

                @block.gpsimd
                def _(pool):
                    pool.wait_ge(s_fill, 17)
                    pool.wait_ge(s_ok, 1)
                    self.place_edges(pool, edges, 0)
                    with pool.Fori(1, PEEL) as i:
                        self.place_edges(pool, edges, i)

    def place_edges(self, pool, edges, i):
        REC, IDX, idx_r, rec_r, s_sc, s_cp, s_turn, table = edges
        for h in range(2):
            for r in range(U // 2):
                need(pool, s_sc[h * U // 2 + r], i * 16)
            pool.tensor_copy(idx_r[:, h, :], IDX[:, ds(i * U + h * (U // 2), U // 2)]).then_inc(s_cp, 1)
            pool.tensor_copy(rec_r[:, h, :, :], REC[:, ds(i * U + h * (U // 2), U // 2), :]).then_inc(s_cp, 1)
            pool.wait_ge(s_cp, i * 4 + (2 * h + 2))
            pool.sem_inc(s_turn, 1)
            for r in range(U // 2):
                pool.indirect_dma_start(table, bass.IndirectOffsetOnAxis(idx_r[:, h, r:r + 1], 0),
                                        rec_r[:, h, r, :], None).then_inc(s_sc[h * U // 2 + r], 16)

    def last_edges(self, pool):
        with pool.Fori(PEEL + LAYERS * BESIDE[0], EC // U) as i:
            self.place_edges(pool, self.placing[0], i)
        for s in self.placing[0][4]:
            pool.wait_ge(s, 16 * (EC // U))

    def project(self):
        nc, a, XN = self.nc, self.a, self.XN
        QS, VS, k_tab, v_tab = self.QS, self.VS, self.k_tab, self.v_tab
        s_in, s_q = self.sem("p_in"), self.sem("p_q")
        s_row, s_tr, s_tt, s_mm = (self.sem(f"p_{x}") for x in ("row", "tr", "tt", "mm"))
        s_kv, s_vq = self.sem("p_kv"), self.sem("p_vq")
        s_out = [self.sem(f"p_out{i}") for i in range(2)]
        with ExitStack() as c:
            W = self.sb(c, "p_W", [P, 2, 3 * D])
            bias = self.sb(c, "p_bias", [P, 3, D])
            q01 = self.sb(c, "p_q01", [P, 2])
            row = self.sb(c, "p_rows", [P, 2, D])
            rowT = self.sb(c, "p_rowT", [P, 2, 2, P])
            kv = self.sb(c, "p_kvrow", [P, 2, 2, D])
            qf = self.sb(c, "p_qf", [P, 2, D])
            pt = [self.pb(c, f"p_pt{i}", [P, 2, P]) for i in range(2)]
            pqk = [self.pb(c, f"p_pqk{i}", [P, 2 * D]) for i in range(2)]
            pv = [self.pb(c, f"p_pv{i}", [P, D]) for i in range(2)]
            with nc.Block() as block:

                @block.sync
                def _(sp):
                    sp.dma_start(q01[:, :], a["L0_gnn_query_emb"].rearrange("(c p) -> p c", p=P)).then_inc(s_in, 16)
                    for j, w in enumerate("qkv"):
                        sp.dma_start(W[:, :, j * D:(j + 1) * D], a[f"L0_gnn_W{w}"].rearrange("(c p) f -> p c f", p=P)).then_inc(s_in, 16)
                        sp.dma_start(bias[:, j, :], a[f"L0_gnn_b{w}"].partition_broadcast(P)).then_inc(s_in, 16)

                    def step(i, u):
                        on, t, r = tile(i, u, 1, NU, NT)
                        if on:
                            sp.wait_ge(s_kv, t + 1)
                            sp.dma_start(k_tab[ds(t * P, P), :], kv[:, r % 2, 0, :]).then_inc(s_out[r % 2], 16)
                            sp.dma_start(v_tab[ds(t * P, P), :], kv[:, r % 2, 1, :]).then_inc(s_out[r % 2], 16)
                    steps(sp, NT, NU, 1, step)
                    sp.wait_ge(s_out[0], 32 * (NT - NT // 2))
                    sp.wait_ge(s_out[1], 32 * (NT // 2))

                @block.vector
                def _(dve):
                    dve.wait_ge(s_in, 16 * 7)
                    dve.tensor_scalar(q01[:, :], q01[:, :], 0.1, None, ALU.mult)
                    dve.drain()
                    dve.sem_inc(s_q, 1)

                    def step(i, u):
                        on, t, r = tile(i, u, 0, NU, NT)
                        if on:
                            need(dve, s_tr, t - 1)
                            dve.tensor_copy(row[:, r % 2, :], XN[:, at(t), :]).then_inc(s_row, 1)
                        on, t, r = tile(i, u, 2, NU, NT)
                        if on:
                            b = r % 2
                            dve.wait_ge(s_mm, t + 1)
                            need(dve, s_out[b], 32 * uses(i, u, 2, NU, 2))
                            dve.tensor_tensor(kv[:, b, 0, :], pqk[b][:, D:], bias[:, 1, :], ALU.add)
                            dve.tensor_tensor(kv[:, b, 1, :], pv[b][:, :], bias[:, 2, :], ALU.add)
                            dve.tensor_tensor(qf[:, 0, :], pqk[b][:, 0:D], bias[:, 0, :], ALU.add).then_inc(s_vq, 1)
                            dve.drain()
                            dve.tensor_copy(VS[:, at(t), :], kv[:, b, 1, :]).then_inc(s_kv, 1)
                            dve.tensor_scalar(qf[:, 0, :], qf[:, 0, :], HD ** -0.5, None, ALU.mult)
                            dve.drain()
                            self.split3(dve, [QS[:, at(t), j, :] for j in range(3)], qf[:, 0, :], qf[:, 1, :])
                    steps(dve, NT, NU, 2, step)

                @block.scalar
                def _(act):
                    act.wait_ge(s_q, 1)

                    def step(i, u):
                        on, t, r = tile(i, u, 0, NU, NT)
                        if on:
                            b = r % 2
                            act.wait_ge(s_tr, t + 1)
                            need(act, s_mm, t - 1)
                            act.activation(rowT[:, b, 0, :], pt[b][:, 0, :], ACT.Identity, bias=q01[:, 0:1])
                            act.activation(rowT[:, b, 1, :], pt[b][:, 1, :], ACT.Identity, bias=q01[:, 1:2]).then_inc(s_tt, 1)
                    steps(act, NT, NU, 0, step)

                @block.tensor
                def _(pe):
                    pe.wait_ge(s_in, 16 * 7)

                    def step(i, u):
                        on, t, r = tile(i, u, 0, NU, NT)
                        if on:
                            pe.wait_ge(s_row, t + 1)
                            need(pe, s_tt, t - 1)
                            pe.transpose(pt[r % 2][:, 0, :], row[:, r % 2, 0:P], self.identf[:, :])
                            pe.transpose(pt[r % 2][:, 1, :], row[:, r % 2, P:], self.identf[:, :]).then_inc(s_tr, 1)
                        on, t, r = tile(i, u, 1, NU, NT)
                        if on:
                            b = r % 2
                            pe.wait_ge(s_tt, t + 1)
                            need(pe, s_vq, t - 1)
                            for ch in range(2):
                                pe.matmul(pqk[b][:, :], rowT[:, b, ch, :], W[:, ch, 0:2 * D], start=ch == 0, stop=ch == 1)
                            for ch in range(2):
                                last = pe.matmul(pv[b][:, :], rowT[:, b, ch, :], W[:, ch, 2 * D:], start=ch == 0, stop=ch == 1)
                            last.then_inc(s_mm, 1)
                    steps(pe, NT, NU, 1, step)

    def load_blocks(self, eng, regs, table, i, lag):
        first = i * U + (U - lag)
        eng.load(regs, table[0:1, ds(first, U)])
        return [eng.snap(r, min_val=0, max_val=NT - 1) for r in regs]

    def refill(self, act, i, h, s_got, s_idx, idx, slots):
        for r in range(h * U // 2, h * U // 2 + U // 2):
            need(act, s_got[r], i * 16)
        act.activation(idx[:, h, :], slots[:, ds(i * U + h * (U // 2), U // 2), 0], ACT.Copy).then_inc(s_idx, 1)

    def att_scores(self, c0, by_dst):
        nc, a, QS = self.nc, self.a, self.QS
        n = self.sem
        SL = self.SL = self.sb(c0, "SL", [P, NTL + U, 4])
        SALL = self.SALL = self.sb(c0, "SALL", [P, NTL, HEADS])
        MX = self.MX = self.sb(c0, "MX", [P, NT, HEADS])
        s_in, s_set, s_rel = n("a_in"), n("a_set"), n("a_rel")
        s_idx, s_turn, s_oh, s_tr, s_ev, s_q, s_kf, s_s = (n(f"a_{x}") for x in ("idx", "turn", "oh", "tr", "ev", "q", "kf", "s"))
        s_keep, s_st, s_hi, s_lo, s_mb, s_mx = (n(f"a_{x}") for x in ("keep", "st", "hi", "lo", "mb", "mx"))
        s_got = self.soft_sems("a_got", U)
        with ExitStack() as c:
            sb = lambda name, shape, dt=F32: self.sb(c, "a_" + name, shape, dt)
            pb = lambda name, shape, dt=F32: self.pb(c, "a_" + name, shape, dt)
            idx = sb("idx_", [P, 2, U // 2], I32)
            KG = sb("KG", [P, U, D])
            relf, relr, rel3 = sb("relf", [NREL, HD]), sb("relr", [NREL, HD]), sb("rel3", [NREL, 3, HD], BF16)
            sel = sb("sel", [36, HEADS, P], BF16)
            hl = sb("hl", [36, 4, P], BF16)
            oh, ot = sb("oh_", [P, 2, P], BF16), sb("ot", [P, 2, NREL], BF16)
            ohT, otT, mb = sb("ohT", [P, 2, P], BF16), sb("otT", [NREL, 2, P], BF16), sb("mbias", [P, 8, P], BF16)
            t1, S4, tm = sb("t1", [P, 2, D]), sb("S4", [P, 4, HEADS]), sb("tm", [P, 2, HEADS])
            ptr = [pb(f"ptr{b}", [P, 2, P], BF16) for b in range(2)]
            pq = [pb(f"pq{b}", [P, D + HD]) for b in range(2)]
            pst = [pb(f"pst{b}", [P, P]) for b in range(2)]
            pmb = [pb(f"pmb{b}", [P, HEADS, P]) for b in range(2)]
            with nc.Block() as block:

                @block.sync
                def _(sp):
                    sp.dma_start(SL[:, 0:NTL, :], by_dst.rearrange("(p t) c -> p t c", p=P)).then_inc(s_in, 16)
                    sp.dma_start(relf[:, :], a["L0_gnn_rel_w"]).then_inc(s_rel, 16)

                @block.gpsimd
                def _(pool):
                    pool.memset(sel[:, :, :], 0.0)
                    pool.memset(hl[:, :, :], 0.0).then_inc(s_set, 1)
                    pool.drain()
                    for b in range(2):
                        pool.affine_select(out=sel[:, :, :], in_=sel[:, :, :], compare_op=ALU.not_equal, fill=1.0,
                                           base=-32 * b, pattern=[[-1, HEADS], [0, P]], channel_multiplier=1).then_inc(s_set, 1)
                        pool.drain()

                    def step(i, u):
                        on, t, r = tile(i, u, 0, U, NTL)
                        if on:
                            need(pool, s_kf, t - (U - 1))
                            if r % (U // 2) == 0:
                                pool.wait_ge(s_idx, i * 2 + (1 + r // (U // 2)))
                            pool.sem_inc(s_turn, 1)
                            pool.indirect_dma_start(KG[:, r, :], None, self.k_tab, bass.IndirectOffsetOnAxis(idx[:, r // (U // 2), ds(r % (U // 2), 1)], 0)).then_inc(s_got[r], 16)
                    steps(pool, NTL, U, 0, step)

                @block.vector
                def _(dve):
                    dve.memset(MX[:, :, :], -BIG)
                    dve.memset(SL[:, NTL:, :], 0.0).then_inc(s_set, 1)
                    dve.wait_ge(s_rel, 16)
                    dve.tensor_scalar(relf[:, :], relf[:, :], 0.2, None, ALU.mult)
                    dve.drain()
                    self.split3(dve, [rel3[:, j, :] for j in range(3)], relf[:, :], relr[:, :])
                    dve.drain()
                    dve.sem_inc(s_rel, 1)
                    dve.wait_ge(s_in, 16)
                    dve.wait_ge(s_set, 4)
                    regs = [dve.alloc_register(f"a_dblk{j}") for j in range(U)]
                    blk = [None]

                    def step(i, u):
                        if u % U == 0:
                            blk[0] = self.load_blocks(dve, regs, self.blk_dst, i + u // U, 7)
                        on3, t3, r3 = tile(i, u, 3, U, NTL)
                        if on3:
                            b3 = r3 % 2
                            dve.wait_ge(s_q, t3 + 1)
                            dve.wait_ge(s_got[r3], i * 16 + 16 * (1 + (u - 3) // U))
                            dve.tensor_tensor(t1[:, b3, :], KG[:, r3, :], pq[b3][:, D:].unsqueeze(1).to_broadcast([P, HEADS, HD]), ALU.add).then_inc(s_kf, 1)
                        on, t, r = tile(i, u, 0, U, NTL)
                        if on:
                            need(dve, s_tr, t - 1)
                            dve.tensor_scalar(oh[:, r % 2, :], self.iota_t[:, 0:P], SL[:, at(t), 1], None, ALU.is_equal)
                            dve.tensor_scalar(ot[:, r % 2, :], self.iota_t[:, 0:NREL], SL[:, at(t), 2], None, ALU.is_equal).then_inc(s_oh, 1)
                        on, t, r = tile(i, u, 5, U, NTL)
                        if on:
                            dve.wait_ge(s_hi, t + 1)
                            dve.tensor_tensor(hl[32:36, r % 4, :], pst[r % 2][0:HEADS, :], hl[0:HEADS, r % 4, :], ALU.subtract).then_inc(s_lo, 1)
                        if on3:
                            dve.drain()
                            dve.tensor_tensor(t1[:, b3, :], t1[:, b3, :], pq[b3][:, 0:D], ALU.mult).then_inc(s_s, 1)
                        on7, t7, r7 = tile(i, u, 7, U, NTL)
                        if on7:
                            dve.wait_ge(s_mb, t7 + 1)
                            dve.tensor_reduce(tm[:, r7 % 2, :], pmb[r7 % 2][:, :, :], AX.X, ALU.max)
                        dve.drain()
                        if on3:
                            need(dve, s_keep, t3 - 3)
                            need(dve, s_st, t3 - 3)
                            dve.tensor_reduce(S4[:, r3 % 4, :], t1[:, b3, :].rearrange("p (h d) -> p h d", h=HEADS), AX.X, ALU.add).then_inc(s_s, 1)
                        if on7:
                            k = blk[0][u % U]
                            need(dve, s_mx, t7)
                            dve.tensor_tensor(MX[:, at(k), :], MX[:, at(k), :], tm[:, r7 % 2, :], ALU.max).then_inc(s_mx, 1)
                    steps(dve, NTL, U, 7, step)

                @block.scalar
                def _(act):
                    act.wait_ge(s_in, 16)
                    act.wait_ge(s_set, 4)
                    for h in range(2):
                        self.refill(act, 0, h, s_got, s_idx, idx, SL)

                    def step(i, u):
                        on, t, r = tile(i, u, 1, U, NTL)
                        if on:
                            b = r % 2
                            act.wait_ge(s_tr, t + 1)
                            need(act, s_q, t - 1)
                            act.activation(ohT[:, b, :], ptr[b][:, 0, :], ACT.Copy)
                            act.activation(otT[:, b, :], ptr[b][0:NREL, 1, :], ACT.Copy)
                            need(act, s_mb, t - 7)
                            act.activation(mb[:, r % 8, :], ptr[b][:, 0, :], ACT.Copy, scale=BIG, bias=-BIG).then_inc(s_ev, 1)
                        on, t, r = tile(i, u, 4, U, NTL)
                        if on:
                            act.wait_ge(s_s, t * 2 + 2)
                            act.activation(SALL[:, at(t), :], S4[:, r % 4, :], ACT.Copy).then_inc(s_keep, 1)
                            act.wait_ge(s_st, t + 1)
                            need(act, s_mb, t - 3)
                            act.activation(hl[0:HEADS, r % 4, :], pst[r % 2][0:HEADS, :], ACT.Copy).then_inc(s_hi, 1)
                        if u == U // 2 + 3 or u == 3:
                            h = 0 if u > 3 else 1
                            if not isinstance(i, int) or (u > 3 and i < NTL // U) or (u == 3 and 0 < i < NTL // U):
                                self.refill(act, i + 1 if u > 3 else i, h, s_got, s_idx, idx, SL)
                    steps(act, NTL, U, 4, step)

                @block.tensor
                def _(pe):
                    pe.wait_ge(s_rel, 17)
                    pe.wait_ge(s_set, 4)
                    regs = [pe.alloc_register(f"a_pblk{j}") for j in range(U)]
                    blk = [None]

                    def step(i, u):
                        if u % U == 0:
                            blk[0] = self.load_blocks(pe, regs, self.blk_dst, i + u // U, 2)
                        on, t, r = tile(i, u, 1, U, NTL)
                        if on:
                            b = r % 2
                            pe.wait_ge(s_oh, t + 1)
                            need(pe, s_ev, t - 1)
                            pe.transpose(ptr[b][:, 0, :], oh[:, b, :], self.identb[:, :])
                            pe.transpose(ptr[b][0:NREL, 1, :], ot[:, b, :], self.identb[:, :]).then_inc(s_tr, 1)
                        on, t, r = tile(i, u, 2, U, NTL)
                        if on:
                            b, k = r % 2, blk[0][u % U]
                            pe.wait_ge(s_ev, t + 1)
                            need(pe, s_s, t * 2 - 3)
                            for j in range(3):
                                pe.matmul(pq[b][:, 0:D], ohT[:, b, :], QS[:, at(k), j, :], start=j == 0, stop=j == 2)
                            for j in range(3):
                                last = pe.matmul(pq[b][:, D:], otT[:, b, :], rel3[:, j, :], start=j == 0, stop=j == 2)
                            last.then_inc(s_q, 1)
                        on, t, r = tile(i, u, 4, U, NTL)
                        if on:
                            pe.wait_ge(s_s, t * 2 + 2)
                            need(pe, s_lo, t - 1)
                            pe.transpose(pst[r % 2][0:HEADS, :], S4[:, r % 4, :], self.identf[:, :]).then_inc(s_st, 1)
                        on, t, r = tile(i, u, 6, U, NTL)
                        if on:
                            b = r % 2
                            pe.wait_ge(s_lo, t + 1)
                            need(pe, s_mx, t - 1)
                            pe.matmul(pmb[b][:, :, :], self.identb[:, :], mb[:, r % 8, :].unsqueeze(1).to_broadcast([P, HEADS, P]), start=True, stop=False)
                            for h in range(HEADS):
                                last = pe.matmul(pmb[b][:, h, :], sel[:, h, :], hl[:, r % 4, :], start=False, stop=h == HEADS - 1)
                            last.then_inc(s_mb, 1)
                    steps(pe, NTL, U, 6, step)

    def att_sums(self):
        nc = self.nc
        SL, SALL, MX, ACC = self.SL, self.SALL, self.MX, self.ACC
        n = self.sem
        s_set, s_idx, s_turn, s_oh, s_tr, s_ev, s_me, s_d, s_ex = (n(f"s_{x}") for x in ("set", "idx", "turn", "oh", "tr", "ev", "me", "d", "ex"))
        s_vw, s_pv, s_acc = n("s_vw"), n("s_pv"), n("s_acc")
        s_got = self.soft_sems("s_got", U)
        with ExitStack() as c:
            sb = lambda name, shape, dt=F32: self.sb(c, "s_" + name, shape, dt)
            pb = lambda name, shape, dt=F32: self.pb(c, "s_" + name, shape, dt)
            idx = sb("idx_", [P, 2, U // 2], I32)
            VG = sb("VG", [P, U, D])
            MX3, rest = sb("MX3", [P, 3, NT, HEADS], BF16), sb("rest", [P, NT, HEADS])
            oh, ohT = sb("oh_", [P, U, P]), sb("ohT", [P, 2, P], BF16)
            dd = sb("dd", [P, 2, HEADS])
            VW = sb("VW", [P, 4, D + HEADS])
            ptr = [pb(f"ptr{b}", [P, P]) for b in range(2)]
            pme = [pb(f"pme{b}", [P, HEADS]) for b in range(2)]
            ppv = [pb(f"ppv{b}", [P, D + HEADS]) for b in range(2)]
            with nc.Block() as block:

                @block.gpsimd
                def _(pool):
                    def step(i, u):
                        on, t, r = tile(i, u, 0, U, NTL)
                        if on:
                            need(pool, s_vw, t - (U - 1))
                            if r % (U // 2) == 0:
                                pool.wait_ge(s_idx, i * 2 + (1 + r // (U // 2)))
                            pool.sem_inc(s_turn, 1)
                            pool.indirect_dma_start(VG[:, r, :], None, self.v_tab, bass.IndirectOffsetOnAxis(idx[:, r // (U // 2), ds(r % (U // 2), 1)], 0)).then_inc(s_got[r], 16)
                    steps(pool, NTL, U, 0, step)

                @block.vector
                def _(dve):
                    dve.memset(ACC[:, :, :], 0.0)
                    self.split3(dve, [MX3[:, j, :, :] for j in range(3)], MX[:, :, :], rest[:, :, :])
                    dve.drain()
                    dve.sem_inc(s_set, 1)
                    regs = [dve.alloc_register(f"s_dblk{j}") for j in range(U)]
                    blk = [None]

                    def step(i, u):
                        if u % U == 0:
                            blk[0] = self.load_blocks(dve, regs, self.blk_dst, i + u // U, 6)
                        on, t, r = tile(i, u, 0, U, NTL)
                        if on:
                            need(dve, s_pv, t - (U - 1))
                            dve.tensor_scalar(oh[:, r, :], self.iota_t[:, 0:P], SL[:, at(t), 1], None, ALU.is_equal).then_inc(s_oh, 1)
                        on, t, r = tile(i, u, 3, U, NTL)
                        if on:
                            dve.wait_ge(s_me, t + 1)
                            need(dve, s_ex, t - 1)
                            dve.tensor_tensor(dd[:, r % 2, :], SALL[:, at(t), :], pme[r % 2][:, :], ALU.subtract).then_inc(s_d, 1)
                        on, t, r = tile(i, u, 4, U, NTL)
                        if on:
                            dve.wait_ge(s_ex, t + 1)
                            dve.wait_ge(s_got[r], i * 16 + 16 * (1 + (u - 4) // U))
                            dve.tensor_tensor(VW[:, r % 4, 0:D].rearrange("p (h d) -> p h d", h=HEADS), VG[:, r, :].rearrange("p (h d) -> p h d", h=HEADS),
                                              VW[:, r % 4, D:].unsqueeze(2).to_broadcast([P, HEADS, HD]), ALU.mult).then_inc(s_vw, 1)
                        on, t, r = tile(i, u, 6, U, NTL)
                        if on:
                            k = blk[0][u % U]
                            dve.wait_ge(s_pv, t + 1)
                            need(dve, s_acc, t)
                            dve.tensor_tensor(ACC[:, at(k), :], ACC[:, at(k), :], ppv[r % 2][:, :], ALU.add).then_inc(s_acc, 1)
                    steps(dve, NTL, U, 6, step)

                @block.scalar
                def _(act):
                    for h in range(2):
                        self.refill(act, 0, h, s_got, s_idx, idx, SL)

                    def step(i, u):
                        on, t, r = tile(i, u, 1, U, NTL)
                        if on:
                            act.wait_ge(s_tr, t + 1)
                            need(act, s_me, t - 1)
                            act.activation(ohT[:, r % 2, :], ptr[r % 2][:, :], ACT.Copy).then_inc(s_ev, 1)
                        on, t, r = tile(i, u, 3, U, NTL)
                        if on:
                            act.wait_ge(s_d, t + 1)
                            need(act, s_pv, t - 3)
                            act.activation(VW[:, r % 4, D:], dd[:, r % 2, :], ACT.Exp).then_inc(s_ex, 1)
                        if u == U // 2 + 3 or u == 3:
                            h = 0 if u > 3 else 1
                            if not isinstance(i, int) or (u > 3 and i < NTL // U) or (u == 3 and 0 < i < NTL // U):
                                self.refill(act, i + 1 if u > 3 else i, h, s_got, s_idx, idx, SL)
                    steps(act, NTL, U, 3, step)

                @block.tensor
                def _(pe):
                    pe.wait_ge(s_set, 1)
                    regs = [pe.alloc_register(f"s_pblk{j}") for j in range(U)]
                    blk = [None]

                    def step(i, u):
                        if u % U == 0:
                            blk[0] = self.load_blocks(pe, regs, self.blk_dst, i + u // U, 2)
                        on, t, r = tile(i, u, 1, U, NTL)
                        if on:
                            pe.wait_ge(s_oh, t + 1)
                            need(pe, s_ev, t - 1)
                            pe.transpose(ptr[r % 2][:, :], oh[:, r, :], self.identf[:, :]).then_inc(s_tr, 1)
                        on, t, r = tile(i, u, 2, U, NTL)
                        if on:
                            k = blk[0][u % U]
                            pe.wait_ge(s_ev, t + 1)
                            need(pe, s_d, t - 1)
                            for j in range(3):
                                last = pe.matmul(pme[r % 2][:, :], ohT[:, r % 2, :], MX3[:, j, at(k), :], start=j == 0, stop=j == 2)
                            last.then_inc(s_me, 1)
                        on, t, r = tile(i, u, 5, U, NTL)
                        if on:
                            pe.wait_ge(s_vw, t + 1)
                            need(pe, s_acc, t - 1)
                            pe.matmul(ppv[r % 2][:, :], oh[:, r, :], VW[:, r % 4, :], start=True, stop=True).then_inc(s_pv, 1)
                    steps(pe, NTL, U, 5, step)

    def att_out(self):
        nc, a = self.nc, self.a
        ACC, VS, XN, RES = self.ACC, self.VS, self.XN, self.RES
        n = self.sem
        s_x, s_in, s_row, s_tr, s_tt, s_mm, s_g, s_st, s_sd = (n(f"o_{x}") for x in ("x", "in", "row", "tr", "tt", "mm", "g", "st", "sd"))
        with ExitStack() as c:
            sb = lambda name, shape, dt=F32: self.sb(c, "o_" + name, shape, dt)
            pb = lambda name, shape, dt=F32: self.pb(c, "o_" + name, shape, dt)
            X = sb("X", [P, NT, D])
            W, vec = sb("W", [P, 2, D]), sb("vec", [P, 3, D])
            none, rden = sb("none", [P, NT, HEADS]), sb("rden", [P, NT, HEADS])
            row, alt, rowT = sb("rows", [P, 2, D]), sb("alt", [P, D]), sb("rowT", [P, 2, 2, P])
            st, mean, rstd = sb("stats", [P, NT, 6]), sb("mean", [P, NT]), sb("rstd", [P, NT])
            pt = [pb(f"pt{b}", [P, 2, P]) for b in range(2)]
            po = [pb(f"po{b}", [P, D]) for b in range(2)]
            heads = lambda x: x.rearrange("p (h d) -> p h d", h=HEADS)
            with nc.Block() as block:

                @block.sync
                def _(sp):
                    sp.dma_start(W[:, :, :], a["L0_gnn_Wo"].rearrange("(c p) f -> p c f", p=P)).then_inc(s_in, 16)
                    for j, x in enumerate(("bo", "gamma", "beta")):
                        sp.dma_start(vec[:, j, :], a[f"L0_gnn_{x}"].partition_broadcast(P)).then_inc(s_in, 16)
                    sp.wait_ge(s_x, 1)
                    sp.dma_start(X[:, 0:NT - 1, :], a["x"][0:(NT - 1) * P, :].rearrange("(t p) d -> p t d", p=P)).then_inc(s_x, 16)
                    sp.dma_start(X[0:TAIL, NT - 1, :], a["x"][(NT - 1) * P:N, :]).then_inc(s_x, 16)

                @block.vector
                def _(dve):
                    dve.memset(X[:, NT - 1, :], 0.0).then_inc(s_x, 1)
                    dve.tensor_scalar(none[:, :, :], ACC[:, :, D:], 0.0, None, ALU.is_equal)
                    dve.drain()
                    dve.tensor_tensor(rden[:, :, :], ACC[:, :, D:], none[:, :, :], ALU.add)
                    dve.drain()
                    dve.reciprocal(rden[:, :, :], rden[:, :, :])
                    dve.wait_ge(s_in, 64)
                    dve.drain()

                    def step(i, u):
                        on, t, r = tile(i, u, 0, NU, NT)
                        if on:
                            b = r % 2
                            need(dve, s_tr, t - 1)
                            need(dve, s_row, t)
                            dve.tensor_tensor(heads(row[:, b, :]), heads(ACC[:, at(t), 0:D].squeeze(1)), rden[:, at(t), :].squeeze(1).unsqueeze(2).to_broadcast([P, HEADS, HD]), ALU.mult)
                            dve.tensor_tensor(heads(alt[:, :]), heads(VS[:, at(t), :].squeeze(1)), none[:, at(t), :].squeeze(1).unsqueeze(2).to_broadcast([P, HEADS, HD]), ALU.mult)
                            dve.drain()
                            dve.tensor_tensor(row[:, b, :], row[:, b, :], alt[:, :], ALU.add).then_inc(s_row, 1)
                        on, t, r = tile(i, u, 2, NU, NT)
                        if on:
                            dve.wait_ge(s_mm, t + 1)
                            dve.tensor_tensor(ACC[:, at(t), 0:D], XN[:, at(t), :], po[r % 2][:, :], ALU.add).then_inc(s_g, 1)
                            dve.drain()
                            dve.tensor_tensor(ACC[:, at(t), 0:D], ACC[:, at(t), 0:D], vec[:, 0, :], ALU.add)
                            dve.drain()
                            dve.bn_stats(st[:, at(t), :], ACC[:, at(t), 0:D])
                    steps(dve, NT, NU, 2, step)
                    dve.drain()
                    self.finish_stats(dve, st, mean[:, :], rstd[:, :], NT).then_inc(s_st, 1)
                    dve.wait_ge(s_sd, 1)
                    dve.reciprocal(rstd[:, :], rstd[:, :])
                    dve.wait_ge(s_x, 33)
                    dve.drain()
                    with dve.Fori(0, NT) as t:
                        dve.tensor_scalar(ACC[:, at(t), 0:D], ACC[:, at(t), 0:D], mean[:, at(t)], rstd[:, at(t)], ALU.subtract, ALU.mult)
                        dve.tensor_tensor(X[:, at(t), :], X[:, at(t), :], vec[:, 2, :], ALU.add)
                        dve.drain()
                        dve.tensor_tensor(RES[:, at(t), :], RES[:, at(t), :], X[:, at(t), :], ALU.add)
                        dve.tensor_tensor(ACC[:, at(t), 0:D], ACC[:, at(t), 0:D], vec[:, 1, :], ALU.mult)
                        dve.drain()
                        dve.tensor_tensor(RES[:, at(t), :], RES[:, at(t), :], ACC[:, at(t), 0:D], ALU.add)

                @block.scalar
                def _(act):
                    def step(i, u):
                        on, t, r = tile(i, u, 0, NU, NT)
                        if on:
                            b = r % 2
                            act.wait_ge(s_tr, t + 1)
                            need(act, s_mm, t - 1)
                            act.activation(rowT[:, b, :, :], pt[b][:, :, :], ACT.Copy).then_inc(s_tt, 1)
                    steps(act, NT, NU, 0, step)
                    act.wait_ge(s_st, 1)
                    act.activation(rstd[:, :], rstd[:, :], ACT.Sqrt, bias=self.eps[:, :]).then_inc(s_sd, 1)

                @block.tensor
                def _(pe):
                    pe.wait_ge(s_in, 64)

                    def step(i, u):
                        on, t, r = tile(i, u, 0, NU, NT)
                        if on:
                            b = r % 2
                            pe.wait_ge(s_row, t + 1)
                            need(pe, s_tt, t - 1)
                            pe.transpose(pt[b][:, 0, :], row[:, b, 0:P], self.identf[:, :])
                            pe.transpose(pt[b][:, 1, :], row[:, b, P:], self.identf[:, :]).then_inc(s_tr, 1)
                        on, t, r = tile(i, u, 1, NU, NT)
                        if on:
                            b = r % 2
                            pe.wait_ge(s_tt, t + 1)
                            need(pe, s_g, t - 1)
                            for ch in range(2):
                                last = pe.matmul(po[b][:, :], rowT[:, b, ch, :], W[:, ch, :], start=ch == 0, stop=ch == 1)
                            last.then_inc(s_mm, 1)
                    steps(pe, NT, NU, 1, step)

    def mix0(self):
        nc, a, H = self.nc, self.a, self.RES
        MH, MD, FF, FC, GT = 8, 32, 1024, 8, 5
        SCALE = MD ** -0.25
        NG, GH = NT // GT, GT * P // 2
        n = self.sem
        names = ("w", "wf", "st", "sd", "row", "tr", "tt", "mm", "qk", "v", "cm", "cmt", "cmr", "dg", "cmb", "cbs", "kd", "ek", "cx", "cn", "ct", "ctt", "m",
                 "ms", "qd", "qe", "qr", "qtr", "qt", "y", "h", "st2", "sd2", "frow", "ftr", "ftt", "u", "gel", "fy", "fh")
        S = {x: n("m_" + x) for x in names}
        s = lambda x: S[x]
        with ExitStack() as c:
            sb = lambda name, shape, dt=F32: self.sb(c, "m_" + name, shape, dt)
            pb = lambda name, shape, dt=F32: self.pb(c, "m_" + name, shape, dt)
            Wqkv, Wo = sb("Wqkv", [P, 2, 3 * D]), sb("Wo", [P, 2, D])
            g1, b1, g2, b2, bf = (sb(x, [P, k]) for x, k in (("g1", 2), ("b1", 2), ("g2", 2), ("b2", 2), ("bf", FC)))
            brow = sb("brow", [1, 2, D])
            st, mean, rstd = sb("stats", [P, NT, 6]), sb("mean", [P, NT]), sb("rstd", [P, NT])
            row, rowT = sb("rows", [P, 2, D]), sb("rowT", [P, 2, 2, P])
            QK = sb("QK", [P, NT, 2 * D])
            VX = sb("VX", [P, NT, 2, P + 1])
            CM, cmT, dg, CMB = sb("CM", [P, D]), sb("cmT", [P, 2]), sb("dg", [P, 2, P]), sb("CMB", [P, D])
            KD, EK = sb("KD", [P, 2, D]), sb("EK", [P, 2, D])
            bd = sb("bd", [P, P])
            rd, CN, CT, M = sb("rd", [P, 2]), sb("CN", [P, 2, P]), sb("CT", [P, 2, P]), sb("M", [P, 2, D])
            qm, qs = sb("qm", [P, 2, MH]), sb("qs", [P, 2, MH])
            QD, QE = sb("QD", [P, 2, D]), sb("QE", [P, 2, D])
            flat = VX[:, :, :, :].rearrange("p t c n -> p (t c n)")
            W1 = flat[:, 0:2 * FF].rearrange("p (c f) -> p c f", c=2)
            W2 = flat[:, 2 * FF:2 * FF + FC * D].rearrange("p (c f) -> p c f", c=FC)
            G = QK[:, 0:10, :].rearrange("p t c -> p (t c)").rearrange("p (f n) -> p f n", f=FC)
            hT = QK[:, 10:15, :].rearrange("p t c -> p (t c)")[:, 0:2 * GT * P].rearrange("p (c n) -> p c n", c=2)
            banks = [pb(f"bank{b}", [P, 512]) for b in range(8)]
            pt = [banks[b][:, 0:D].rearrange("p (c n) -> p c n", c=2) for b in range(2)]
            pqk, pv = [banks[2], banks[3]], [banks[4][:, 0:D], banks[5][:, 0:D]]
            pcx = [banks[6][:, 0:P + 1], banks[7][:, 0:P + 1]]
            py = [banks[4][:, 0:D], banks[5][:, 0:D]]
            mh = lambda x: x.rearrange("p (h d) -> p h d", h=MH)
            with nc.Block() as block:

                @block.gpsimd
                def _(pool):
                    v = bd[:, :].rearrange("p (h d) -> p h d", d=MD)
                    pool.affine_select(out=v, in_=self.ones[:, :].rearrange("p (h d) -> p h d", d=MD), compare_op=ALU.is_ge, fill=0.0,
                                       base=0, pattern=[[-MD, P // MD], [0, MD]], channel_multiplier=1)
                    pool.drain()
                    pool.affine_select(out=v, in_=v, compare_op=ALU.is_ge, fill=0.0,
                                       base=MD - 1, pattern=[[MD, P // MD], [0, MD]], channel_multiplier=-1)

                @block.vector
                def _(dve):
                    with dve.Fori(0, NT) as t:
                        dve.bn_stats(st[:, at(t), :], H[:, at(t), :])

            with nc.Fori(0, LAYERS) as layer:
                with nc.Block() as block:

                    @block.gpsimd
                    def _(pool):
                        for edges, bodies in zip(self.placing, BESIDE):
                            with pool.Fori(0, bodies) as j:
                                self.place_edges(pool, edges, layer * bodies + (j + PEEL))

                    @block.sync
                    def _(sp):
                        w = lambda x: a["L0_mix_" + x]
                        for j, x in enumerate(("Wq", "Wk", "Wv")):
                            sp.dma_start(Wqkv[:, :, j * D:(j + 1) * D], w(x)[at(layer), :, :].squeeze(0).rearrange("(c p) f -> p c f", p=P)).then_inc(s("w"), 16)
                        for dst, x in ((g1, "ln1_g"), (b1, "ln1_b"), (g2, "ln2_g"), (b2, "ln2_b"), (bf, "b1")):
                            sp.dma_start(dst[:, :], w(x)[at(layer), :].squeeze(0).rearrange("(c p) -> p c", p=P)).then_inc(s("w"), 16)
                        sp.dma_start(brow[:, 0, :], w("bo")[at(layer), :]).then_inc(s("w"), 16)
                        sp.dma_start(brow[:, 1, :], w("b2")[at(layer), :]).then_inc(s("w"), 16)
                        sp.dma_start(Wo[:, :, :], w("Wo")[at(layer), :, :].squeeze(0).rearrange("(c p) f -> p c f", p=P)).then_inc(s("w"), 16)
                        sp.wait_ge(s("cx"), NT)
                        sp.dma_start(W1, w("W1")[at(layer), :, :].squeeze(0).rearrange("(c p) f -> p c f", p=P)).then_inc(s("wf"), 16)
                        sp.dma_start(W2, w("W2")[at(layer), :, :].squeeze(0).rearrange("(c p) f -> p c f", p=P)).then_inc(s("wf"), 16)
                    WALL = 16 * 11

                    @block.vector
                    def _(dve):
                        self.finish_stats(dve, st, mean[:, :], rstd[:, :], NT).then_inc(s("st"), 1)
                        dve.memset(CM[:, :], -BIG)
                        dve.memset(VX[:, :, :, P:], 1.0)
                        dve.wait_ge(s("sd"), 1)
                        dve.reciprocal(rstd[:, :], rstd[:, :])
                        dve.drain()

                        def step(i, u):
                            on, t, r = tile(i, u, 0, NU, NT)
                            if on:
                                need(dve, s("tr"), t - 1)
                                dve.tensor_scalar(row[:, r % 2, :], H[:, at(t), :], mean[:, at(t)], rstd[:, at(t)],
                                                  ALU.subtract, ALU.mult).then_inc(s("row"), 1)
                            on, t, r = tile(i, u, 2, NU, NT)
                            if on:
                                dve.wait_ge(s("mm"), t + 1)
                                dve.tensor_copy(VX[:, at(t), :, 0:P], pv[r % 2].rearrange("p (c n) -> p c n", c=2)).then_inc(s("v"), 1)
                                rows = slice(0, TAIL if isinstance(t, int) and t == NT - 1 else P)
                                need(dve, s("cm"), t)
                                dve.wait_ge(s("qk"), t + 1)
                                dve.tensor_tensor(CM[rows, :], CM[rows, :], QK[rows, at(t), D:], ALU.max).then_inc(s("cm"), 1)
                        steps(dve, NT, NU, 2, step)
                        dve.wait_ge(s("cmt"), 1)
                        dve.tensor_reduce(cmT[:, :], pt[0], AX.X, ALU.max)
                        dve.drain()
                        for ch in range(2):
                            last = dve.tensor_scalar(dg[:, ch, :], self.identf[:, :], cmT[:, ch:ch + 1], None, ALU.mult)
                        last.then_inc(s("dg"), 1)
                        dve.wait_ge(s("cmb"), 1)
                        dve.tensor_copy(CMB[:, :], banks[2][:, 0:D])
                        dve.drain()

                        def step(i, u):
                            on, t, r = tile(i, u, 0, NU, NT)
                            if on:
                                need(dve, s("ek"), t - 1)
                                dve.tensor_tensor(KD[:, r % 2, :], QK[:, at(t), D:], CMB[:, :], ALU.subtract).then_inc(s("kd"), 1)
                        steps(dve, NT, NU, 0, step)
                        dve.wait_ge(s("cx"), NT)
                        for ch in range(2):
                            dve.reciprocal(rd[:, ch:ch + 1], pcx[ch][:, P:])
                        dve.drain()
                        for ch in range(2):
                            last = dve.scalar_tensor_tensor(out=CN[:, ch, :], in0=pcx[ch][:, 0:P], scalar=rd[:, ch:ch + 1], in1=bd[:, :], op0=ALU.mult, op1=ALU.mult)
                        last.then_inc(s("cn"), 1)
                        dve.wait_ge(s("ctt"), 1)
                        dve.tensor_copy(CT[:, :, :], pt[0]).then_inc(s("ct"), 1)
                        dve.wait_ge(s("m"), 1)
                        dve.tensor_copy(M[:, :, :], banks[2][:, :].rearrange("p (c n) -> p c n", c=2)).then_inc(s("ms"), 1)

                        def step(i, u):
                            on, t, r = tile(i, u, 1, NU, NT)
                            if on:
                                b = r % 2
                                dve.wait_ge(s("qe"), t + 1)
                                dve.tensor_reduce(qs[:, b, :], mh(QE[:, b, :]), AX.X, ALU.add)
                            on0, t0, r0 = tile(i, u, 0, NU, NT)
                            if on0:
                                b0 = r0 % 2
                                need(dve, s("qe"), t0 - 1)
                                dve.tensor_reduce(qm[:, b0, :], mh(QK[:, at(t0), 0:D].squeeze(1)), AX.X, ALU.max)
                            dve.drain()
                            if on:
                                dve.reciprocal(qs[:, b, :], qs[:, b, :])
                            if on0:
                                dve.tensor_tensor(mh(QD[:, b0, :]), mh(QK[:, at(t0), 0:D].squeeze(1)), qm[:, b0, :].unsqueeze(2).to_broadcast([P, MH, MD]), ALU.subtract).then_inc(s("qd"), 1)
                            dve.drain()
                            if on:
                                dve.tensor_tensor(mh(QE[:, b, :]), mh(QE[:, b, :]), qs[:, b, :].unsqueeze(2).to_broadcast([P, MH, MD]), ALU.mult).then_inc(s("qr"), 1)
                            on, t, r = tile(i, u, 3, NU, NT)
                            if on:
                                dve.wait_ge(s("y"), t + 1)
                                dve.tensor_tensor(H[:, at(t), :], H[:, at(t), :], py[r % 2], ALU.add).then_inc(s("h"), 1)
                                dve.drain()
                                dve.bn_stats(st[:, at(t), :], H[:, at(t), :])
                        steps(dve, NT, NU, 3, step)
                        dve.drain()
                        self.finish_stats(dve, st, mean[:, :], rstd[:, :], NT).then_inc(s("st2"), 1)
                        dve.wait_ge(s("sd2"), 1)
                        dve.reciprocal(rstd[:, :], rstd[:, :])
                        dve.drain()

                        def step(i, u):
                            for k in (0, 1):
                                on, g, _ = tile(i, u, k, 1, NG)
                                if on:
                                    for j in range(GT):
                                        t = g * GT + j
                                        if k == 0:
                                            need(dve, s("ftr"), t - 1 if j else t)
                                            dve.tensor_scalar(row[:, j % 2, :], H[:, at(t), :], mean[:, at(t)], rstd[:, at(t)],
                                                              ALU.subtract, ALU.mult).then_inc(s("frow"), 1)
                                        else:
                                            dve.wait_ge(s("fy"), t + 1)
                                            dve.tensor_tensor(H[:, at(t), :], H[:, at(t), :], py[j % 2], ALU.add).then_inc(s("fh"), 1)
                                            dve.drain()
                                            dve.bn_stats(st[:, at(t), :], H[:, at(t), :])
                        steps(dve, NG, 1, 1, step)

                    @block.scalar
                    def _(act):
                        act.wait_ge(s("st"), 1)
                        act.activation(rstd[:, :], rstd[:, :], ACT.Sqrt, bias=self.eps[:, :]).then_inc(s("sd"), 1)
                        act.wait_ge(s("w"), WALL)

                        def step(i, u):
                            on, t, r = tile(i, u, 0, NU, NT)
                            if on:
                                b = r % 2
                                act.wait_ge(s("tr"), t + 1)
                                need(act, s("mm"), t - 1)
                                for ch in range(2):
                                    last = act.activation(rowT[:, b, ch, :], pt[b][:, ch, :], ACT.Identity, scale=g1[:, ch:ch + 1], bias=b1[:, ch:ch + 1])
                                last.then_inc(s("tt"), 1)
                            on, t, r = tile(i, u, 1, NU, NT)
                            if on:
                                act.wait_ge(s("mm"), t + 1)
                                act.activation(QK[:, at(t), :], pqk[r % 2][:, :], ACT.Copy).then_inc(s("qk"), 1)
                        steps(act, NT, NU, 1, step)

                        def step(i, u):
                            on, t, r = tile(i, u, 0, NU, NT)
                            if on:
                                act.wait_ge(s("kd"), t + 1)
                                need(act, s("cx"), t - 1)
                                act.activation(EK[:, r % 2, :], KD[:, r % 2, :], ACT.Exp, scale=SCALE).then_inc(s("ek"), 1)
                        steps(act, NT, NU, 0, step)

                        def step(i, u):
                            on, t, r = tile(i, u, 0, NU, NT)
                            if on:
                                act.wait_ge(s("qd"), t + 1)
                                need(act, s("qtr"), t - 1)
                                act.activation(QE[:, r % 2, :], QD[:, r % 2, :], ACT.Exp, scale=SCALE).then_inc(s("qe"), 1)
                            on, t, r = tile(i, u, 2, NU, NT)
                            if on:
                                act.wait_ge(s("qtr"), t + 1)
                                need(act, s("y"), t - 1)
                                act.activation(rowT[:, r % 2, :, :], pt[r % 2], ACT.Copy).then_inc(s("qt"), 1)
                        steps(act, NT, NU, 2, step)
                        act.wait_ge(s("st2"), 1)
                        act.activation(rstd[:, :], rstd[:, :], ACT.Sqrt, bias=self.eps[:, :]).then_inc(s("sd2"), 1)

                        def step(i, u):
                            on, g, _ = tile(i, u, 0, 1, NG)
                            if on:
                                need(act, s("u"), g * (2 * FC))
                                for j in range(GT):
                                    t = g * GT + j
                                    act.wait_ge(s("ftr"), t + 1)
                                    for ch in range(2):
                                        last = act.activation(hT[:, ch, j * P:(j + 1) * P], pt[j % 2][:, ch, :], ACT.Identity, scale=g2[:, ch:ch + 1], bias=b2[:, ch:ch + 1])
                                    last.then_inc(s("ftt"), 1)
                                need(act, s("fy"), g * GT)
                                for f in range(FC):
                                    for h in range(2):
                                        act.wait_ge(s("u"), g * (2 * FC) + (2 * f + h + 1))
                                        act.activation(G[:, f, h * GH:(h + 1) * GH], banks[(2, 3, 6, 7)[2 * (f % 2) + h]][:, 0:GH], ACT.Gelu, bias=bf[:, f:f + 1]).then_inc(s("gel"), 1)
                        steps(act, NG, 1, 0, step)

                    @block.tensor
                    def _(pe):
                        pe.wait_ge(s("w"), WALL)

                        def step(i, u):
                            on, t, r = tile(i, u, 0, NU, NT)
                            if on:
                                b = r % 2
                                pe.wait_ge(s("row"), t + 1)
                                need(pe, s("tt"), t - 1)
                                pe.transpose(pt[b][:, 0, :], row[:, b, 0:P], self.identf[:, :])
                                pe.transpose(pt[b][:, 1, :], row[:, b, P:], self.identf[:, :]).then_inc(s("tr"), 1)
                            on, t, r = tile(i, u, 1, NU, NT)
                            if on:
                                b = r % 2
                                pe.wait_ge(s("tt"), t + 1)
                                need(pe, s("qk"), t - 1)
                                need(pe, s("v"), t - 1)
                                for ch in range(2):
                                    pe.matmul(pqk[b][:, :], rowT[:, b, ch, :], Wqkv[:, ch, 0:2 * D], start=ch == 0, stop=ch == 1)
                                for ch in range(2):
                                    last = pe.matmul(pv[b], rowT[:, b, ch, :], Wqkv[:, ch, 2 * D:], start=ch == 0, stop=ch == 1)
                                last.then_inc(s("mm"), 1)
                        steps(pe, NT, NU, 1, step)
                        pe.wait_ge(s("cm"), NT)
                        pe.wait_ge(s("qk"), NT)
                        pe.transpose(pt[0][:, 0, :], CM[:, 0:P], self.identf[:, :])
                        pe.transpose(pt[0][:, 1, :], CM[:, P:], self.identf[:, :]).then_inc(s("cmt"), 1)
                        pe.wait_ge(s("dg"), 1)
                        pe.matmul(banks[2][:, 0:D], self.ones[:, :], dg[:, :, :], start=True, stop=True).then_inc(s("cmb"), 1)

                        def step(i, u):
                            on, t, r = tile(i, u, 0, NU, NT)
                            if on:
                                pe.wait_ge(s("ek"), t + 1)
                                first, final = isinstance(t, int) and t == 0, isinstance(t, int) and t == NT - 1
                                rows = slice(0, TAIL if final else P)
                                for ch in range(2):
                                    last = pe.matmul(pcx[ch], EK[rows, r % 2, ch * P:(ch + 1) * P], VX[rows, at(t), ch, :], start=first, stop=final)
                                last.then_inc(s("cx"), 1)
                        steps(pe, NT, NU, 0, step)
                        pe.wait_ge(s("cn"), 1)
                        for ch in range(2):
                            last = pe.transpose(pt[0][:, ch, :], CN[:, ch, :], self.identf[:, :])
                        last.then_inc(s("ctt"), 1)
                        pe.wait_ge(s("ct"), 1)
                        for ch in range(2):
                            last = pe.matmul(banks[2][:, ch * D:(ch + 1) * D], CT[:, ch, :], Wo[:, ch, :], start=True, stop=True)
                        last.then_inc(s("m"), 1)
                        pe.wait_ge(s("ms"), 1)

                        def step(i, u):
                            on, t, r = tile(i, u, 1, NU, NT)
                            if on:
                                b = r % 2
                                pe.wait_ge(s("qr"), t + 1)
                                need(pe, s("qt"), t - 1)
                                pe.transpose(pt[b][:, 0, :], QE[:, b, 0:P], self.identf[:, :])
                                pe.transpose(pt[b][:, 1, :], QE[:, b, P:], self.identf[:, :]).then_inc(s("qtr"), 1)
                            on, t, r = tile(i, u, 2, NU, NT)
                            if on:
                                b = r % 2
                                pe.wait_ge(s("qt"), t + 1)
                                need(pe, s("h"), t - 1)
                                pe.matmul(py[b], self.ones[0:1, :], brow[:, 0, :], start=True, stop=False)
                                for ch in range(2):
                                    last = pe.matmul(py[b], rowT[:, b, ch, :], M[:, ch, :], start=False, stop=ch == 1)
                                last.then_inc(s("y"), 1)
                        steps(pe, NT, NU, 2, step)
                        pe.wait_ge(s("h"), NT)
                        pe.wait_ge(s("qt"), NT)
                        pe.wait_ge(s("wf"), 32)

                        def step(i, u):
                            on, g, _ = tile(i, u, 0, 1, NG)
                            if on:
                                for j in range(GT):
                                    t = g * GT + j
                                    pe.wait_ge(s("frow"), t + 1)
                                    need(pe, s("ftt"), t - 1 if j else t)
                                    pe.transpose(pt[j % 2][:, 0, :], row[:, j % 2, 0:P], self.identf[:, :])
                                    pe.transpose(pt[j % 2][:, 1, :], row[:, j % 2, P:], self.identf[:, :]).then_inc(s("ftr"), 1)
                            on, g1_, _ = tile(i, u, 1, 1, NG)
                            if on:
                                pe.wait_ge(s("gel"), (g1_ + 1) * (2 * FC))
                                for j in range(GT):
                                    t = g1_ * GT + j
                                    need(pe, s("fh"), t - 1 if j else t)
                                    pe.matmul(py[j % 2], self.ones[0:1, :], brow[:, 1, :], start=True, stop=False)
                                    for f in range(FC):
                                        last = pe.matmul(py[j % 2], G[:, f, j * P:(j + 1) * P], W2[:, f, :], start=False, stop=f == FC - 1)
                                    last.then_inc(s("fy"), 1)
                            on, g, _ = tile(i, u, 0, 1, NG)
                            if on:
                                pe.wait_ge(s("ftt"), (g + 1) * GT)
                                for f in range(FC):
                                    for h in range(2):
                                        need(pe, s("gel"), g * (2 * FC) + (2 * f + h - 3))
                                        for ch in range(2):
                                            last = pe.matmul(banks[(2, 3, 6, 7)[2 * (f % 2) + h]][:, 0:GH], W1[:, ch, f * P:(f + 1) * P], hT[:, ch, h * GH:(h + 1) * GH],
                                                             start=ch == 0, stop=ch == 1)
                                        last.then_inc(s("u"), 1)
                        steps(pe, NG, 1, 1, step)

                with nc.Block() as block:

                    @block.gpsimd
                    def _(pool):
                        for x in names:
                            pool.sem_clear(S[x])

            with nc.Block() as block:

                @block.gpsimd
                def _(pool):
                    for s in self.placing[1][4]:
                        pool.wait_ge(s, 16 * (EC // U))

    def norm_rows(self, which):
        nc, XN, RES = self.nc, self.XN, self.RES
        s_st, s_sd = self.sem(which + "_st"), self.sem(which + "_sd")
        with ExitStack() as c:
            st = self.sb(c, which + "_stats", [P, NT, 6])
            mean, rstd = self.sb(c, which + "_mean", [P, NT]), self.sb(c, which + "_rstd", [P, NT])
            with nc.Block() as block:

                @block.vector
                def _(dve):
                    with dve.Fori(0, NT) as t:
                        dve.bn_stats(st[:, at(t), :], RES[:, at(t), :])
                    dve.drain()
                    self.finish_stats(dve, st, mean[:, :], rstd[:, :], NT).then_inc(s_st, 1)
                    dve.wait_ge(s_sd, 1)
                    dve.reciprocal(rstd[:, :], rstd[:, :])
                    dve.drain()
                    with dve.Fori(0, NT) as t:
                        dve.tensor_scalar(XN[:, at(t), :], RES[:, at(t), :], mean[:, at(t)], rstd[:, at(t)], ALU.subtract, ALU.mult)

                @block.scalar
                def _(act):
                    act.wait_ge(s_st, 1)
                    act.activation(rstd[:, :], rstd[:, :], ACT.Sqrt, bias=self.eps[:, :]).then_inc(s_sd, 1)

    def route(self, ctx, xs_tab):
        nc, a, XN = self.nc, self.a, self.XN
        n = self.sem
        self.SLOT = SLOT = self.sb(ctx, "SLOT", [P, NT, 2], I32)
        self.GATE = GATE = self.sb(ctx, "GATE", [P, NT, 2])
        self.XTILE = XTILE = self.sb(ctx, "XTILE", [1, XT], I32)
        s_in, s_row, s_tr, s_tt, s_mm, s_lg, s_d, s_e, s_oh, s_pf, s_z, s_slot, s_turn = (n(f"r_{x}") for x in (
            "in", "row", "tr", "tt", "mm", "lg", "d", "e", "oh", "pf", "z", "slot", "turn"))
        s_sc = self.soft_sems("r_sc", 2)
        with ExitStack() as c:
            sb = lambda name, shape, dt=F32: self.sb(c, "r_" + name, shape, dt)
            pb = lambda name, shape, dt=F32: self.pb(c, "r_" + name, shape, dt)
            gw, gb = sb("gw", [P, 2, NX]), sb("gb", [P, NX])
            row, rowT = sb("rows", [P, 2, D]), sb("rowT", [P, 2, 2, P])
            LG, TMP, FIRST = sb("LG", [P, NT, NX]), sb("TMP", [P, NT, NX]), sb("FIRST", [P, NT, NX])
            OH1, OH2, OH = sb("OH1", [P, NT, NX]), sb("OH2", [P, NT, NX]), sb("OH", [P, NT, NX])
            m1, m2, ix, sf = (sb(x, [P, NT]) for x in ("m1", "m2", "ix", "sf"))
            TOT, CUM = sb("TOT", [P, NX, NT]), sb("CUM", [P, NX, NT])
            te, ti, tb = sb("te", [P, NX]), sb("ti", [P, NX], I32), sb("tb", [P, NX])
            xt = sb("xt", [1, XT])
            zero = sb("zero", [P, 8, D])
            srow, sidx = sb("srow", [P, 2, D]), sb("sidx", [P, 2, 2], I32)
            pt = [pb(f"pt{b}", [P, 2, P]) for b in range(2)]
            pl = [pb(f"pl{b}", [P, NX]) for b in range(2)]
            ppf, ptot = pb("ppf", [P, NT, NX]), pb("ptot", [P, NT, NX])
            wide = lambda x: x.unsqueeze(2).to_broadcast([P, NT, NX])
            iota_e = self.iota_t[:, 0:NX].unsqueeze(1).to_broadcast([P, NT, NX])
            with nc.Block() as block:

                @block.sync
                def _(sp):
                    sp.dma_start(gw[:, :, :], a["L0_ffn_gate_w"].rearrange("(c p) f -> p c f", p=P)).then_inc(s_in, 16)
                    sp.dma_start(gb[:, :], a["L0_ffn_gate_b"].partition_broadcast(P)).then_inc(s_in, 16)
                    sp.wait_ge(s_z, 1)
                    for j in range(XT // 8):
                        sp.dma_start(xs_tab.rearrange("(p t) d -> p t d", p=P)[:, j * 8:(j + 1) * 8, :], zero[:, :, :]).then_inc(s_z, 16)

                @block.vector
                def _(dve):
                    dve.memset(zero[:, :, :], 0.0).then_inc(s_z, 1)
                    dve.memset(xt[:, :], 0.0)
                    dve.wait_ge(s_in, 32)

                    def step(i, u):
                        on, t, r = tile(i, u, 0, NU, NT)
                        if on:
                            need(dve, s_tr, t - 1)
                            dve.tensor_copy(row[:, r % 2, :], XN[:, at(t), :]).then_inc(s_row, 1)
                        on, t, r = tile(i, u, 2, NU, NT)
                        if on:
                            dve.wait_ge(s_mm, t + 1)
                            dve.tensor_tensor(LG[:, at(t), :], pl[r % 2][:, :], gb[:, :], ALU.add).then_inc(s_lg, 1)
                    steps(dve, NT, NU, 2, step)
                    dve.drain()
                    for m, oh in ((m1, OH1), (m2, OH2)):
                        dve.tensor_reduce(m[:, :], LG[:, :, :], AX.X, ALU.max)
                        dve.drain()
                        dve.tensor_tensor(TMP[:, :, :], LG[:, :, :], wide(m[:, :]), ALU.is_lt)
                        dve.drain()
                        dve.scalar_tensor_tensor(out=FIRST[:, :, :], in0=TMP[:, :, :], scalar=float(NX), in1=iota_e, op0=ALU.mult, op1=ALU.add)
                        dve.drain()
                        dve.tensor_reduce(ix[:, :], FIRST[:, :, :], AX.X, ALU.min)
                        dve.drain()
                        dve.tensor_tensor(oh[:, :, :], iota_e, wide(ix[:, :]), ALU.is_equal)
                        dve.drain()
                        dve.scalar_tensor_tensor(out=LG[:, :, :], in0=oh[:, :, :], scalar=-BIG, in1=LG[:, :, :], op0=ALU.mult, op1=ALU.add)
                        dve.drain()
                        dve.tensor_scalar(oh[:, NT - 1, :], oh[:, NT - 1, :], self.lower[:, TAIL:TAIL + 1], None, ALU.mult)
                        dve.drain()
                    dve.tensor_tensor(m2[:, :], m2[:, :], m1[:, :], ALU.subtract).then_inc(s_d, 1)
                    dve.tensor_tensor(OH[:, :, :], OH1[:, :, :], OH2[:, :, :], ALU.add).then_inc(s_oh, 1)
                    dve.wait_ge(s_e, 1)
                    dve.tensor_scalar(m1[:, :], m2[:, :], 1.0, None, ALU.add)
                    dve.drain()
                    dve.reciprocal(m1[:, :], m1[:, :])
                    dve.drain()
                    dve.tensor_copy(GATE[:, :, 0], m1[:, :])
                    dve.tensor_tensor(GATE[:, :, 1], m1[:, :], m2[:, :], ALU.mult)
                    dve.wait_ge(s_pf, 1)
                    dve.tensor_copy(TOT[:, :, :], ptot[:, :, :].rearrange("p t e -> p e t"))
                    dve.drain()
                    for e in range(NX):
                        dve.tensor_tensor_scan(CUM[:, e, :], TOT[:, e, :], self.zeros[:, 0:NT], 0.0, ALU.add, ALU.add)
                    dve.drain()
                    dve.tensor_scalar(te[:, :], CUM[:, :, NT - 1], float(P - 1), None, ALU.add)
                    dve.drain()
                    dve.tensor_copy(ti[:, :], te[:, :])
                    dve.drain()
                    dve.tensor_scalar(ti[:, :], ti[:, :], 7, None, ALU.arith_shift_right)
                    dve.drain()
                    dve.tensor_copy(te[:, :], ti[:, :])
                    dve.drain()
                    dve.tensor_tensor_scan(tb[:, :], te[:, :], self.zeros[:, 0:NX], 0.0, ALU.add, ALU.add)
                    dve.drain()
                    dve.tensor_tensor(tb[:, :], tb[:, :], te[:, :], ALU.subtract)
                    dve.tensor_tensor(CUM[:, :, :], CUM[:, :, :], TOT[:, :, :], ALU.subtract)
                    dve.drain()
                    for e in range(1, NX):
                        dve.scalar_tensor_tensor(out=xt[:, :], in0=self.iota_t[0:1, 0:XT], scalar=tb[0:1, e:e + 1], in1=xt[:, :], op0=ALU.is_ge, op1=ALU.add)
                        dve.drain()
                    dve.tensor_copy(XTILE[:, :], xt[:, :])
                    dve.tensor_scalar(tb[:, :], tb[:, :], float(P), None, ALU.mult)
                    dve.tensor_tensor(TMP[:, :, :], ppf[:, :, :], CUM[:, :, :].rearrange("p e t -> p t e"), ALU.add)
                    dve.drain()
                    dve.tensor_tensor(TMP[:, :, :], TMP[:, :, :], tb[:, :].unsqueeze(1).to_broadcast([P, NT, NX]), ALU.add)
                    dve.drain()
                    for j, oh in enumerate((OH1, OH2)):
                        dve.tensor_tensor(FIRST[:, :, :], TMP[:, :, :], oh[:, :, :], ALU.mult)
                        dve.drain()
                        dve.tensor_reduce(sf[:, :], FIRST[:, :, :], AX.X, ALU.add)
                        dve.drain()
                        dve.tensor_copy(SLOT[:, :, j], sf[:, :])
                    dve.drain()
                    dve.sem_inc(s_slot, 1)

                @block.scalar
                def _(act):
                    def step(i, u):
                        on, t, r = tile(i, u, 0, NU, NT)
                        if on:
                            act.wait_ge(s_tr, t + 1)
                            need(act, s_mm, t - 1)
                            act.activation(rowT[:, r % 2, :, :], pt[r % 2][:, :, :], ACT.Copy).then_inc(s_tt, 1)
                    steps(act, NT, NU, 0, step)
                    act.wait_ge(s_d, 1)
                    act.activation(m2[:, :], m2[:, :], ACT.Exp).then_inc(s_e, 1)

                @block.tensor
                def _(pe):
                    pe.wait_ge(s_in, 32)

                    def step(i, u):
                        on, t, r = tile(i, u, 0, NU, NT)
                        if on:
                            b = r % 2
                            pe.wait_ge(s_row, t + 1)
                            need(pe, s_tt, t - 1)
                            pe.transpose(pt[b][:, 0, :], row[:, b, 0:P], self.identf[:, :])
                            pe.transpose(pt[b][:, 1, :], row[:, b, P:], self.identf[:, :]).then_inc(s_tr, 1)
                        on, t, r = tile(i, u, 1, NU, NT)
                        if on:
                            b = r % 2
                            pe.wait_ge(s_tt, t + 1)
                            need(pe, s_lg, t - 1)
                            for ch in range(2):
                                last = pe.matmul(pl[b][:, :], rowT[:, b, ch, :], gw[:, ch, :], start=ch == 0, stop=ch == 1)
                            last.then_inc(s_mm, 1)
                    steps(pe, NT, NU, 1, step)
                    pe.wait_ge(s_oh, 1)
                    pe.matmul(ppf[:, :, :], self.lower[:, :], OH[:, :, :], start=True, stop=True)
                    pe.matmul(ptot[:, :, :], self.ones[:, :], OH[:, :, :], start=True, stop=True).then_inc(s_pf, 1)

                @block.gpsimd
                def _(pool):
                    pool.wait_ge(s_slot, 1)
                    pool.wait_ge(s_z, 1 + 16 * (XT // 8))

                    def step(i, u):
                        on, t, r = tile(i, u, 0, 2, NT)
                        if on:
                            rows = TAIL if isinstance(t, int) and t == NT - 1 else P
                            need(pool, s_sc[r], i * 32)
                            pool.tensor_copy(srow[:, r, :], XN[:, at(t), :])
                            pool.tensor_copy(sidx[:, r, :], SLOT[:, at(t), :].squeeze(1))
                            pool.drain()
                            for j in range(2):
                                pool.sem_inc(s_turn, 1)
                                pool.indirect_dma_start(xs_tab, bass.IndirectOffsetOnAxis(sidx[0:rows, r, j:j + 1], 0), srow[0:rows, r, :], None).then_inc(s_sc[r], 16)
                    steps(pool, NT, 2, 0, step)
                    for r in range(2):
                        pool.wait_ge(s_sc[r], 32 * ((NT + 1 - r) // 2))

    def experts(self, xs_tab, ys_tab):
        nc, a, XTILE = self.nc, self.a, self.XTILE
        n = self.sem
        HC = HX // P
        s_x, s_w, s_w3 = [n(f"e_x{i}") for i in range(4)], [n(f"e_w{i}") for i in range(4)], [n(f"e_w3{i}") for i in range(4)]
        s_out = [n(f"e_out{i}") for i in range(2)]
        s_tr, s_tt, s_h, s_sl, s_hid, s_htr, s_ht, s_y, s_ys = (n(f"e_{x}") for x in ("tr", "tt", "h", "sl", "hid", "htr", "ht", "y", "ys"))
        XU = 4
        with ExitStack() as c:
            sb = lambda name, shape, dt=F32: self.sb(c, "e_" + name, shape, dt)
            pb = lambda name, shape, dt=F32: self.pb(c, "e_" + name, shape, dt)
            XS, xT = sb("XS", [P, XU, D]), sb("xT", [P, 2, 2, P])
            W1, W2, W3 = sb("W1", [P, XU, 2, HX]), sb("W2", [P, XU, 2, HX]), sb("W3", [P, XU, HC, D])
            sl, hid, hidT, ys = sb("sl", [P, 2, HX]), sb("hid", [P, 2, HX]), sb("hidT", [P, 2, HC, P]), sb("ys", [P, 2, D])
            pt = pb("pt", [P, 2, P])
            ph1, ph2 = [pb(f"ph1{b}", [P, HX]) for b in range(2)], [pb(f"ph2{b}", [P, HX]) for b in range(2)]
            pht = pb("pht", [P, HC, P])
            py = [pb(f"py{b}", [P, D]) for b in range(2)]
            with nc.Block() as block:

                @block.sync
                def _(sp):
                    regs = [sp.alloc_register(f"e_x{j}") for j in range(XU)]
                    ex = [None]

                    def step(i, u):
                        if u % XU == 0 and (not isinstance(i, int) or i < XT // XU):
                            sp.load(regs, XTILE[0:1, ds(i * XU, XU)])
                            ex[0] = [sp.snap(g, min_val=0, max_val=NX - 1) for g in regs]
                        on, t, r = tile(i, u, 0, XU, XT)
                        if on:
                            e = ex[0][r]
                            need(sp, s_tr, t - 3)
                            sp.dma_start(XS[:, r, :], xs_tab[ds(t * P, P), :]).then_inc(s_x[r], 16)
                            need(sp, s_h, t - 3)
                            sp.dma_start(W1[:, r, :, :], a["L0_ffn_w1"][at(e), :, :].squeeze(0).rearrange("(c p) f -> p c f", p=P)).then_inc(s_w[r], 16)
                            sp.dma_start(W2[:, r, :, :], a["L0_ffn_w2"][at(e), :, :].squeeze(0).rearrange("(c p) f -> p c f", p=P)).then_inc(s_w[r], 16)
                            need(sp, s_y, t - 3)
                            sp.dma_start(W3[:, r, :, :], a["L0_ffn_w3"][at(e), :, :].squeeze(0).rearrange("(c p) f -> p c f", p=P)).then_inc(s_w3[r], 16)
                    steps(sp, XT, XU, 0, step)

                @block.gpsimd
                def _(pool):
                    if self.placing:
                        self.last_edges(pool)

                @block.vector
                def _(dve):
                    def step(i, u):
                        on, t, r = tile(i, u, 0, XU, XT)
                        if on:
                            b = r % 2
                            dve.wait_ge(s_sl, t + 1)
                            need(dve, s_htr, t - 1)
                            dve.tensor_tensor(hid[:, b, :], sl[:, b, :], ph2[b][:, :], ALU.mult).then_inc(s_hid, 1)
                        on, t, r = tile(i, u, 3, XU, XT)
                        if on:
                            b = r % 2
                            dve.wait_ge(s_y, t + 1)
                            need(dve, s_out[b], 16 * uses(i, u, 3, XU, 2))
                            dve.tensor_copy(ys[:, b, :], py[b][:, :]).then_inc(s_ys, 1)
                    steps(dve, XT, XU, 3, step)

                @block.scalar
                def _(act):
                    def step(i, u):
                        on, t, r = tile(i, u, 0, XU, XT)
                        if on:
                            act.wait_ge(s_tr, t + 1)
                            need(act, s_h, t - 1)
                            act.activation(xT[:, r % 2, :, :], pt[:, :, :], ACT.Copy).then_inc(s_tt, 1)
                        on, t, r = tile(i, u, 1, XU, XT)
                        if on:
                            act.wait_ge(s_h, t + 1)
                            need(act, s_hid, t - 1)
                            act.activation(sl[:, r % 2, :], ph1[r % 2][:, :], ACT.Silu).then_inc(s_sl, 1)
                        on, t, r = tile(i, u, 2, XU, XT)
                        if on:
                            act.wait_ge(s_htr, t + 1)
                            need(act, s_y, t - 1)
                            act.activation(hidT[:, r % 2, :, :], pht[:, :, :], ACT.Copy).then_inc(s_ht, 1)
                        on, t, r = tile(i, u, 4, XU, XT)
                        if on:
                            act.wait_ge(s_ys, t + 1)
                            act.dma_start(ys_tab[ds(t * P, P), :], ys[:, r % 2, :]).then_inc(s_out[r % 2], 16)
                    steps(act, XT, XU, 4, step)
                    for b in range(2):
                        act.wait_ge(s_out[b], 16 * XT // 2)

                @block.tensor
                def _(pe):
                    def step(i, u):
                        on, t, r = tile(i, u, 0, XU, XT)
                        if on:
                            pe.wait_ge(s_x[r], i * 16 + 16)
                            need(pe, s_tt, t)
                            pe.transpose(pt[:, 0, :], XS[:, r, 0:P], self.identf[:, :])
                            pe.transpose(pt[:, 1, :], XS[:, r, P:], self.identf[:, :]).then_inc(s_tr, 1)
                        on, t, r = tile(i, u, 1, XU, XT)
                        if on:
                            b = r % 2
                            pe.wait_ge(s_tt, t + 1)
                            pe.wait_ge(s_w[r], i * 32 + 32 * (1 + (u - 1) // XU))
                            need(pe, s_hid, t - 1)
                            for W, ph in ((W1, ph1), (W2, ph2)):
                                for ch in range(2):
                                    last = pe.matmul(ph[b][:, :], xT[:, b, ch, :], W[:, r, ch, :], start=ch == 0, stop=ch == 1)
                            last.then_inc(s_h, 1)
                        on, t, r = tile(i, u, 2, XU, XT)
                        if on:
                            pe.wait_ge(s_hid, t + 1)
                            need(pe, s_ht, t)
                            for f in range(HC):
                                last = pe.transpose(pht[:, f, :], hid[:, r % 2, f * P:(f + 1) * P], self.identf[:, :])
                            last.then_inc(s_htr, 1)
                        on, t, r = tile(i, u, 3, XU, XT)
                        if on:
                            b = r % 2
                            pe.wait_ge(s_ht, t + 1)
                            pe.wait_ge(s_w3[r], i * 16 + 16 * (1 + (u - 3) // XU))
                            need(pe, s_ys, t - 1)
                            for f in range(HC):
                                last = pe.matmul(py[b][:, :], hidT[:, b, f, :], W3[:, r, f, :], start=f == 0, stop=f == HC - 1)
                            last.then_inc(s_y, 1)
                    steps(pe, XT, XU, 3, step)

    def combine(self, ys_tab):
        nc, RES, SLOT, GATE = self.nc, self.RES, self.SLOT, self.GATE
        n = self.sem
        s_used, s_turn = n("c_used"), n("c_turn")
        s_got = self.soft_sems("c_got", 2)
        with ExitStack() as c:
            Y, idx = self.sb(c, "c_Y", [P, 2, 2, D]), self.sb(c, "c_idx", [P, 2, 2], I32)
            with nc.Block() as block:

                @block.gpsimd
                def _(pool):
                    def step(i, u):
                        on, t, r = tile(i, u, 0, 2, NT)
                        if on:
                            need(pool, s_used, t - 1)
                            need(pool, s_got[r], i * 32)
                            pool.tensor_copy(idx[:, r, :], SLOT[:, at(t), :].squeeze(1))
                            pool.drain()
                            for j in range(2):
                                pool.sem_inc(s_turn, 1)
                                pool.indirect_dma_start(Y[:, r, j, :], None, ys_tab, bass.IndirectOffsetOnAxis(idx[:, r, j:j + 1], 0)).then_inc(s_got[r], 16)
                    steps(pool, NT, 2, 0, step)

                @block.vector
                def _(dve):
                    def step(i, u):
                        on, t, r = tile(i, u, 0, 2, NT)
                        if on:
                            dve.wait_ge(s_got[r], i * 32 + 32)
                            for j in range(2):
                                last = dve.scalar_tensor_tensor(out=RES[:, at(t), :], in0=Y[:, r, j, :], scalar=GATE[:, at(t), j], in1=RES[:, at(t), :], op0=ALU.mult, op1=ALU.add)
                                if j:
                                    last.then_inc(s_used, 1)
                                dve.drain()
                    steps(dve, NT, 2, 0, step)


    def batch_norm(self, HB, tabs):
        nc, a, XN = self.nc, self.a, self.XN
        n = self.sem
        s_in, s_sum, s_mean, s_sq, s_var, s_sd, s_row, s_tr, s_tt, s_mm, s_f = (n(f"b_{x}") for x in (
            "in", "sum", "mean", "sq", "var", "sd", "row", "tr", "tt", "mm", "f"))
        s_out = [n(f"b_out{i}") for i in range(2)]
        with ExitStack() as c:
            sb = lambda name, shape, dt=F32: self.sb(c, "b_" + name, shape, dt)
            pb = lambda name, shape, dt=F32: self.pb(c, "b_" + name, shape, dt)
            W, vec, bias = sb("W", [P, 2, 2 * D]), sb("vec", [P, 2, D]), sb("bias", [P, 2, D])
            mean, var, sq = sb("mean", [P, D]), sb("var", [P, D]), sb("sq", [P, 2, D])
            row, rowT, fo = sb("rows", [P, 2, D]), sb("rowT", [P, 2, 2, P]), sb("fo", [P, 2, 2, D])
            pt = [pb(f"pt{b}", [P, 2, P]) for b in range(2)]
            pf = [pb(f"pf{b}", [P, 2 * D]) for b in range(2)]
            psum, pvar = pb("psum", [P, D]), pb("pvar", [P, D])
            with nc.Block() as block:

                @block.sync
                def _(sp):
                    for j, x in enumerate(("in", "out")):
                        sp.dma_start(W[:, :, j * D:(j + 1) * D], a[f"L1_gnn_W_{x}"].rearrange("(c p) f -> p c f", p=P)).then_inc(s_in, 16)
                        sp.dma_start(bias[:, j, :], a[f"L1_gnn_b_{x}"].partition_broadcast(P)).then_inc(s_in, 16)
                    for j, x in enumerate(("gamma", "beta")):
                        sp.dma_start(vec[:, j, :], a[f"L1_gnn_{x}"].partition_broadcast(P)).then_inc(s_in, 16)

                    def step(i, u):
                        on, t, r = tile(i, u, 1, NU, NT)
                        if on:
                            sp.wait_ge(s_f, t + 1)
                            for j in range(2):
                                sp.dma_start(tabs[j][ds(t * P, P), :], fo[:, r % 2, j, :]).then_inc(s_out[r % 2], 16)
                    steps(sp, NT, NU, 1, step)
                    sp.wait_ge(s_out[0], 32 * (NT - NT // 2))
                    sp.wait_ge(s_out[1], 32 * (NT // 2))

                @block.vector
                def _(dve):
                    dve.wait_ge(s_in, 96)
                    dve.wait_ge(s_sum, 1)
                    dve.tensor_scalar(mean[:, :], psum[:, :], 1.0 / N, None, ALU.mult)
                    dve.drain()

                    def step(i, u):
                        on, t, r = tile(i, u, 0, NU, NT)
                        if on:
                            need(dve, s_sq, t - 1)
                            dve.tensor_tensor(HB[:, at(t), :], XN[:, at(t), :], mean[:, :], ALU.subtract)
                            dve.drain()
                            dve.tensor_tensor(sq[:, r % 2, :], HB[:, at(t), :], HB[:, at(t), :], ALU.mult).then_inc(s_mean, 1)
                    steps(dve, NT, NU, 0, step)
                    dve.wait_ge(s_sd, 1)
                    dve.reciprocal(var[:, :], var[:, :])
                    dve.drain()
                    dve.tensor_tensor(var[:, :], var[:, :], vec[:, 0, :], ALU.mult)
                    dve.drain()

                    def step(i, u):
                        on, t, r = tile(i, u, 0, NU, NT)
                        if on:
                            dve.tensor_tensor(HB[:, at(t), :], HB[:, at(t), :], var[:, :], ALU.mult)
                            dve.drain()
                            need(dve, s_tr, t - 1)
                            dve.tensor_tensor(row[:, r % 2, :], HB[:, at(t), :], vec[:, 1, :], ALU.add).then_inc(s_row, 1)
                            dve.drain()
                            dve.tensor_copy(HB[:, at(t), :], row[:, r % 2, :])
                        on, t, r = tile(i, u, 2, NU, NT)
                        if on:
                            b = r % 2
                            dve.wait_ge(s_mm, t + 1)
                            need(dve, s_out[b], 32 * uses(i, u, 2, NU, 2))
                            dve.tensor_tensor(fo[:, b, :, :], pf[b][:, :].rearrange("p (j d) -> p j d", j=2), bias[:, :, :], ALU.add).then_inc(s_f, 1)
                            dve.drain()
                    steps(dve, NT, NU, 2, step)

                @block.scalar
                def _(act):
                    act.wait_ge(s_var, 1)
                    act.activation(var[:, :], pvar[:, :], ACT.Sqrt, scale=1.0 / N, bias=self.eps[:, :]).then_inc(s_sd, 1)

                    def step(i, u):
                        on, t, r = tile(i, u, 0, NU, NT)
                        if on:
                            act.wait_ge(s_tr, t + 1)
                            need(act, s_mm, t - 1)
                            act.activation(rowT[:, r % 2, :, :], pt[r % 2][:, :, :], ACT.Copy).then_inc(s_tt, 1)
                    steps(act, NT, NU, 0, step)

                @block.tensor
                def _(pe):
                    for t in (0, NT - 1):
                        if t:
                            with pe.Fori(1, NT - 1) as i:
                                pe.matmul(psum[:, :], self.ones[:, :], XN[:, at(i), :], start=False, stop=False)
                        rows = slice(0, TAIL if t else P)
                        last = pe.matmul(psum[:, :], self.ones[rows, :], XN[rows, t, :], start=t == 0, stop=t == NT - 1)
                    last.then_inc(s_sum, 1)

                    def step(i, u):
                        on, t, r = tile(i, u, 0, NU, NT)
                        if on:
                            first, final = isinstance(t, int) and t == 0, isinstance(t, int) and t == NT - 1
                            rows = slice(0, TAIL if final else P)
                            pe.wait_ge(s_mean, t + 1)
                            last = pe.matmul(pvar[:, :], self.ones[rows, :], sq[rows, r % 2, :], start=first, stop=final)
                            last.then_inc(s_sq, 1)
                            if final:
                                pe.wait_ge(s_sq, NT)
                                pe.sem_inc(s_var, 1)
                    steps(pe, NT, NU, 0, step)
                    pe.wait_ge(s_in, 96)

                    def step(i, u):
                        on, t, r = tile(i, u, 0, NU, NT)
                        if on:
                            b = r % 2
                            pe.wait_ge(s_row, t + 1)
                            need(pe, s_tt, t - 1)
                            pe.transpose(pt[b][:, 0, :], row[:, b, 0:P], self.identf[:, :])
                            pe.transpose(pt[b][:, 1, :], row[:, b, P:], self.identf[:, :]).then_inc(s_tr, 1)
                        on, t, r = tile(i, u, 1, NU, NT)
                        if on:
                            b = r % 2
                            pe.wait_ge(s_tt, t + 1)
                            need(pe, s_f, t - 1)
                            for ch in range(2):
                                last = pe.matmul(pf[b][:, :], rowT[:, b, ch, :], W[:, ch, :], start=ch == 0, stop=ch == 1)
                            last.then_inc(s_mm, 1)
                    steps(pe, NT, NU, 1, step)

    def edge_sums(self, w, slots, col, blk_tab, tab, ACC):
        nc = self.nc
        n = self.sem
        s_in, s_set, s_idx, s_turn, s_oh, s_pv, s_acc = (n(f"{w}_{x}") for x in ("in", "set", "idx", "turn", "oh", "pv", "acc"))
        s_got = self.soft_sems(w + "_got", U)
        with ExitStack() as c:
            SL = self.sb(c, w + "_SL", [P, NTL, 4])
            idx = self.sb(c, w + "_idx", [P, 2, U // 2], I32)
            FG, oh = self.sb(c, w + "_FG", [P, U, D]), self.sb(c, w + "_oh", [P, 4, P])
            pf = [self.pb(c, f"{w}_pf{b}", [P, D]) for b in range(4)]
            with nc.Block() as block:

                @block.sync
                def _(sp):
                    sp.dma_start(SL[:, :, :], slots.rearrange("(p t) c -> p t c", p=P)).then_inc(s_in, 16)

                @block.gpsimd
                def _(pool):
                    def step(i, u):
                        on, t, r = tile(i, u, 0, U, NTL)
                        if on:
                            need(pool, s_pv, t - (U - 1))
                            if r % (U // 2) == 0:
                                pool.wait_ge(s_idx, i * 2 + (1 + r // (U // 2)))
                            pool.sem_inc(s_turn, 1)
                            pool.indirect_dma_start(FG[:, r, :], None, tab, bass.IndirectOffsetOnAxis(idx[:, r // (U // 2), ds(r % (U // 2), 1)], 0)).then_inc(s_got[r], 16)
                    steps(pool, NTL, U, 0, step)

                @block.vector
                def _(dve):
                    dve.memset(ACC[:, :, :], 0.0)
                    dve.wait_ge(s_in, 16)
                    dve.drain()
                    regs = [dve.alloc_register(f"{w}_dblk{j}") for j in range(U)]
                    blk = [None]

                    def step(i, u):
                        if u % U == 0:
                            blk[0] = self.load_blocks(dve, regs, blk_tab, i + u // U, 2)
                        on, t, r = tile(i, u, 0, U, NTL)
                        if on:
                            need(dve, s_pv, t - 3)
                            dve.tensor_scalar(oh[:, r % 4, :], self.iota_t[:, 0:P], SL[:, at(t), 1], SL[:, at(t), col], ALU.is_equal, ALU.mult).then_inc(s_oh, 1)
                        on, t, r = tile(i, u, 2, U, NTL)
                        if on:
                            k = blk[0][u % U]
                            dve.wait_ge(s_pv, t + 1)
                            need(dve, s_acc, t)
                            dve.tensor_tensor(ACC[:, at(k), :], ACC[:, at(k), :], pf[r % 4][:, :], ALU.add).then_inc(s_acc, 1)
                    steps(dve, NTL, U, 2, step)

                @block.scalar
                def _(act):
                    act.wait_ge(s_in, 16)
                    for h in range(2):
                        self.refill(act, 0, h, s_got, s_idx, idx, SL)
                    with act.Fori(1, NTL // U) as i:
                        for h in range(2):
                            self.refill(act, i, h, s_got, s_idx, idx, SL)

                @block.tensor
                def _(pe):
                    def step(i, u):
                        on, t, r = tile(i, u, 0, U, NTL)
                        if on:
                            pe.wait_ge(s_oh, t + 1)
                            pe.wait_ge(s_got[r], i * 16 + 16)
                            need(pe, s_acc, t - 3)
                            pe.matmul(pf[r % 4][:, :], oh[:, r % 4, :], FG[:, r, :], start=True, stop=True).then_inc(s_pv, 1)
                    steps(pe, NTL, U, 0, step)

    def lin_att(self, M2):
        nc, a, XN = self.nc, self.a, self.XN
        LH, LD = 8, 64
        LI = LH * LD
        LC = LI // P
        LU = 8
        n = self.sem
        s_in, s_row, s_tr, s_tt, s_mm, s_cen, s_sq, s_va, s_sd, s_kn, s_dot, s_cd, s_ct, s_ctt, s_m, s_ms, s_m2 = (n(f"l_{x}") for x in (
            "in", "row", "tr", "tt", "mm", "cen", "sq", "va", "sd", "kn", "dot", "cd", "ct", "ctt", "m", "ms", "m2"))
        with ExitStack() as c:
            sb = lambda name, shape, dt=F32: self.sb(c, "l_" + name, shape, dt)
            pb = lambda name, shape, dt=F32: self.pb(c, "l_" + name, shape, dt)
            W, Wq, WoT = sb("W", [P, 2, 2 * LI]), sb("Wq", [P, LC, D]), sb("WoT", [P, LC, D])
            row, rowT = sb("rows", [P, 2, D]), sb("rowT", [P, 2, 2, P])
            KV, SQ = sb("KV", [P, 4, 2, LI]), sb("SQ", [P, 2, 2, LI])
            mu, va = sb("mu", [P, 2, 2 * LH]), sb("va", [P, 2, 2 * LH])
            bd, CD, CDT, M = sb("bd", [P, P]), sb("CD", [P, LC, P]), sb("CDT", [P, LC, P]), sb("M", [P, LC, D])
            banks = [pb(f"bank{b}", [P, 512]) for b in range(8)]
            pt = [banks[b][:, 0:D].rearrange("p (c n) -> p c n", c=2) for b in range(2)]
            pk, pv, pd = banks[2], banks[3], banks[4:8]
            hd = lambda x, h: x.rearrange("p (h d) -> p h d", h=h)
            with nc.Block() as block:

                @block.sync
                def _(sp):
                    sp.dma_start(W[:, :, :], a["L1_mix_WqkvT"][:, LI:].rearrange("(c p) f -> p c f", p=P)).then_inc(s_in, 16)
                    sp.dma_start(Wq[:, :, :], a["L1_mix_Wqkv"][0:LI, :].rearrange("(c p) f -> p c f", p=P)).then_inc(s_in, 16)
                    sp.dma_start(WoT[:, :, :], a["L1_mix_WoutT"].rearrange("(c p) f -> p c f", p=P)).then_inc(s_in, 16)

                @block.gpsimd
                def _(pool):
                    v = bd[:, :].rearrange("p (h d) -> p h d", d=LD)
                    pool.affine_select(out=v, in_=self.ones[:, :].rearrange("p (h d) -> p h d", d=LD), compare_op=ALU.is_ge, fill=0.0,
                                       base=0, pattern=[[-LD, P // LD], [0, LD]], channel_multiplier=1)
                    pool.drain()
                    pool.affine_select(out=v, in_=v, compare_op=ALU.is_ge, fill=0.0,
                                       base=LD - 1, pattern=[[LD, P // LD], [0, LD]], channel_multiplier=-1)
                    pool.drain()
                    pool.sem_inc(s_cd, 1)

                @block.vector
                def _(dve):
                    def step(i, u):
                        on, t, r = tile(i, u, 0, LU, NT)
                        if on:
                            need(dve, s_tr, t - 1)
                            dve.tensor_copy(row[:, r % 2, :], XN[:, at(t), :]).then_inc(s_row, 1)
                        on, t, r = tile(i, u, 2, LU, NT)
                        if on:
                            b = r % 2
                            dve.wait_ge(s_mm, t + 1)
                            dve.tensor_reduce(mu[:, b, 0:LH], hd(pk[:, :], LH), AX.X, ALU.add)
                            dve.tensor_reduce(mu[:, b, LH:], hd(pv[:, :], LH), AX.X, ALU.add)
                            dve.drain()
                            dve.tensor_scalar(mu[:, b, :], mu[:, b, :], 1.0 / LD, None, ALU.mult)
                            dve.drain()
                            need(dve, s_dot, t - 3)
                            for j, p in enumerate((pk, pv)):
                                last = dve.tensor_tensor(hd(KV[:, r % 4, j, :], LH), hd(p[:, :], LH),
                                                         mu[:, b, j * LH:(j + 1) * LH].unsqueeze(2).to_broadcast([P, LH, LD]), ALU.subtract)
                            last.then_inc(s_cen, 1)
                            dve.drain()
                        on, t, r = tile(i, u, 3, LU, NT)
                        if on:
                            b = r % 2
                            dve.wait_ge(s_sq, t + 1)
                            dve.tensor_reduce(va[:, b, :], SQ[:, b, :, :].rearrange("p j (h d) -> p (j h) d", h=LH), AX.X, ALU.add).then_inc(s_va, 1)
                        on, t, r = tile(i, u, 4, LU, NT)
                        if on:
                            b = r % 2
                            dve.wait_ge(s_sd, t + 1)
                            dve.tensor_tensor(va[:, b, 0:LH], va[:, b, 0:LH], va[:, b, LH:], ALU.mult)
                            dve.drain()
                            dve.reciprocal(va[:, b, 0:LH], va[:, b, 0:LH])
                            dve.drain()
                            dve.tensor_tensor(hd(KV[:, r % 4, 0, :], LH), hd(KV[:, r % 4, 0, :], LH), va[:, b, 0:LH].unsqueeze(2).to_broadcast([P, LH, LD]), ALU.mult).then_inc(s_kn, 1)
                            dve.drain()
                    steps(dve, NT, LU, 4, step)
                    dve.wait_ge(s_cd, 1)
                    dve.wait_ge(s_dot, NT)
                    for f in range(LC):
                        last = dve.tensor_tensor(CD[:, f, :], pd[f][:, 0:P], bd[:, :], ALU.mult)
                    last.then_inc(s_cd, 1)
                    dve.wait_ge(s_ct, 1)
                    dve.tensor_copy(CDT[:, :, :], banks[2][:, :].rearrange("p (c n) -> p c n", c=LC)).then_inc(s_ctt, 1)
                    dve.wait_ge(s_m, 1)
                    for j in range(2):
                        last = dve.tensor_copy(M[:, 2 * j:2 * j + 2, :], banks[4 + j][:, :].rearrange("p (c n) -> p c n", c=2))
                    last.then_inc(s_ms, 1)
                    dve.wait_ge(s_m2, 1)
                    dve.tensor_scalar(M2[:, :, :], banks[3][:, :].rearrange("p (c n) -> p c n", c=2), 1.0 / N, None, ALU.mult)

                @block.scalar
                def _(act):
                    def step(i, u):
                        on, t, r = tile(i, u, 0, LU, NT)
                        if on:
                            act.wait_ge(s_tr, t + 1)
                            need(act, s_mm, t - 1)
                            act.activation(rowT[:, r % 2, :, :], pt[r % 2], ACT.Copy).then_inc(s_tt, 1)
                        on, t, r = tile(i, u, 2, LU, NT)
                        if on:
                            act.wait_ge(s_cen, t + 1)
                            need(act, s_va, t - 1)
                            act.activation(SQ[:, r % 2, :, :], KV[:, r % 4, :, :], ACT.Square).then_inc(s_sq, 1)
                        on, t, r = tile(i, u, 3, LU, NT)
                        if on:
                            act.wait_ge(s_va, t + 1)
                            act.activation(va[:, r % 2, :], va[:, r % 2, :], ACT.Sqrt, scale=1.0 / LD, bias=self.eps[:, :]).then_inc(s_sd, 1)
                    steps(act, NT, LU, 3, step)

                @block.tensor
                def _(pe):
                    pe.wait_ge(s_in, 48)

                    def step(i, u):
                        on, t, r = tile(i, u, 0, LU, NT)
                        if on:
                            b = r % 2
                            pe.wait_ge(s_row, t + 1)
                            need(pe, s_tt, t - 1)
                            pe.transpose(pt[b][:, 0, :], row[:, b, 0:P], self.identf[:, :])
                            pe.transpose(pt[b][:, 1, :], row[:, b, P:], self.identf[:, :]).then_inc(s_tr, 1)
                        on, t, r = tile(i, u, 1, LU, NT)
                        if on:
                            b = r % 2
                            pe.wait_ge(s_tt, t + 1)
                            need(pe, s_cen, t)
                            for j, p in enumerate((pk, pv)):
                                for ch in range(2):
                                    last = pe.matmul(p[:, :], rowT[:, b, ch, :], W[:, ch, j * LI:(j + 1) * LI], start=ch == 0, stop=ch == 1)
                            last.then_inc(s_mm, 1)
                        on, t, r = tile(i, u, 4, LU, NT)
                        if on:
                            b = r % 2
                            first, final = isinstance(t, int) and t == 0, isinstance(t, int) and t == NT - 1
                            rows = slice(0, TAIL if final else P)
                            pe.wait_ge(s_kn, t + 1)
                            for f in range(LC):
                                last = pe.matmul(pd[f][:, 0:P], KV[rows, r % 4, 0, f * P:(f + 1) * P], KV[rows, r % 4, 1, f * P:(f + 1) * P], start=first, stop=final)
                            last.then_inc(s_dot, 1)
                    steps(pe, NT, LU, 4, step)
                    pe.wait_ge(s_cd, 2)
                    for f in range(LC):
                        last = pe.transpose(banks[2][:, f * P:(f + 1) * P], CD[:, f, :], self.identf[:, :])
                    last.then_inc(s_ct, 1)
                    pe.wait_ge(s_ctt, 1)
                    for f in range(LC):
                        last = pe.matmul(banks[4 + f // 2][:, (f % 2) * D:(f % 2 + 1) * D], CDT[:, f, :], WoT[:, f, :], start=True, stop=True)
                    last.then_inc(s_m, 1)
                    pe.wait_ge(s_ms, 1)
                    for ch in range(2):
                        for f in range(LC):
                            last = pe.matmul(banks[3][:, ch * D:(ch + 1) * D], Wq[:, f, ch * P:(ch + 1) * P], M[:, f, :], start=f == 0, stop=f == LC - 1)
                    last.then_inc(s_m2, 1)

    def gates(self, HB, AIN, AOUT, M2):
        nc, a, XN, RES = self.nc, self.a, self.XN, self.RES
        n = self.sem
        s_in, s_row, s_tr, s_tt, s_mm, s_gt, s_dn, s_rs = (n(f"g_{x}") for x in ("in", "row", "tr", "tt", "mm", "gt", "dn", "rs"))
        with ExitStack() as c:
            sb = lambda name, shape, dt=F32: self.sb(c, "g_" + name, shape, dt)
            pb = lambda name, shape, dt=F32: self.pb(c, "g_" + name, shape, dt)
            W, b_row, bo = sb("W", [P, 6, 2 * D]), sb("b_row", [1, 2 * D]), sb("bo", [1, D])
            row, rowT = sb("rows", [P, 2, 4, D]), sb("rowT", [P, 2, 8, P])
            gi, gn = sb("gi", [P, 2, D]), sb("gn", [P, 2, D])
            pt = [pb(f"pt{b}", [P, 4, P]) for b in range(4)]
            pg = [pb(f"pg{b}", [P, 2 * D]) for b in range(2)]
            pm = [pb(f"pm{b}", [P, D]) for b in range(2)]
            with nc.Block() as block:

                @block.sync
                def _(sp):
                    sp.dma_start(W[:, 0:4, :], a["L1_gnn_W_x2i"].rearrange("(c p) f -> p c f", p=P)).then_inc(s_in, 16)
                    sp.dma_start(W[:, 4:6, :], a["L1_gnn_W_h2h"].rearrange("(c p) f -> p c f", p=P)).then_inc(s_in, 16)
                    sp.dma_start(b_row[:, :], a["L1_gnn_b_x2i"].partition_broadcast(1)).then_inc(s_in, 16)
                    sp.dma_start(bo[:, :], a["L1_mix_bout"].partition_broadcast(1)).then_inc(s_in, 16)

                @block.vector
                def _(dve):
                    def step(i, u):
                        on, t, r = tile(i, u, 0, NU, NT)
                        if on:
                            b = r % 2
                            need(dve, s_tr, t - 1)
                            for j, x in enumerate((AIN, AOUT, HB, XN)):
                                last = dve.tensor_copy(row[:, b, j, :], x[:, at(t), :])
                            last.then_inc(s_row, 1)
                        on, t, r = tile(i, u, 2, NU, NT)
                        if on:
                            b = r % 2
                            dve.wait_ge(s_gt, t + 1)
                            dve.tensor_tensor(HB[:, at(t), :], HB[:, at(t), :], gn[:, b, :], ALU.subtract)
                            dve.tensor_tensor(RES[:, at(t), :], RES[:, at(t), :], pm[b][:, :], ALU.add).then_inc(s_rs, 1)
                            dve.drain()
                            dve.tensor_tensor(HB[:, at(t), :], HB[:, at(t), :], gi[:, b, :], ALU.mult)
                            dve.tensor_tensor(RES[:, at(t), :], RES[:, at(t), :], gn[:, b, :], ALU.add).then_inc(s_dn, 1)
                            dve.drain()
                            dve.tensor_tensor(RES[:, at(t), :], RES[:, at(t), :], HB[:, at(t), :], ALU.add)
                    steps(dve, NT, NU, 2, step)

                @block.scalar
                def _(act):
                    def step(i, u):
                        on, t, r = tile(i, u, 0, NU, NT)
                        if on:
                            b = r % 2
                            act.wait_ge(s_tr, t + 1)
                            need(act, s_mm, t - 1)
                            act.activation(rowT[:, b, 0:4, :], pt[2 * b][:, :, :], ACT.Copy)
                            act.activation(rowT[:, b, 4:8, :], pt[2 * b + 1][:, :, :], ACT.Copy).then_inc(s_tt, 1)
                        on, t, r = tile(i, u, 1, NU, NT)
                        if on:
                            b = r % 2
                            act.wait_ge(s_mm, t + 1)
                            need(act, s_dn, t - 1)
                            act.activation(gi[:, b, :], pg[b][:, 0:D], ACT.Sigmoid)
                            act.activation(gn[:, b, :], pg[b][:, D:], ACT.Tanh).then_inc(s_gt, 1)
                    steps(act, NT, NU, 1, step)

                @block.tensor
                def _(pe):
                    pe.wait_ge(s_in, 64)

                    def step(i, u):
                        on, t, r = tile(i, u, 0, NU, NT)
                        if on:
                            b = r % 2
                            pe.wait_ge(s_row, t + 1)
                            need(pe, s_tt, t - 1)
                            for j in range(8):
                                last = pe.transpose(pt[2 * b + j // 4][:, j % 4, :], row[:, b, j // 2, (j % 2) * P:(j % 2 + 1) * P], self.identf[:, :])
                            last.then_inc(s_tr, 1)
                        on, t, r = tile(i, u, 1, NU, NT)
                        if on:
                            b = r % 2
                            pe.wait_ge(s_tt, t + 1)
                            need(pe, s_gt, t - 1)
                            need(pe, s_rs, t - 1)
                            pe.matmul(pg[b][:, :], self.ones[0:1, :], b_row[:, :], start=True, stop=False)
                            for j in range(6):
                                pe.matmul(pg[b][:, :], rowT[:, b, j, :], W[:, j, :], start=False, stop=j == 5)
                            pe.matmul(pm[b][:, :], self.ones[0:1, :], bo[:, :], start=True, stop=False)
                            for ch in range(2):
                                last = pe.matmul(pm[b][:, :], rowT[:, b, 6 + ch, :], M2[:, ch, :], start=False, stop=ch == 1)
                            last.then_inc(s_mm, 1)
                    steps(pe, NT, NU, 1, step)

    def last_ffn(self, w_tab, out):
        nc, a, XN, RES = self.nc, self.a, self.XN, self.RES
        FF, FC, GT = 1024, 8, 5
        NG, GH = NT // GT, GT * P // 2
        KEEP = max(1, N // 2) - 1
        n = self.sem
        s_in, s_row, s_tr, s_tt, s_u, s_gel, s_y, s_yr, s_res, s_out = (n(f"f_{x}") for x in ("in", "row", "tr", "tt", "u", "gel", "y", "yr", "res", "out"))
        s_wr, s_w, s_st, s_ld, s_gm, s_gt, s_g1, s_gb, s_cd, s_pf = (n(f"k_{x}") for x in ("wr", "w", "st", "ld", "gm", "gt", "g1", "gb", "cd", "pf"))
        with ExitStack() as c:
            sb = lambda name, shape, dt=F32: self.sb(c, "f_" + name, shape, dt)
            pb = lambda name, shape, dt=F32: self.pb(c, "f_" + name, shape, dt)
            W1, W2, bf, brow = sb("W1", [P, 2, FF]), sb("W2", [P, FC, D]), sb("bf", [P, FC]), sb("brow", [1, D])
            row, hT, G1 = sb("rows", [P, 2, D]), sb("hT", [P, 2, GT * P]), sb("G1", [P, FC, GT * P])
            Y, WSEL = sb("Y", [P, NT, D]), sb("WSEL", [P, NT])
            wr, br, prod = sb("wr", [P, D]), sb("br", [P, 1]), sb("prod", [P, 4, D])
            w, wc, off = sb("w", [P, NT]), sb("wc", [P, NT]), sb("off", [P, 1])
            ROW, HIT = sb("ROW", [P, NT * P]), sb("HIT", [P, NT * P])
            G, GA, GK, gm, g1 = sb("G", [P, NT]), sb("GA", [P, NT]), sb("GK", [P, NT]), sb("gm", [P, 1]), sb("g1", [1, 1])
            gs, cand, pre, cum, left = sb("gs", [P, 1]), sb("cand", [P, NT]), sb("pre", [P, NT]), sb("cum", [P, NT]), sb("left", [P, 1])
            pt = [pb(f"pt{b}", [P, 2, P]) for b in range(2)]
            pu = [pb(f"pu{b}", [P, GH]) for b in range(4)]
            py = [pb(f"py{b}", [P, D]) for b in range(2)]
            pgm, pgb, ppf = pt[0][0:1, 0, :], pt[1][:, 0, 0:1], pu[0][:, 0:2 * NT]
            with nc.Block() as block:

                @block.sync
                def _(sp):
                    sp.dma_start(W1[:, :, :], a["L1_ffn_w1"].rearrange("(c p) f -> p c f", p=P)).then_inc(s_in, 16)
                    sp.dma_start(W2[:, :, :], a["L1_ffn_w2"].rearrange("(c p) f -> p c f", p=P)).then_inc(s_in, 16)
                    sp.dma_start(bf[:, :], a["L1_ffn_b1"].rearrange("(c p) -> p c", p=P)).then_inc(s_in, 16)
                    sp.dma_start(brow[:, :], a["L1_ffn_b2"].partition_broadcast(1)).then_inc(s_in, 16)
                    sp.dma_start(wr[:, :], a["L1_ffn_wr"].rearrange("d o -> (d o)").partition_broadcast(P)).then_inc(s_wr, 16)
                    sp.dma_start(br[:, :], a["L1_ffn_br"].partition_broadcast(P)).then_inc(s_wr, 16)
                    sp.wait_ge(s_w, 1)
                    sp.dma_start(w_tab.rearrange("(t p) -> p t", p=P), wc[:, :]).then_inc(s_st, 16)
                    sp.wait_ge(s_st, 16)
                    sp.dma_start(ROW[:, :], w_tab.partition_broadcast(P)).then_inc(s_ld, 16)
                    for g in range(NG):
                        sp.wait_ge(s_res, (g + 1) * GT)
                        k = GT if g < NG - 1 else GT - 1
                        sp.dma_start(out[g * GT * P:(g * GT + k) * P, :].rearrange("(t p) d -> p t d", p=P), RES[:, g * GT:g * GT + k, :]).then_inc(s_out, 16)
                    sp.dma_start(out[(NT - 1) * P:N, :], RES[0:TAIL, NT - 1, :]).then_inc(s_out, 16)
                    sp.wait_ge(s_out, 16 * (NG + 1))

                @block.vector
                def _(dve):
                    dve.wait_ge(s_wr, 32)
                    with dve.Fori(0, NT) as t:
                        dve.tensor_tensor(RES[:, at(t), :], RES[:, at(t), :], XN[:, at(t), :], ALU.add)
                        dve.tensor_tensor(prod[:, 0, :], XN[:, at(t), :], wr[:, :], ALU.mult)
                        dve.drain()
                        dve.tensor_reduce(w[:, at(t)], prod[:, 0, :], AX.X, ALU.add)
                        dve.drain()
                    dve.tensor_scalar(w[:, :], w[:, :], br[:, :], None, ALU.add)
                    dve.tensor_scalar(off[:, :], self.lower[:, TAIL:TAIL + 1], BIG, -BIG, ALU.mult, ALU.add)
                    dve.drain()
                    dve.tensor_copy(wc[:, :], w[:, :])
                    dve.drain()
                    dve.tensor_scalar(wc[:, NT - 1:], wc[:, NT - 1:], self.lower[:, TAIL:TAIL + 1], off[:, :], ALU.mult, ALU.add)
                    dve.drain()
                    dve.sem_inc(s_w, 1)
                    dve.wait_ge(s_ld, 16)
                    for t in range(NT):
                        dve.tensor_scalar(HIT[:, :], ROW[:, :], wc[:, t:t + 1], None, ALU.is_gt, ALU.add, accum_out=G[:, t:t + 1])
                        dve.drain()
                    dve.tensor_scalar(GA[:, :], G[:, :], float(KEEP), None, ALU.is_lt)
                    dve.tensor_scalar(GK[:, :], G[:, :], 1.0, None, ALU.add)
                    dve.drain()
                    dve.tensor_tensor(GK[:, :], GK[:, :], GA[:, :], ALU.mult)
                    dve.drain()
                    dve.tensor_reduce(gm[:, :], GK[:, :], AX.X, ALU.max).then_inc(s_gm, 1)
                    dve.wait_ge(s_gt, 1)
                    dve.tensor_reduce(g1[:, :], pgm, AX.X, ALU.max).then_inc(s_g1, 1)
                    dve.wait_ge(s_gb, 1)
                    dve.tensor_scalar(gs[:, :], pgb, -1.0, None, ALU.add)
                    dve.drain()
                    dve.tensor_scalar(left[:, :], gs[:, :], -1.0, float(KEEP), ALU.mult, ALU.add)
                    dve.tensor_scalar(cand[:, :], G[:, :], gs[:, :], None, ALU.is_equal).then_inc(s_cd, 1)
                    dve.tensor_scalar(GA[:, :], G[:, :], gs[:, :], None, ALU.is_lt)
                    dve.wait_ge(s_pf, 1)
                    dve.tensor_copy(pre[:, :], ppf[:, NT:2 * NT])
                    dve.drain()
                    dve.tensor_tensor_scan(cum[:, :], pre[:, :], self.zeros[:, 0:NT], 0.0, ALU.add, ALU.add)
                    dve.drain()
                    dve.tensor_tensor(cum[:, :], cum[:, :], pre[:, :], ALU.subtract)
                    dve.drain()
                    dve.tensor_tensor(cum[:, :], cum[:, :], ppf[:, 0:NT], ALU.add)
                    dve.drain()
                    dve.scalar_tensor_tensor(out=cum[:, :], in0=cum[:, :], scalar=left[:, :], in1=cand[:, :], op0=ALU.is_lt, op1=ALU.mult)
                    dve.drain()
                    dve.tensor_tensor(GA[:, :], GA[:, :], cum[:, :], ALU.add)
                    dve.drain()
                    dve.tensor_tensor(WSEL[:, :], GA[:, :], w[:, :], ALU.mult)
                    dve.wait_ge(s_yr, NT)
                    dve.drain()
                    with dve.Fori(0, NT) as t:
                        dve.scalar_tensor_tensor(out=RES[:, at(t), :], in0=Y[:, at(t), :], scalar=WSEL[:, at(t)], in1=RES[:, at(t), :],
                                                 op0=ALU.mult, op1=ALU.add).then_inc(s_res, 1)

                @block.scalar
                def _(act):
                    act.wait_ge(s_in, 64)

                    def step(i, u):
                        on, g, _ = tile(i, u, 0, 1, NG)
                        if on:
                            need(act, s_u, g * (2 * FC))
                            for j in range(GT + 1):
                                if j < GT:
                                    need(act, s_tr, g * GT + (j - 1) if j else g * GT)
                                    act.activation(row[:, j % 2, :], XN[:, at(g * GT + j), :], ACT.Copy).then_inc(s_row, 1)
                                if j:
                                    act.wait_ge(s_tr, g * GT + j)
                                    act.activation(hT[:, :, (j - 1) * P:j * P], pt[(j - 1) % 2][:, :, :], ACT.Copy).then_inc(s_tt, 1)
                        on, gy, _ = tile(i, u, 1, 1, NG)
                        if on:
                            for j in range(GT):
                                act.wait_ge(s_y, gy * GT + (j + 1))
                                act.activation(Y[:, at(gy * GT + j), :], py[j % 2][:, :], ACT.Copy).then_inc(s_yr, 1)
                        if tile(i, u, 0, 1, NG)[0]:
                            for f in range(FC):
                                for h in range(2):
                                    act.wait_ge(s_u, g * (2 * FC) + (2 * f + h + 1))
                                    act.activation(G1[:, f, h * GH:(h + 1) * GH], pu[2 * (f % 2) + h][:, :], ACT.Gelu_apprx_tanh, bias=bf[:, f:f + 1]).then_inc(s_gel, 1)
                    steps(act, NG, 1, 1, step)

                @block.tensor
                def _(pe):
                    pe.wait_ge(s_in, 64)

                    def step(i, u):
                        on, g, _ = tile(i, u, 0, 1, NG)
                        if on:
                            for j in range(GT):
                                t = g * GT + j
                                pe.wait_ge(s_row, t + 1)
                                need(pe, s_tt, t - 1 if j else t)
                                pe.transpose(pt[j % 2][:, 0, :], row[:, j % 2, 0:P], self.identf[:, :])
                                pe.transpose(pt[j % 2][:, 1, :], row[:, j % 2, P:], self.identf[:, :]).then_inc(s_tr, 1)
                        on, gy, _ = tile(i, u, 1, 1, NG)
                        if on:
                            pe.wait_ge(s_gel, (gy + 1) * (2 * FC))
                            for j in range(GT):
                                t = gy * GT + j
                                need(pe, s_yr,  t - 1 if j else t)
                                pe.matmul(py[j % 2][:, :], self.ones[0:1, :], brow[:, :], start=True, stop=False)
                                for f in range(FC):
                                    last = pe.matmul(py[j % 2][:, :], G1[:, f, j * P:(j + 1) * P], W2[:, f, :], start=False, stop=f == FC - 1)
                                last.then_inc(s_y, 1)
                        on, g, _ = tile(i, u, 0, 1, NG)
                        if on:
                            pe.wait_ge(s_tt, (g + 1) * GT)
                            for f in range(FC):
                                for h in range(2):
                                    need(pe, s_gel, g * (2 * FC) + (2 * f + h - 3))
                                    for ch in range(2):
                                        last = pe.matmul(pu[2 * (f % 2) + h][:, :], W1[:, ch, f * P:(f + 1) * P], hT[:, ch, h * GH:(h + 1) * GH],
                                                         start=ch == 0, stop=ch == 1)
                                    last.then_inc(s_u, 1)
                    steps(pe, NG, 1, 1, step)
                    pe.wait_ge(s_yr, NT)
                    pe.wait_ge(s_gm, 1)
                    pe.transpose(pgm, gm[:, :], self.identf[:, :]).then_inc(s_gt, 1)
                    pe.wait_ge(s_g1, 1)
                    pe.matmul(pgb, self.ones[0:1, :], g1[:, :], start=True, stop=True).then_inc(s_gb, 1)
                    pe.wait_ge(s_cd, 1)
                    pe.matmul(ppf[:, 0:NT], self.lower[:, :], cand[:, :], start=True, stop=True)
                    pe.matmul(ppf[:, NT:2 * NT], self.ones[:, :], cand[:, :], start=True, stop=True).then_inc(s_pf, 1)

    def run(self, out):
        a = self.a
        self.k_tab, self.v_tab = self.dram("k_tab", [NT * P, D]), self.dram("v_tab", [NT * P, D])
        by_dst, by_src = self.dram("by_dst", [P * NTL, 4]), self.dram("by_src", [P * NTL, 4])
        self.stage(self.constants)
        self.blk_dst = self.sb(self.ctx, "blk_dst", [1, NTL + 2 * U], I32)
        self.blk_src = self.sb(self.ctx, "blk_src", [1, NTL + 2 * U], I32)
        self.XN = self.sb(self.ctx, "XN", [P, NT, D])
        self.RES = self.sb(self.ctx, "RES", [P, NT, D])
        with ExitStack() as by_source:
            self.stage(self.norm_x)
            with ExitStack() as by_node:
                self.stage(self.bucket, by_source, "bs", a["src"], a["dst"], [a["edge_weight_n2"]], by_src, self.blk_src)
                self.stage(self.bucket, by_node, "bd", a["dst"], a["src"], [a["edge_type_64"], a["edge_weight"]], by_dst, self.blk_dst)
                self.stage(self.mix0)
            with ExitStack() as att:
                self.QS = self.sb(att, "QS", [P, NT, 3, D], BF16)
                self.VS = self.sb(att, "VS", [P, NT, D])
                self.stage(self.project)
                with ExitStack() as slots:
                    self.stage(self.att_scores, slots, by_dst)
                    self.ACC = self.QS[:, :, :, :].rearrange("p t j d -> p (t j d)").bitcast(F32)[:, 0:NT * (D + HEADS)].rearrange("p (t d) -> p t d", t=NT)
                    self.stage(self.att_sums)
                self.stage(self.att_out)
            xs_tab, ys_tab = self.dram("xs_tab", [XT * P, D]), self.dram("ys_tab", [XT * P, D])
            self.stage(self.norm_rows, "n1")
            with ExitStack() as moe:
                self.stage(self.route, moe, xs_tab)
                self.stage(self.experts, xs_tab, ys_tab)
                self.stage(self.combine, ys_tab)
        with ExitStack() as l1:
            HB = self.sb(l1, "HB", [P, NT, D])
            AIN, AOUT = self.sb(l1, "AIN", [P, NT, D]), self.sb(l1, "AOUT", [P, NT, D])
            M2 = self.sb(l1, "M2", [P, 2, D])
            fi_tab, fo_tab = self.dram("fi_tab", [NT * P, D]), self.dram("fo_tab", [NT * P, D])
            self.stage(self.norm_rows, "n2")
            self.stage(self.batch_norm, HB, (fi_tab, fo_tab))
            self.stage(self.lin_att, M2)
            self.stage(self.edge_sums, "ei", by_dst, 3, self.blk_dst, fi_tab, AIN)
            self.stage(self.edge_sums, "eo", by_src, 2, self.blk_src, fo_tab, AOUT)
            self.stage(self.gates, HB, AIN, AOUT, M2)
        self.stage(self.norm_rows, "n3")
        w_tab = self.dram("w_tab", [NT * P])
        self.stage(self.last_ffn, w_tab, out)



def build(nc, a, out):
    k = Kernel(nc, a)
    with k.ctx, nc.allow_non_contiguous_dma(reason="small vectors, one element per partition"):
        k.run(out)


def kernel(**inputs):
    import numpy as np
    import concourse.bacc as bacc
    from concourse.bass_utils import run_bass_kernel_spmd

    arrays = {k: np.ascontiguousarray(v) for k, v in inputs.items() if k != "L1_ffn_attention_mask"}
    for x in ("Wqkv", "Wout"):
        arrays[f"L1_mix_{x}T"] = np.ascontiguousarray(arrays[f"L1_mix_{x}"].T)
    nc = bacc.Bacc("TRN2", target_bir_lowering=False, num_devices=1)
    a = {k: nc.dram_tensor(f"in_{k}", v.shape, mybir.dt.from_np(v.dtype), kind="ExternalInput").ap() for k, v in arrays.items()}
    out = nc.dram_tensor("out_0_dram", (N, D), F32, kind="ExternalOutput").ap()
    build(nc, a, out)
    r = run_bass_kernel_spmd(nc, [{f"in_{k}": v for k, v in arrays.items()}], core_ids=[0])
    return r.results[0]["out_0_dram"]
```

```python
import concourse.bass as bass
from concourse import mybir
from contextlib import ExitStack

F32 = mybir.dt.float32
BF16 = mybir.dt.bfloat16
I32 = mybir.dt.int32
ALU = mybir.AluOpType
ACT = mybir.ActivationFunctionType
AX = mybir.AxisListType
ds = bass.ds

N = 3125
D = 256
P = 128
NT = -(-N // P)
TAIL = N - (NT - 1) * P
NU = 4
E = 100000
EP = 125
EC = E // EP
U = 8
NTL = -(-(E // P + 1 + NT) // U) * U
PEEL = 4
LAYERS = 4
BESIDE = 15, (EC // U - PEEL) // LAYERS
HEADS, HD, NREL = 4, 64, 64
NX, HX, TOP = 16, 512, 2
XT = (TOP * N + NX * (P - 1)) // P
BIG = 1e30
EPS = 1e-5


def need(eng, sem, value):
    if not isinstance(value, int) or value > 0:
        eng.wait_ge(sem, value)


def steps(eng, count, unroll, lag, step, peel=1):
    for u in range(peel * unroll):
        step(u // unroll, u % unroll)
    with eng.Fori(peel, count // unroll) as i:
        for u in range(unroll):
            step(i, u)
    for u in range(count % unroll + lag):
        step(count // unroll, u)


def tile(i, u, k, unroll, count):
    t, r = i * unroll + (u - k), (u - k) % unroll
    return not isinstance(t, int) or 0 <= t < count, t, r


def uses(i, u, k, unroll, ring):
    v = u - k
    return (i + v // unroll) * (unroll // ring) + (v % unroll) // ring


def at(t):
    return ds(t, 1)


class LinAtt:

    LH, LD = 8, 64
    LI = LH * LD
    LC = LI // P

    def __init__(self, k, c, LB):
        assert LB >= 4
        self.k, self.M2, LI, LC = k, k.M2, self.LI, self.LC
        sb = lambda name, shape, dt=F32: k.sb(c, "l_" + name, shape, dt)
        (self.s_in, self.s_row, self.s_tr, self.s_tt, self.s_mm, self.s_cen, self.s_sq, self.s_va, self.s_sd, self.s_kn, self.s_dot,
         self.s_bd, self.s_cd, self.s_ct, self.s_ctt, self.s_m, self.s_ms, self.s_m2) = (k.sem(f"l_{x}") for x in (
             "in", "row", "tr", "tt", "mm", "cen", "sq", "va", "sd", "kn", "dot", "bd", "cd", "ct", "ctt", "m", "ms", "m2"))
        self.W, self.Wq, self.WoT = sb("W", [P, 2, 2 * LI]), sb("Wq", [P, LC, D]), sb("WoT", [P, LC, D])
        self.row, self.rowT = sb("row", [P, D]), sb("rowT", [P, 2, P])
        self.KV, self.SQ = sb("KV", [P, 2, LI]), sb("SQ", [P, 2, LI])
        self.mu, self.va = sb("mu", [P, 2 * self.LH]), sb("va", [P, 2 * self.LH])
        self.node = sb("node", [P, NT])
        self.DOT = sb("DOT", [P, LI])
        self.bd, self.CD, self.CDT, self.M = sb("bd", [P, P]), sb("CD", [P, LC, P]), sb("CDT", [P, LC, P]), sb("M", [P, LC, D])
        self.pt, self.pk, self.pv, self.pd = (k.pb(c, "l_" + x, [P, 512]) for x in ("pt", "pk", "pv", "pd"))

    def heads(self, x):
        return x.rearrange("p (h d) -> p h d", d=self.LD)

    def load(self, sp):
        a, LI = self.k.a, self.LI
        sp.dma_start(self.W[:, :, :], a["L1_mix_WqkvT"][:, LI:].rearrange("(c p) f -> p c f", p=P)).then_inc(self.s_in, 16)
        sp.dma_start(self.Wq[:, :, :], a["L1_mix_Wqkv"][0:LI, :].rearrange("(c p) f -> p c f", p=P)).then_inc(self.s_in, 16)
        sp.dma_start(self.WoT[:, :, :], a["L1_mix_WoutT"].rearrange("(c p) f -> p c f", p=P)).then_inc(self.s_in, 16)

    def mask(self, pool):
        LD, v = self.LD, self.heads(self.bd[:, :])
        pool.affine_select(out=v, in_=self.heads(self.k.ones[:, :]), compare_op=ALU.is_ge, fill=0.0,
                           base=0, pattern=[[-LD, P // LD], [0, LD]], channel_multiplier=1)
        pool.drain()
        pool.affine_select(out=v, in_=v, compare_op=ALU.is_ge, fill=0.0,
                           base=LD - 1, pattern=[[LD, P // LD], [0, LD]], channel_multiplier=-1).then_inc(self.s_bd, 1)

    def set_up(self, dve):
        dve.memset(self.DOT[:, :], 0.0)
        dve.memset(self.node[:, 0:NT - 1], 1.0)
        dve.tensor_copy(self.node[:, NT - 1:], self.k.lower[:, TAIL:TAIL + 1])

    def ready(self, pe):
        pe.wait_ge(self.s_in, 48)

    def on_dve(self, dve, T, q, u):
        LH, heads = self.LH, self.heads
        wide = lambda x: x.unsqueeze(2).to_broadcast([P, LH, self.LD])
        K, V, va = self.KV[:, 0, :], self.KV[:, 1, :], self.va
        if (q, u) == (0, 0):
            dve.tensor_copy(self.row[:, :], self.k.XN[:, at(T), :]).then_inc(self.s_row, 1)
        if (q, u) == (2, 1):
            dve.wait_ge(self.s_mm, T + 1)
            dve.tensor_reduce(self.mu[:, 0:LH], heads(self.pk[:, :]), AX.X, ALU.add)
            dve.tensor_reduce(self.mu[:, LH:], heads(self.pv[:, :]), AX.X, ALU.add)
            dve.drain()
            dve.tensor_scalar(self.mu[:, :], self.mu[:, :], 1.0 / self.LD, None, ALU.mult)
            dve.drain()
        if (q, u) == (2, 3):
            dve.tensor_tensor(heads(K), heads(self.pk[:, :]), wide(self.mu[:, 0:LH]), ALU.subtract)
            dve.tensor_tensor(heads(V), heads(self.pv[:, :]), wide(self.mu[:, LH:]), ALU.subtract).then_inc(self.s_cen, 1)
        if (q, u) == (3, 0):
            dve.wait_ge(self.s_sq, T + 1)
            dve.tensor_reduce(va[:, :], self.SQ[:, :, :].rearrange("p j (h d) -> p (j h) d", h=LH), AX.X, ALU.add).then_inc(self.s_va, 1)
        if (q, u) == (3, 4):
            dve.wait_ge(self.s_sd, T + 1)
            dve.tensor_tensor(va[:, 0:LH], va[:, 0:LH], va[:, LH:], ALU.mult)
            dve.drain()
            dve.reciprocal(va[:, 0:LH], va[:, 0:LH])
            dve.drain()
            dve.tensor_scalar(va[:, 0:LH], va[:, 0:LH], self.node[:, at(T)], None, ALU.mult)
            dve.drain()
            dve.tensor_tensor(heads(K), heads(K), wide(va[:, 0:LH]), ALU.mult).then_inc(self.s_kn, 1)
        if (q, u) == (3, 7):
            dve.wait_ge(self.s_dot, T + 1)
            dve.tensor_tensor(self.DOT[:, :], self.DOT[:, :], self.pd[:, :], ALU.add)
            dve.drain()

    def on_act(self, act, T, q):
        if q == 0:
            act.wait_ge(self.s_tr, T + 1)
            act.activation(self.rowT[:, :, :], self.pt[:, 0:D].rearrange("p (c n) -> p c n", c=2), ACT.Copy).then_inc(self.s_tt, 1)
        if q == 2:
            act.wait_ge(self.s_cen, T + 1)
            act.activation(self.SQ[:, :, :], self.KV[:, :, :], ACT.Square).then_inc(self.s_sq, 1)
        if q == 3:
            act.wait_ge(self.s_va, T + 1)
            act.activation(self.va[:, :], self.va[:, :], ACT.Sqrt, scale=1.0 / self.LD, bias=self.k.eps[:, :]).then_inc(self.s_sd, 1)

    def on_pe(self, pe, T, q, u):
        LI = self.LI
        if (q, u) == (0, 2):
            pe.wait_ge(self.s_row, T + 1)
            pe.transpose(self.pt[:, 0:P], self.row[:, 0:P], self.k.identf[:, :])
            pe.transpose(self.pt[:, P:D], self.row[:, P:], self.k.identf[:, :]).then_inc(self.s_tr, 1)
        if q == 1 and u % 2 == 0:
            if u == 0:
                pe.wait_ge(self.s_tt, T + 1)
            j, ch = u // 4, (u // 2) % 2
            last = pe.matmul((self.pk, self.pv)[j][:, :], self.rowT[:, ch, :], self.W[:, ch, j * LI:(j + 1) * LI], start=ch == 0, stop=ch == 1)
            if u == 6:
                last.then_inc(self.s_mm, 1)
        if (q, u) == (3, 5):
            pe.wait_ge(self.s_kn, T + 1)
            for f in range(self.LC):
                last = pe.matmul(self.pd[:, f * P:(f + 1) * P], self.KV[:, 0, f * P:(f + 1) * P], self.KV[:, 1, f * P:(f + 1) * P], start=True, stop=True)
            last.then_inc(self.s_dot, 1)

    def finish_dve(self, dve):
        chunks = lambda x: x.rearrange("p (c n) -> p c n", c=2)
        dve.wait_ge(self.s_bd, 1)
        dve.tensor_tensor(self.CD[:, :, :], self.DOT[:, :].rearrange("p (c n) -> p c n", c=self.LC),
                          self.bd[:, :].unsqueeze(1).to_broadcast([P, self.LC, P]), ALU.mult).then_inc(self.s_cd, 1)
        dve.wait_ge(self.s_ct, 1)
        dve.tensor_copy(self.CDT[:, :, :], self.pk[:, :].rearrange("p (c n) -> p c n", c=self.LC)).then_inc(self.s_ctt, 1)
        dve.wait_ge(self.s_m, 1)
        dve.tensor_copy(self.M[:, 0:2, :], chunks(self.pv[:, :]))
        dve.tensor_copy(self.M[:, 2:4, :], chunks(self.pd[:, :])).then_inc(self.s_ms, 1)
        dve.wait_ge(self.s_m2, 1)
        dve.tensor_scalar(self.M2[:, :, :], chunks(self.pt[:, :]), 1.0 / N, None, ALU.mult)

    def finish_pe(self, pe):
        LC = self.LC
        pe.wait_ge(self.s_cd, 1)
        for f in range(LC):
            last = pe.transpose(self.pk[:, f * P:(f + 1) * P], self.CD[:, f, :], self.k.identf[:, :])
        last.then_inc(self.s_ct, 1)
        pe.wait_ge(self.s_ctt, 1)
        for f in range(LC):
            last = pe.matmul((self.pv, self.pd)[f // 2][:, (f % 2) * D:(f % 2 + 1) * D], self.CDT[:, f, :], self.WoT[:, f, :], start=True, stop=True)
        last.then_inc(self.s_m, 1)
        pe.wait_ge(self.s_ms, 1)
        for ch in range(2):
            for f in range(LC):
                last = pe.matmul(self.pt[:, ch * D:(ch + 1) * D], self.Wq[:, f, ch * P:(ch + 1) * P], self.M[:, f, :], start=f == 0, stop=f == LC - 1)
        last.then_inc(self.s_m2, 1)


class GateIn:

    def __init__(self, k, c, LB):
        assert LB >= 4
        self.k = k
        sb = lambda name, shape, dt=F32: k.sb(c, "h_" + name, shape, dt)
        self.s_in, self.s_row, self.s_tr, self.s_tt, self.s_mm, self.s_mx, self.s_pr, self.s_rs = (k.sem(f"h_{x}") for x in (
            "in", "row", "tr", "tt", "mm", "mx", "pr", "rs"))
        self.W, self.b_row, self.bo = sb("W", [P, 4, 2 * D]), sb("b_row", [1, 2 * D]), sb("bo", [1, D])
        self.row, self.rowT = sb("row", [P, 3, D]), sb("rowT", [P, 6, P])
        self.pt, self.pt2, self.pg, self.pm = (k.pb(c, "h_" + x, [P, 512]) for x in ("pt", "pt2", "pg", "pm"))

    def load(self, sp):
        a = self.k.a
        sp.dma_start(self.W[:, 0:2, :], a["L1_gnn_W_x2i"][0:D, :].rearrange("(c p) f -> p c f", p=P)).then_inc(self.s_in, 16)
        sp.dma_start(self.W[:, 2:4, :], a["L1_gnn_W_h2h"].rearrange("(c p) f -> p c f", p=P)).then_inc(self.s_in, 16)
        sp.dma_start(self.b_row[:, :], a["L1_gnn_b_x2i"].partition_broadcast(1)).then_inc(self.s_in, 16)
        sp.dma_start(self.bo[:, :], a["L1_mix_bout"].partition_broadcast(1)).then_inc(self.s_in, 16)

    def mask(self, pool):
        pass

    def set_up(self, dve):
        pass

    def ready(self, pe):
        pe.wait_ge(self.s_in, 64)

    def on_dve(self, dve, T, q, u):
        k = self.k
        if (q, u) == (0, 0):
            dve.tensor_copy(self.row[:, 0, :], k.AIN[:, at(T), :])
            dve.tensor_copy(self.row[:, 1, :], k.HB[:, at(T), :])
        if (q, u) == (0, 1):
            dve.tensor_copy(self.row[:, 2, :], k.XN[:, at(T), :]).then_inc(self.s_row, 1)
        if (q, u) == (3, 1):
            dve.wait_ge(self.s_mx, T + 1)
            dve.tensor_tensor(k.RES[:, at(T), :], k.RES[:, at(T), :], self.pm[:, 0:D], ALU.add).then_inc(self.s_rs, 1)

    def on_act(self, act, T, q):
        k = self.k
        if q == 0:
            act.wait_ge(self.s_tr, T + 1)
            act.activation(self.rowT[:, 0:4, :], self.pt[:, :].rearrange("p (c n) -> p c n", c=4), ACT.Copy)
            act.activation(self.rowT[:, 4:6, :], self.pt2[:, 0:D].rearrange("p (c n) -> p c n", c=2), ACT.Copy).then_inc(self.s_tt, 1)
        if q == 2:
            act.wait_ge(self.s_mm, T + 1)
            act.activation(k.AIN[:, at(T), :], self.pg[:, 0:D], ACT.Copy)
            act.activation(k.XN[:, at(T), :], self.pg[:, D:], ACT.Copy).then_inc(self.s_pr, 1)

    def on_pe(self, pe, T, q, u):
        ones, ident = self.k.ones[0:1, :], self.k.identf[:, :]
        if (q, u) == (0, 3):
            pe.wait_ge(self.s_row, T + 1)
            for j in range(6):
                dst = self.pt[:, j * P:(j + 1) * P] if j < 4 else self.pt2[:, (j - 4) * P:(j - 3) * P]
                last = pe.transpose(dst, self.row[:, j // 2, (j % 2) * P:(j % 2 + 1) * P], ident)
            last.then_inc(self.s_tr, 1)
        if q == 1 and u % 2 == 0:
            if u == 0:
                pe.wait_ge(self.s_tt, T + 1)
                pe.matmul(self.pg[:, :], ones, self.b_row[:, :], start=True, stop=False)
            j = u // 2
            last = pe.matmul(self.pg[:, :], self.rowT[:, j, :], self.W[:, j, :], start=False, stop=j == 3)
            if j == 3:
                last.then_inc(self.s_mm, 1)
        if (q, u) == (2, 0):
            pe.matmul(self.pm[:, 0:D], ones, self.bo[:, :], start=True, stop=False)
            for ch in range(2):
                last = pe.matmul(self.pm[:, 0:D], self.rowT[:, 4 + ch, :], self.k.M2[:, ch, :], start=False, stop=ch == 1)
            last.then_inc(self.s_mx, 1)
        if (q, u) == (3, 6):
            pe.wait_ge(self.s_pr, T + 1)
            pe.wait_ge(self.s_rs, T + 1)

    def finish_dve(self, dve):
        pass

    def finish_pe(self, pe):
        pass


class Kernel:
    def __init__(self, nc, a):
        self.nc, self.a = nc, a
        self.ctx = ExitStack()
        self.sems, self.live = None, []
        self.placing = []

    def sb(self, ctx, name, shape, dt=F32):
        return ctx.enter_context(self.nc.sbuf_tensor(name, shape, dt))

    def pb(self, ctx, name, shape, dt=F32):
        return ctx.enter_context(self.nc.psum_tensor(name, shape, dt))

    def sem(self, name):
        s = self.sems.enter_context(self.nc.semaphore(name))
        self.live.append(s)
        return s

    def soft_sems(self, name, n):
        return [self.ctx.enter_context(self.nc.semaphore(f"{name}{i}")) for i in range(n)]

    def stage(self, build, *args):
        with ExitStack() as self.sems:
            self.live = []
            build(*args)
            with self.nc.Block() as block:

                @block.gpsimd
                def _(pool):
                    for s in self.live:
                        pool.sem_clear(s)

    def dram(self, name, shape, dt=F32):
        return self.nc.dram_tensor(name, shape, dt, kind="Internal").ap()

    def constants(self):
        nc, c = self.nc, self.ctx
        self.identf = identf = self.sb(c, "identf", [P, P])
        self.identb = identb = self.sb(c, "identb", [P, P], BF16)
        self.ones = ones = self.sb(c, "ones", [P, P])
        self.lower = lower = self.sb(c, "lower", [P, P])
        self.iota_t = iota_t = self.sb(c, "iota_t", [P, NTL])
        self.eps = eps = self.sb(c, "eps", [P, 1])
        self.zeros = self.sb(c, "zeros", [P, P])
        scratch = ExitStack()
        iota_i = self.sb(scratch, "iota_i", [P, NTL], I32)
        c_set, c_io = self.sem("c_set"), self.sem("c_io")
        with scratch, nc.Block() as block:

            @block.gpsimd
            def _(pool):
                pool.iota(iota_i[:, :], pattern=[[1, NTL]], base=0, channel_multiplier=0).then_inc(c_io, 1)
                pool.memset(identf[:, :], 0.0)
                pool.memset(ones[:, :], 1.0)
                pool.memset(eps[:, :], EPS)
                pool.drain()
                pool.affine_select(out=identf[:, :], in_=identf[:, :], compare_op=ALU.not_equal, fill=1.0,
                                   base=0, pattern=[[-1, P]], channel_multiplier=1).then_inc(c_set, 1)
                pool.affine_select(out=lower[:, :], in_=ones[:, :], compare_op=ALU.is_gt, fill=0.0,
                                   base=0, pattern=[[1, P]], channel_multiplier=-1)

            @block.vector
            def _(dve):
                dve.wait_ge(c_io, 1)
                dve.tensor_copy(iota_t[:, :], iota_i[:, :])
                dve.wait_ge(c_set, 1)
                dve.tensor_copy(identb[:, :], identf[:, :])
                dve.memset(self.zeros[:, :], 0.0)

    def finish_stats(self, dve, st, mean, var, n):
        dve.tensor_tensor(mean, st[:, 0:n, 1], st[:, 0:n, 4], ALU.subtract)
        dve.tensor_tensor(var, st[:, 0:n, 2], st[:, 0:n, 5], ALU.add)
        dve.drain()
        dve.tensor_tensor(mean, mean, mean, ALU.mult)
        dve.tensor_scalar(var, var, 1.0 / D, None, ALU.mult)
        dve.drain()
        dve.scalar_tensor_tensor(out=var, in0=mean, scalar=0.25, in1=var, op0=ALU.mult, op1=ALU.add)
        dve.drain()
        dve.tensor_tensor(mean, st[:, 0:n, 1], st[:, 0:n, 4], ALU.add)
        dve.drain()
        return dve.tensor_scalar(mean, mean, 0.5, None, ALU.mult)

    def split3(self, dve, parts, x, rest):
        dve.tensor_copy(parts[0], x)
        dve.drain()
        dve.tensor_tensor(rest, x, parts[0], ALU.subtract)
        dve.drain()
        dve.tensor_copy(parts[1], rest)
        dve.drain()
        dve.tensor_tensor(parts[2], rest, parts[1], ALU.subtract)

    def norm_x(self):
        nc, a, XN, RES = self.nc, self.a, self.XN, self.RES
        z_tail, s_in, s_st, s_sd, s_xn = (self.sem(f"x_{x}") for x in ("z", "in", "st", "sd", "xn"))
        with ExitStack() as c:
            X = self.sb(c, "x_X", [P, NT, D])
            st = self.sb(c, "x_stats", [P, NT, 6])
            mean, rstd = self.sb(c, "x_mean", [P, NT]), self.sb(c, "x_rstd", [P, NT])
            with nc.Block() as block:

                @block.sync
                def _(sp):
                    sp.wait_ge(z_tail, 1)
                    sp.dma_start(X[:, 0:NT - 1, :], a["x"][0:(NT - 1) * P, :].rearrange("(t p) d -> p t d", p=P)).then_inc(s_in, 16)
                    sp.dma_start(X[0:TAIL, NT - 1, :], a["x"][(NT - 1) * P:N, :]).then_inc(s_in, 16)

                @block.vector
                def _(dve):
                    dve.memset(X[:, NT - 1, :], 0.0).then_inc(z_tail, 1)
                    dve.wait_ge(s_in, 32)
                    with dve.Fori(0, NT) as t:
                        dve.bn_stats(st[:, at(t), :], X[:, at(t), :])
                    dve.drain()
                    self.finish_stats(dve, st, mean[:, :], rstd[:, :], NT).then_inc(s_st, 1)
                    dve.wait_ge(s_sd, 1)
                    dve.reciprocal(rstd[:, :], rstd[:, :])
                    dve.drain()
                    with dve.Fori(0, NT) as t:
                        dve.tensor_scalar(XN[:, at(t), :], X[:, at(t), :], mean[:, at(t)], rstd[:, at(t)],
                                          ALU.subtract, ALU.mult).then_inc(s_xn, 1)

                @block.scalar
                def _(act):
                    act.wait_ge(s_st, 1)
                    act.activation(rstd[:, :], rstd[:, :], ACT.Sqrt, bias=self.eps[:, :]).then_inc(s_sd, 1)
                    act.wait_ge(s_xn, NT)
                    act.activation(RES[:, :, :], XN[:, :, :], ACT.Copy)

    def bucket(self, keep, which, key, other, cols, table, blocks):
        nc, a = self.nc, self.a
        n = self.sem
        s_in, s_c, s_pf, s_fill, s_ok, s_pc, s_pa = (n(f"{which}_{x}") for x in ("in", "cnt", "pref", "fill", "ok", "pc", "pa"))
        s_sc = self.soft_sems(f"{which}_sc", U)
        REC, IDX = self.sb(keep, f"{which}_rec", [EP, EC, 4]), self.sb(keep, f"{which}_idx", [EP, EC], I32)
        idx_r, rec_r = self.sb(keep, f"{which}_idx_r", [EP, 2, U // 2], I32), self.sb(keep, f"{which}_rec_r", [EP, 2, U // 2, 4])
        s_cp, s_turn = (self.ctx.enter_context(nc.semaphore(f"{which}_{x}")) for x in ("cp", "turn"))
        edges = (REC, IDX, idx_r, rec_r, s_sc, s_cp, s_turn, table)
        self.placing.append(edges)
        with ExitStack() as c:
            sb = lambda name, shape, dt=F32: self.sb(c, f"{which}_{name}", shape, dt)
            KI, OI = sb("ki", [EP, EC], I32), sb("oi", [EP, EC], I32)
            CI = sb("ci", [EP, 2, EC], I32)
            BL, MK, SC, POS = sb("bl", [EP, EC], BF16), sb("mk", [EP, 2, EC], BF16), sb("scn", [EP, 2, EC]), sb("pos", [EP, EC])
            ZERO = sb("zero", [EP, EC])
            CNT = sb("cnt", [EP, NT])
            TI, TT, CUM, CUME, BASE = sb("ti", [P, NT], I32), sb("tt", [P, NT]), sb("cum", [P, NT]), sb("cume", [P, NT]), sb("base", [P, NT])
            FILL = sb("fillb", [P, NTL, 4])
            bl1 = sb("bl1", [1, NTL])
            pp = self.pb(c, f"{which}_pp", [P, 2, NT])
            with nc.Block() as block:

                @block.sync
                def _(sp):
                    sp.dma_start(KI[:, :], key.rearrange("(p e) -> p e", p=EP)).then_inc(s_in, 16)
                    sp.dma_start(OI[:, :], other.rearrange("(p e) -> p e", p=EP)).then_inc(s_in, 16)
                    for j, x in enumerate(cols):
                        dst = CI[:, j, :] if x.dtype == I32 else CI[:, j, :].bitcast(F32)
                        sp.dma_start(dst, x.rearrange("(p e) -> p e", p=EP)).then_inc(s_in, 16)
                    sp.wait_ge(s_fill, 1)
                    sp.dma_start(table.rearrange("(p t) c -> p t c", p=P), FILL[:, :, :]).then_inc(s_fill, 16)

                @block.vector
                def _(dve):
                    dve.memset(FILL[:, :, :], 0.0)
                    dve.memset(ZERO[:, :], 0.0)
                    dve.memset(POS[:, :], 0.0)
                    dve.memset(bl1[:, :], 0.0)
                    dve.memset(blocks[:, :], 0)
                    dve.drain()
                    dve.memset(FILL[:, :, 1:2], -1.0).then_inc(s_fill, 1)
                    dve.wait_ge(s_in, 16 * (2 + len(cols)))
                    dve.tensor_copy(SC[:, 0, :], KI[:, :])
                    dve.tensor_scalar(IDX[:, :], KI[:, :], 7, None, ALU.arith_shift_right)
                    dve.drain()
                    dve.tensor_copy(BL[:, :], IDX[:, :])
                    dve.tensor_copy(REC[:, :, 0], OI[:, :])
                    for j, x in enumerate(cols):
                        dve.tensor_copy(REC[:, :, 2 + j], CI[:, j, :] if x.dtype == I32 else CI[:, j, :].bitcast(F32))
                    if len(cols) == 1:
                        dve.tensor_copy(REC[:, :, 3], ZERO[:, :])
                    dve.drain()
                    dve.scalar_tensor_tensor(out=REC[:, :, 1], in0=BL[:, :], scalar=-float(P), in1=SC[:, 0, :], op0=ALU.mult, op1=ALU.add)
                    for b in range(NT):
                        dve.tensor_scalar(MK[:, 0, :], BL[:, :], float(b), None, ALU.is_equal, ALU.add, accum_out=CNT[:, b:b + 1])
                        dve.drain()
                    dve.tensor_copy(CNT[:, :], CNT[:, :]).then_inc(s_c, 1)
                    dve.wait_ge(s_pf, 1)
                    dve.tensor_scalar(TT[:, :], pp[:, 1, :], float(P - 1), None, ALU.add)
                    dve.drain()
                    dve.tensor_copy(TI[:, :], TT[:, :])
                    dve.drain()
                    dve.tensor_scalar(TI[:, :], TI[:, :], 7, None, ALU.arith_shift_right)
                    dve.drain()
                    dve.tensor_copy(TT[:, :], TI[:, :])
                    dve.drain()
                    dve.tensor_tensor_scan(CUM[:, :], TT[:, :], self.zeros[:, 0:NT], 0.0, ALU.add, ALU.add)
                    dve.drain()
                    dve.tensor_tensor(CUME[:, :], CUM[:, :], TT[:, :], ALU.subtract)
                    dve.drain()
                    dve.scalar_tensor_tensor(out=BASE[:, :], in0=CUME[:, :], scalar=float(P), in1=pp[:, 0, :], op0=ALU.mult, op1=ALU.add)
                    dve.drain()
                    dve.tensor_scalar(BASE[:, :], BASE[:, :], -1.0, None, ALU.add)
                    dve.drain()
                    for b in range(1, NT):
                        dve.scalar_tensor_tensor(out=bl1[:, :], in0=self.iota_t[0:1, :], scalar=CUME[0:1, b:b + 1], in1=bl1[:, :],
                                                 op0=ALU.is_ge, op1=ALU.add)
                        dve.drain()
                    dve.tensor_copy(blocks[:, U:U + NTL], bl1[:, :])
                    def step(i, u):
                        on, b, r = tile(i, u, 0, 2, NT)
                        if on:
                            dve.tensor_scalar(MK[:, r, :], BL[:, :], self.iota_t[0:EP, at(b)], None, ALU.is_equal)
                            dve.drain()
                            need(dve, s_pa, b - 1)
                            dve.tensor_tensor_scan(SC[:, r, :], MK[:, r, :], ZERO[:, :], 0.0, ALU.add, ALU.add)
                            dve.drain()
                            dve.scalar_tensor_tensor(out=SC[:, r, :], in0=SC[:, r, :], scalar=BASE[0:EP, at(b)], in1=MK[:, r, :], op0=ALU.add, op1=ALU.mult).then_inc(s_pc, 1)
                    steps(dve, NT, 2, 0, step)
                    dve.wait_ge(s_pa, NT)
                    dve.tensor_copy(IDX[:, :], POS[:, :])
                    dve.drain()
                    dve.tensor_scalar(KI[:, :], IDX[:, :], P - 1, None, ALU.bitwise_and)
                    dve.tensor_scalar(IDX[:, :], IDX[:, :], 7, None, ALU.arith_shift_right)
                    dve.drain()
                    dve.scalar_tensor_tensor(out=IDX[:, :], in0=KI[:, :], scalar=float(NTL), in1=IDX[:, :], op0=ALU.mult, op1=ALU.add).then_inc(s_ok, 1)

                @block.tensor
                def _(pe):
                    pe.wait_ge(s_c, 1)
                    pe.matmul(pp[:, 0, :], self.lower[0:EP, :], CNT[:, :], start=True, stop=True)
                    pe.matmul(pp[:, 1, :], self.ones[0:EP, :], CNT[:, :], start=True, stop=True).then_inc(s_pf, 1)

                @block.gpsimd
                def _(pool):
                    def step(i, u):
                        on, b, r = tile(i, u, 0, 2, NT)
                        if on:
                            pool.wait_ge(s_pc, b + 1)
                            need(pool, s_pa, b)
                            pool.tensor_tensor(POS[:, :], POS[:, :], SC[:, r, :], ALU.add).then_inc(s_pa, 1)
                    steps(pool, NT, 2, 0, step)
                    pool.wait_ge(s_fill, 17)
                    pool.wait_ge(s_ok, 1)
                    self.place_edges(pool, edges, 0)
                    with pool.Fori(1, PEEL) as i:
                        self.place_edges(pool, edges, i)

    def place_edges(self, pool, edges, i):
        REC, IDX, idx_r, rec_r, s_sc, s_cp, s_turn, table = edges
        for h in range(2):
            for r in range(U // 2):
                need(pool, s_sc[h * U // 2 + r], i * 16)
            pool.tensor_copy(idx_r[:, h, :], IDX[:, ds(i * U + h * (U // 2), U // 2)]).then_inc(s_cp, 1)
            pool.tensor_copy(rec_r[:, h, :, :], REC[:, ds(i * U + h * (U // 2), U // 2), :]).then_inc(s_cp, 1)
            pool.wait_ge(s_cp, i * 4 + (2 * h + 2))
            pool.sem_inc(s_turn, 1)
            for r in range(U // 2):
                pool.indirect_dma_start(table, bass.IndirectOffsetOnAxis(idx_r[:, h, r:r + 1], 0),
                                        rec_r[:, h, r, :], None).then_inc(s_sc[h * U // 2 + r], 16)

    def last_edges(self, pool):
        with pool.Fori(PEEL + LAYERS * BESIDE[0], EC // U) as i:
            self.place_edges(pool, self.placing[0], i)
        for s in self.placing[0][4]:
            pool.wait_ge(s, 16 * (EC // U))

    def project(self):
        nc, a, XN = self.nc, self.a, self.XN
        QS, VS, k_tab, v_tab = self.QS, self.VS, self.k_tab, self.v_tab
        s_in, s_q = self.sem("p_in"), self.sem("p_q")
        s_row, s_tr, s_tt, s_mm = (self.sem(f"p_{x}") for x in ("row", "tr", "tt", "mm"))
        s_kv, s_vq = self.sem("p_kv"), self.sem("p_vq")
        s_out = [self.sem(f"p_out{i}") for i in range(2)]
        with ExitStack() as c:
            W = self.sb(c, "p_W", [P, 2, 3 * D])
            bias = self.sb(c, "p_bias", [P, 3, D])
            q01 = self.sb(c, "p_q01", [P, 2])
            row = self.sb(c, "p_rows", [P, 2, D])
            rowT = self.sb(c, "p_rowT", [P, 2, 2, P])
            kv = self.sb(c, "p_kvrow", [P, 2, 2, D])
            qf = self.sb(c, "p_qf", [P, 2, D])
            pt = [self.pb(c, f"p_pt{i}", [P, 2, P]) for i in range(2)]
            pqk = [self.pb(c, f"p_pqk{i}", [P, 2 * D]) for i in range(2)]
            pv = [self.pb(c, f"p_pv{i}", [P, D]) for i in range(2)]
            with nc.Block() as block:

                @block.sync
                def _(sp):
                    sp.dma_start(q01[:, :], a["L0_gnn_query_emb"].rearrange("(c p) -> p c", p=P)).then_inc(s_in, 16)
                    for j, w in enumerate("qkv"):
                        sp.dma_start(W[:, :, j * D:(j + 1) * D], a[f"L0_gnn_W{w}"].rearrange("(c p) f -> p c f", p=P)).then_inc(s_in, 16)
                        sp.dma_start(bias[:, j, :], a[f"L0_gnn_b{w}"].partition_broadcast(P)).then_inc(s_in, 16)

                    def step(i, u):
                        on, t, r = tile(i, u, 1, NU, NT)
                        if on:
                            sp.wait_ge(s_kv, t + 1)
                            sp.dma_start(k_tab[ds(t * P, P), :], kv[:, r % 2, 0, :]).then_inc(s_out[r % 2], 16)
                            sp.dma_start(v_tab[ds(t * P, P), :], kv[:, r % 2, 1, :]).then_inc(s_out[r % 2], 16)
                    steps(sp, NT, NU, 1, step)
                    sp.wait_ge(s_out[0], 32 * (NT - NT // 2))
                    sp.wait_ge(s_out[1], 32 * (NT // 2))

                @block.vector
                def _(dve):
                    dve.wait_ge(s_in, 16 * 7)
                    dve.tensor_scalar(q01[:, :], q01[:, :], 0.1, None, ALU.mult)
                    dve.drain()
                    dve.sem_inc(s_q, 1)

                    def step(i, u):
                        on, t, r = tile(i, u, 0, NU, NT)
                        if on:
                            need(dve, s_tr, t - 1)
                            dve.tensor_copy(row[:, r % 2, :], XN[:, at(t), :]).then_inc(s_row, 1)
                        on, t, r = tile(i, u, 2, NU, NT)
                        if on:
                            b = r % 2
                            dve.wait_ge(s_mm, t + 1)
                            need(dve, s_out[b], 32 * uses(i, u, 2, NU, 2))
                            dve.tensor_tensor(kv[:, b, 0, :], pqk[b][:, D:], bias[:, 1, :], ALU.add)
                            dve.tensor_tensor(kv[:, b, 1, :], pv[b][:, :], bias[:, 2, :], ALU.add)
                            dve.tensor_tensor(qf[:, 0, :], pqk[b][:, 0:D], bias[:, 0, :], ALU.add).then_inc(s_vq, 1)
                            dve.drain()
                            dve.tensor_copy(VS[:, at(t), :], kv[:, b, 1, :]).then_inc(s_kv, 1)
                            dve.tensor_scalar(qf[:, 0, :], qf[:, 0, :], HD ** -0.5, None, ALU.mult)
                            dve.drain()
                            self.split3(dve, [QS[:, at(t), j, :] for j in range(3)], qf[:, 0, :], qf[:, 1, :])
                    steps(dve, NT, NU, 2, step)

                @block.scalar
                def _(act):
                    act.wait_ge(s_q, 1)

                    def step(i, u):
                        on, t, r = tile(i, u, 0, NU, NT)
                        if on:
                            b = r % 2
                            act.wait_ge(s_tr, t + 1)
                            need(act, s_mm, t - 1)
                            act.activation(rowT[:, b, 0, :], pt[b][:, 0, :], ACT.Identity, bias=q01[:, 0:1])
                            act.activation(rowT[:, b, 1, :], pt[b][:, 1, :], ACT.Identity, bias=q01[:, 1:2]).then_inc(s_tt, 1)
                    steps(act, NT, NU, 0, step)

                @block.tensor
                def _(pe):
                    pe.wait_ge(s_in, 16 * 7)

                    def step(i, u):
                        on, t, r = tile(i, u, 0, NU, NT)
                        if on:
                            pe.wait_ge(s_row, t + 1)
                            need(pe, s_tt, t - 1)
                            pe.transpose(pt[r % 2][:, 0, :], row[:, r % 2, 0:P], self.identf[:, :])
                            pe.transpose(pt[r % 2][:, 1, :], row[:, r % 2, P:], self.identf[:, :]).then_inc(s_tr, 1)
                        on, t, r = tile(i, u, 1, NU, NT)
                        if on:
                            b = r % 2
                            pe.wait_ge(s_tt, t + 1)
                            need(pe, s_vq, t - 1)
                            for ch in range(2):
                                pe.matmul(pqk[b][:, :], rowT[:, b, ch, :], W[:, ch, 0:2 * D], start=ch == 0, stop=ch == 1)
                            for ch in range(2):
                                last = pe.matmul(pv[b][:, :], rowT[:, b, ch, :], W[:, ch, 2 * D:], start=ch == 0, stop=ch == 1)
                            last.then_inc(s_mm, 1)
                    steps(pe, NT, NU, 1, step)

    def load_blocks(self, eng, regs, table, i, lag):
        first = i * U + (U - lag)
        eng.load(regs, table[0:1, ds(first, U)])
        return [eng.snap(r, min_val=0, max_val=NT - 1) for r in regs]

    def refill(self, act, i, h, s_got, s_idx, idx, slots):
        for r in range(h * U // 2, h * U // 2 + U // 2):
            need(act, s_got[r], i * 16)
        act.activation(idx[:, h, :], slots[:, ds(i * U + h * (U // 2), U // 2), 0], ACT.Copy).then_inc(s_idx, 1)

    def att_scores(self, c0, by_dst):
        nc, a, QS = self.nc, self.a, self.QS
        n = self.sem
        SL = self.SL = self.sb(c0, "SL", [P, NTL + U, 4])
        SALL = self.SALL = self.sb(c0, "SALL", [P, NTL, HEADS])
        MX = self.MX = self.sb(c0, "MX", [P, NT, HEADS])
        s_in, s_set, s_rel = n("a_in"), n("a_set"), n("a_rel")
        s_idx, s_turn, s_aw, s_oh, s_tr, s_ev, s_q, s_kf, s_s = (n(f"a_{x}") for x in ("idx", "turn", "aw", "oh", "tr", "ev", "q", "kf", "s"))
        s_keep, s_st, s_hi, s_lo, s_mb, s_mx = (n(f"a_{x}") for x in ("keep", "st", "hi", "lo", "mb", "mx"))
        s_got = self.soft_sems("a_got", U)
        with ExitStack() as c:
            sb = lambda name, shape, dt=F32: self.sb(c, "a_" + name, shape, dt)
            pb = lambda name, shape, dt=F32: self.pb(c, "a_" + name, shape, dt)
            idx = sb("idx_", [P, 2, U // 2], I32)
            KG = sb("KG", [P, U, D])
            relf, relr, rel3 = sb("relf", [NREL, HD]), sb("relr", [NREL, HD]), sb("rel3", [NREL, 3, HD], BF16)
            sel = sb("sel", [36, HEADS, P], BF16)
            hl = sb("hl", [36, 4, P], BF16)
            away, oht = sb("away", [P, 2, P + NREL], BF16), sb("oht", [P, 2, P + NREL], BF16)
            ohT, otT, mb = sb("ohT", [P, 2, P], BF16), sb("otT", [NREL, 2, P], BF16), sb("mbias", [P, 8, P], BF16)
            t1, S4, tm = sb("t1", [P, 2, D]), sb("S4", [P, 4, HEADS]), sb("tm", [P, 2, HEADS])
            ptr = [pb(f"ptr{b}", [P, 2, P], BF16) for b in range(2)]
            pq = [pb(f"pq{b}", [P, D + HD]) for b in range(2)]
            pst = [pb(f"pst{b}", [P, P]) for b in range(2)]
            pmb = [pb(f"pmb{b}", [P, HEADS, P]) for b in range(2)]
            with nc.Block() as block:

                @block.sync
                def _(sp):
                    sp.dma_start(SL[:, 0:NTL, :], by_dst.rearrange("(p t) c -> p t c", p=P)).then_inc(s_in, 16)
                    sp.dma_start(relf[:, :], a["L0_gnn_rel_w"]).then_inc(s_rel, 16)

                @block.gpsimd
                def _(pool):
                    pool.memset(sel[:, :, :], 0.0)
                    pool.memset(hl[:, :, :], 0.0).then_inc(s_set, 1)
                    pool.drain()
                    for b in range(2):
                        pool.affine_select(out=sel[:, :, :], in_=sel[:, :, :], compare_op=ALU.not_equal, fill=1.0,
                                           base=-32 * b, pattern=[[-1, HEADS], [0, P]], channel_multiplier=1).then_inc(s_set, 1)
                        pool.drain()

                    def step(i, u):
                        on, t, r = tile(i, u, 0, U, NTL)
                        if on:
                            need(pool, s_kf, t - (U - 1))
                            if r % (U // 2) == 0:
                                pool.wait_ge(s_idx, i * 2 + (1 + r // (U // 2)))
                            pool.sem_inc(s_turn, 1)
                            pool.indirect_dma_start(KG[:, r, :], None, self.k_tab, bass.IndirectOffsetOnAxis(idx[:, r // (U // 2), ds(r % (U // 2), 1)], 0)).then_inc(s_got[r], 16)
                    steps(pool, NTL, U, 0, step, 2)

                @block.vector
                def _(dve):
                    dve.memset(MX[:, :, :], -BIG)
                    dve.memset(SL[:, NTL:, :], 0.0).then_inc(s_set, 1)
                    dve.wait_ge(s_rel, 16)
                    dve.tensor_scalar(relf[:, :], relf[:, :], 0.2, None, ALU.mult)
                    dve.drain()
                    self.split3(dve, [rel3[:, j, :] for j in range(3)], relf[:, :], relr[:, :])
                    dve.drain()
                    dve.sem_inc(s_rel, 1)
                    dve.wait_ge(s_in, 16)
                    dve.wait_ge(s_set, 4)
                    regs = [dve.alloc_register(f"a_dblk{j}") for j in range(U)]
                    blk = [None]

                    def step(i, u):
                        if u % U == 0:
                            blk[0] = self.load_blocks(dve, regs, self.blk_dst, i + u // U, 8)
                        on_s, t_s, r_s = tile(i, u, 4, U, NTL)
                        if on_s:
                            b_s = r_s % 2
                            dve.wait_ge(s_q, t_s + 1)
                            dve.wait_ge(s_got[r_s], i * 16 + 16 * (1 + (u - 4) // U))
                            dve.tensor_tensor(t1[:, b_s, :], KG[:, r_s, :], pq[b_s][:, D:].unsqueeze(1).to_broadcast([P, HEADS, HD]), ALU.add).then_inc(s_kf, 1)
                        on, t, r = tile(i, u, 6, U, NTL)
                        if on:
                            dve.wait_ge(s_hi, t + 1)
                            dve.tensor_tensor(hl[32:36, r % 4, :], pst[r % 2][0:HEADS, :], hl[0:HEADS, r % 4, :], ALU.subtract).then_inc(s_lo, 1)
                        if on_s:
                            dve.drain()
                            dve.tensor_tensor(t1[:, b_s, :], t1[:, b_s, :], pq[b_s][:, 0:D], ALU.mult).then_inc(s_s, 1)
                        on_m, t_m, r_m = tile(i, u, 8, U, NTL)
                        if on_m:
                            dve.wait_ge(s_mb, t_m + 1)
                            dve.tensor_reduce(tm[:, r_m % 2, :], pmb[r_m % 2][:, :, :], AX.X, ALU.max)
                        dve.drain()
                        if on_s:
                            need(dve, s_keep, t_s - 3)
                            need(dve, s_st, t_s - 3)
                            dve.tensor_reduce(S4[:, r_s % 4, :], t1[:, b_s, :].rearrange("p (h d) -> p h d", h=HEADS), AX.X, ALU.add).then_inc(s_s, 1)
                        if on_m:
                            k = blk[0][u % U]
                            dve.tensor_tensor(MX[:, at(k), :], MX[:, at(k), :], tm[:, r_m % 2, :], ALU.max).then_inc(s_mx, 1)
                    steps(dve, NTL, U, 8, step, 2)

                @block.scalar
                def _(act):
                    act.wait_ge(s_in, 16)
                    act.wait_ge(s_set, 4)
                    for h in range(2):
                        self.refill(act, 0, h, s_got, s_idx, idx, SL)

                    def step(i, u):
                        on, t, r = tile(i, u, 0, U, NTL)
                        if on:
                            need(act, s_oh, t - 1)
                            act.activation(away[:, r % 2, 0:P], self.iota_t[:, 0:P], ACT.Abs, scale=-1.0, bias=SL[:, at(t), 1])
                            act.activation(away[:, r % 2, P:], self.iota_t[:, 0:NREL], ACT.Abs, scale=-1.0, bias=SL[:, at(t), 2]).then_inc(s_aw, 1)
                        on, t, r = tile(i, u, 1, U, NTL)
                        if on:
                            act.wait_ge(s_aw, t + 1)
                            need(act, s_tr, t - 1)
                            act.activation(oht[:, r % 2, :], away[:, r % 2, :], ACT.Relu, scale=-1.0, bias=self.ones[:, 0:1]).then_inc(s_oh, 1)
                        on, t, r = tile(i, u, 2, U, NTL)
                        if on:
                            b = r % 2
                            act.wait_ge(s_tr, t + 1)
                            need(act, s_q, t - 1)
                            act.activation(ohT[:, b, :], ptr[b][:, 0, :], ACT.Copy)
                            act.activation(otT[:, b, :], ptr[b][0:NREL, 1, :], ACT.Copy)
                            need(act, s_mb, t - 7)
                            act.activation(mb[:, r % 8, :], ptr[b][:, 0, :], ACT.Copy, scale=BIG, bias=-BIG).then_inc(s_ev, 1)
                        on, t, r = tile(i, u, 5, U, NTL)
                        if on:
                            act.wait_ge(s_s, t * 2 + 2)
                            act.activation(SALL[:, at(t), :], S4[:, r % 4, :], ACT.Copy).then_inc(s_keep, 1)
                            act.wait_ge(s_st, t + 1)
                            need(act, s_mb, t - 3)
                            act.activation(hl[0:HEADS, r % 4, :], pst[r % 2][0:HEADS, :], ACT.Copy).then_inc(s_hi, 1)
                        if u == U // 2 + 3 or u == 3:
                            h = 0 if u > 3 else 1
                            if not isinstance(i, int) or (u > 3 and i < NTL // U) or (u == 3 and 0 < i < NTL // U):
                                self.refill(act, i + 1 if u > 3 else i, h, s_got, s_idx, idx, SL)
                    steps(act, NTL, U, 5, step, 2)

                @block.tensor
                def _(pe):
                    pe.wait_ge(s_rel, 17)
                    pe.wait_ge(s_set, 4)
                    regs = [pe.alloc_register(f"a_pblk{j}") for j in range(U)]
                    blk = [None]

                    def step(i, u):
                        if u % U == 0:
                            blk[0] = self.load_blocks(pe, regs, self.blk_dst, i + u // U, 3)
                        on, t, r = tile(i, u, 2, U, NTL)
                        if on:
                            b = r % 2
                            pe.wait_ge(s_oh, t + 1)
                            need(pe, s_ev, t - 1)
                            pe.transpose(ptr[b][:, 0, :], oht[:, b, 0:P], self.identb[:, :])
                            pe.transpose(ptr[b][0:NREL, 1, :], oht[:, b, P:], self.identb[:, :]).then_inc(s_tr, 1)
                        on, t, r = tile(i, u, 3, U, NTL)
                        if on:
                            b, k = r % 2, blk[0][u % U]
                            pe.wait_ge(s_ev, t + 1)
                            need(pe, s_s, t * 2 - 3)
                            for j in range(3):
                                pe.matmul(pq[b][:, 0:D], ohT[:, b, :], QS[:, at(k), j, :], start=j == 0, stop=j == 2)
                            for j in range(3):
                                last = pe.matmul(pq[b][:, D:], otT[:, b, :], rel3[:, j, :], start=j == 0, stop=j == 2)
                            last.then_inc(s_q, 1)
                        on, t, r = tile(i, u, 5, U, NTL)
                        if on:
                            pe.wait_ge(s_s, t * 2 + 2)
                            need(pe, s_lo, t - 1)
                            pe.transpose(pst[r % 2][0:HEADS, :], S4[:, r % 4, :], self.identf[:, :]).then_inc(s_st, 1)
                        on, t, r = tile(i, u, 7, U, NTL)
                        if on:
                            b = r % 2
                            pe.wait_ge(s_lo, t + 1)
                            need(pe, s_mx, t - 1)
                            pe.matmul(pmb[b][:, :, :], self.identb[:, :], mb[:, r % 8, :].unsqueeze(1).to_broadcast([P, HEADS, P]), start=True, stop=False)
                            for h in range(HEADS):
                                last = pe.matmul(pmb[b][:, h, :], sel[:, h, :], hl[:, r % 4, :], start=False, stop=h == HEADS - 1)
                            last.then_inc(s_mb, 1)
                    steps(pe, NTL, U, 7, step, 2)

    def att_sums(self):
        nc = self.nc
        SL, SALL, MX, ACC = self.SL, self.SALL, self.MX, self.ACC
        n = self.sem
        s_set, s_idx, s_turn, s_oh, s_tr, s_ev, s_me, s_d, s_ex = (n(f"s_{x}") for x in ("set", "idx", "turn", "oh", "tr", "ev", "me", "d", "ex"))
        s_vw, s_pv, s_acc = n("s_vw"), n("s_pv"), n("s_acc")
        s_got = self.soft_sems("s_got", U)
        with ExitStack() as c:
            sb = lambda name, shape, dt=F32: self.sb(c, "s_" + name, shape, dt)
            pb = lambda name, shape, dt=F32: self.pb(c, "s_" + name, shape, dt)
            idx = sb("idx_", [P, 2, U // 2], I32)
            VG = sb("VG", [P, U, D])
            MX3, rest = sb("MX3", [P, 3, NT, HEADS], BF16), sb("rest", [P, NT, HEADS])
            oh, ohT = sb("oh_", [P, U, P]), sb("ohT", [P, 2, P], BF16)
            dd = sb("dd", [P, 2, HEADS])
            VW = sb("VW", [P, 4, D + HEADS])
            ptr = [pb(f"ptr{b}", [P, P]) for b in range(2)]
            pme = [pb(f"pme{b}", [P, HEADS]) for b in range(2)]
            ppv = [pb(f"ppv{b}", [P, D + HEADS]) for b in range(2)]
            with nc.Block() as block:

                @block.gpsimd
                def _(pool):
                    def step(i, u):
                        on, t, r = tile(i, u, 0, U, NTL)
                        if on:
                            need(pool, s_vw, t - (U - 1))
                            if r % (U // 2) == 0:
                                pool.wait_ge(s_idx, i * 2 + (1 + r // (U // 2)))
                            pool.sem_inc(s_turn, 1)
                            pool.indirect_dma_start(VG[:, r, :], None, self.v_tab, bass.IndirectOffsetOnAxis(idx[:, r // (U // 2), ds(r % (U // 2), 1)], 0)).then_inc(s_got[r], 16)
                    steps(pool, NTL, U, 0, step)

                @block.vector
                def _(dve):
                    dve.memset(ACC[:, :, :], 0.0)
                    self.split3(dve, [MX3[:, j, :, :] for j in range(3)], MX[:, :, :], rest[:, :, :])
                    dve.drain()
                    dve.sem_inc(s_set, 1)
                    regs = [dve.alloc_register(f"s_dblk{j}") for j in range(U)]
                    blk = [None]

                    def step(i, u):
                        if u % U == 0:
                            blk[0] = self.load_blocks(dve, regs, self.blk_dst, i + u // U, 6)
                        on, t, r = tile(i, u, 0, U, NTL)
                        if on:
                            need(dve, s_pv, t - (U - 1))
                            dve.tensor_scalar(oh[:, r, :], self.iota_t[:, 0:P], SL[:, at(t), 1], None, ALU.is_equal).then_inc(s_oh, 1)
                        on, t, r = tile(i, u, 3, U, NTL)
                        if on:
                            dve.wait_ge(s_me, t + 1)
                            need(dve, s_ex, t - 1)
                            dve.tensor_tensor(dd[:, r % 2, :], SALL[:, at(t), :], pme[r % 2][:, :], ALU.subtract).then_inc(s_d, 1)
                        on, t, r = tile(i, u, 4, U, NTL)
                        if on:
                            dve.wait_ge(s_ex, t + 1)
                            dve.wait_ge(s_got[r], i * 16 + 16 * (1 + (u - 4) // U))
                            dve.tensor_tensor(VW[:, r % 4, 0:D].rearrange("p (h d) -> p h d", h=HEADS), VG[:, r, :].rearrange("p (h d) -> p h d", h=HEADS),
                                              VW[:, r % 4, D:].unsqueeze(2).to_broadcast([P, HEADS, HD]), ALU.mult).then_inc(s_vw, 1)
                        on, t, r = tile(i, u, 6, U, NTL)
                        if on:
                            k = blk[0][u % U]
                            dve.wait_ge(s_pv, t + 1)
                            need(dve, s_acc, t)
                            dve.tensor_tensor(ACC[:, at(k), :], ACC[:, at(k), :], ppv[r % 2][:, :], ALU.add).then_inc(s_acc, 1)
                    steps(dve, NTL, U, 6, step)

                @block.scalar
                def _(act):
                    for h in range(2):
                        self.refill(act, 0, h, s_got, s_idx, idx, SL)

                    def step(i, u):
                        on, t, r = tile(i, u, 1, U, NTL)
                        if on:
                            act.wait_ge(s_tr, t + 1)
                            need(act, s_me, t - 1)
                            act.activation(ohT[:, r % 2, :], ptr[r % 2][:, :], ACT.Copy).then_inc(s_ev, 1)
                        on, t, r = tile(i, u, 3, U, NTL)
                        if on:
                            act.wait_ge(s_d, t + 1)
                            need(act, s_pv, t - 3)
                            act.activation(VW[:, r % 4, D:], dd[:, r % 2, :], ACT.Exp).then_inc(s_ex, 1)
                        if u == U // 2 + 3 or u == 3:
                            h = 0 if u > 3 else 1
                            if not isinstance(i, int) or (u > 3 and i < NTL // U) or (u == 3 and 0 < i < NTL // U):
                                self.refill(act, i + 1 if u > 3 else i, h, s_got, s_idx, idx, SL)
                    steps(act, NTL, U, 3, step)

                @block.tensor
                def _(pe):
                    pe.wait_ge(s_set, 1)
                    regs = [pe.alloc_register(f"s_pblk{j}") for j in range(U)]
                    blk = [None]

                    def step(i, u):
                        if u % U == 0:
                            blk[0] = self.load_blocks(pe, regs, self.blk_dst, i + u // U, 2)
                        on, t, r = tile(i, u, 1, U, NTL)
                        if on:
                            pe.wait_ge(s_oh, t + 1)
                            need(pe, s_ev, t - 1)
                            pe.transpose(ptr[r % 2][:, :], oh[:, r, :], self.identf[:, :]).then_inc(s_tr, 1)
                        on, t, r = tile(i, u, 2, U, NTL)
                        if on:
                            k = blk[0][u % U]
                            pe.wait_ge(s_ev, t + 1)
                            need(pe, s_d, t - 1)
                            for j in range(3):
                                last = pe.matmul(pme[r % 2][:, :], ohT[:, r % 2, :], MX3[:, j, at(k), :], start=j == 0, stop=j == 2)
                            last.then_inc(s_me, 1)
                        on, t, r = tile(i, u, 5, U, NTL)
                        if on:
                            pe.wait_ge(s_vw, t + 1)
                            need(pe, s_acc, t - 1)
                            pe.matmul(ppv[r % 2][:, :], oh[:, r, :], VW[:, r % 4, :], start=True, stop=True).then_inc(s_pv, 1)
                    steps(pe, NTL, U, 5, step)

    def att_out(self):
        nc, a = self.nc, self.a
        ACC, VS, XN, RES = self.ACC, self.VS, self.XN, self.RES
        n = self.sem
        s_x, s_xr, s_in, s_row, s_tr, s_tt, s_mm, s_g, s_st, s_sd = (n(f"o_{x}") for x in ("x", "xr", "in", "row", "tr", "tt", "mm", "g", "st", "sd"))
        with ExitStack() as c:
            sb = lambda name, shape, dt=F32: self.sb(c, "o_" + name, shape, dt)
            pb = lambda name, shape, dt=F32: self.pb(c, "o_" + name, shape, dt)
            X = sb("X", [P, NT, D])
            W, vec = sb("W", [P, 2, D]), sb("vec", [P, 3, D])
            none, rden = sb("none", [P, NT, HEADS]), sb("rden", [P, NT, HEADS])
            row, alt, rowT = sb("rows", [P, 2, D]), sb("alt", [P, D]), sb("rowT", [P, 2, 2, P])
            st, mean, rstd = sb("stats", [P, NT, 6]), sb("mean", [P, NT]), sb("rstd", [P, NT])
            pt = [pb(f"pt{b}", [P, 2, P]) for b in range(2)]
            po = [pb(f"po{b}", [P, D]) for b in range(2)]
            heads = lambda x: x.rearrange("p (h d) -> p h d", h=HEADS)
            with nc.Block() as block:

                @block.sync
                def _(sp):
                    sp.dma_start(W[:, :, :], a["L0_gnn_Wo"].rearrange("(c p) f -> p c f", p=P)).then_inc(s_in, 16)
                    for j, x in enumerate(("bo", "gamma", "beta")):
                        sp.dma_start(vec[:, j, :], a[f"L0_gnn_{x}"].partition_broadcast(P)).then_inc(s_in, 16)
                    sp.wait_ge(s_x, 1)
                    sp.dma_start(X[:, 0:NT - 1, :], a["x"][0:(NT - 1) * P, :].rearrange("(t p) d -> p t d", p=P)).then_inc(s_x, 16)
                    sp.dma_start(X[0:TAIL, NT - 1, :], a["x"][(NT - 1) * P:N, :]).then_inc(s_x, 16)

                @block.gpsimd
                def _(pool):
                    pool.wait_ge(s_x, 33)
                    pool.wait_ge(s_in, 64)
                    with pool.Fori(0, NT) as t:
                        pool.tensor_tensor(X[:, at(t), :], X[:, at(t), :], vec[:, 2, :], ALU.add)
                    pool.drain()
                    with pool.Fori(0, NT) as t:
                        pool.tensor_tensor(RES[:, at(t), :], RES[:, at(t), :], X[:, at(t), :], ALU.add).then_inc(s_xr, 1)

                @block.vector
                def _(dve):
                    dve.memset(X[:, NT - 1, :], 0.0).then_inc(s_x, 1)
                    dve.tensor_scalar(none[:, :, :], ACC[:, :, D:], 0.0, None, ALU.is_equal)
                    dve.drain()
                    dve.tensor_tensor(rden[:, :, :], ACC[:, :, D:], none[:, :, :], ALU.add)
                    dve.drain()
                    dve.reciprocal(rden[:, :, :], rden[:, :, :])
                    dve.wait_ge(s_in, 64)
                    dve.drain()

                    def step(i, u):
                        on, t, r = tile(i, u, 0, NU, NT)
                        if on:
                            b = r % 2
                            need(dve, s_tr, t - 1)
                            need(dve, s_row, t)
                            dve.tensor_tensor(heads(row[:, b, :]), heads(ACC[:, at(t), 0:D].squeeze(1)), rden[:, at(t), :].squeeze(1).unsqueeze(2).to_broadcast([P, HEADS, HD]), ALU.mult)
                            dve.tensor_tensor(heads(alt[:, :]), heads(VS[:, at(t), :].squeeze(1)), none[:, at(t), :].squeeze(1).unsqueeze(2).to_broadcast([P, HEADS, HD]), ALU.mult)
                            dve.drain()
                            dve.tensor_tensor(row[:, b, :], row[:, b, :], alt[:, :], ALU.add).then_inc(s_row, 1)
                        on, t, r = tile(i, u, 2, NU, NT)
                        if on:
                            dve.wait_ge(s_mm, t + 1)
                            dve.tensor_tensor(ACC[:, at(t), 0:D], XN[:, at(t), :], po[r % 2][:, :], ALU.add).then_inc(s_g, 1)
                            dve.drain()
                            dve.tensor_tensor(ACC[:, at(t), 0:D], ACC[:, at(t), 0:D], vec[:, 0, :], ALU.add)
                            dve.drain()
                            dve.bn_stats(st[:, at(t), :], ACC[:, at(t), 0:D])
                    steps(dve, NT, NU, 2, step)
                    dve.drain()
                    self.finish_stats(dve, st, mean[:, :], rstd[:, :], NT).then_inc(s_st, 1)
                    dve.wait_ge(s_sd, 1)
                    dve.reciprocal(rstd[:, :], rstd[:, :])
                    dve.wait_ge(s_xr, NT)
                    dve.drain()
                    with dve.Fori(0, NT) as t:
                        dve.tensor_scalar(ACC[:, at(t), 0:D], ACC[:, at(t), 0:D], mean[:, at(t)], rstd[:, at(t)], ALU.subtract, ALU.mult)
                        dve.drain()
                        dve.tensor_tensor(ACC[:, at(t), 0:D], ACC[:, at(t), 0:D], vec[:, 1, :], ALU.mult)
                        dve.drain()
                        dve.tensor_tensor(RES[:, at(t), :], RES[:, at(t), :], ACC[:, at(t), 0:D], ALU.add)

                @block.scalar
                def _(act):
                    def step(i, u):
                        on, t, r = tile(i, u, 0, NU, NT)
                        if on:
                            b = r % 2
                            act.wait_ge(s_tr, t + 1)
                            need(act, s_mm, t - 1)
                            act.activation(rowT[:, b, :, :], pt[b][:, :, :], ACT.Copy).then_inc(s_tt, 1)
                    steps(act, NT, NU, 0, step)
                    act.wait_ge(s_st, 1)
                    act.activation(rstd[:, :], rstd[:, :], ACT.Sqrt, bias=self.eps[:, :]).then_inc(s_sd, 1)

                @block.tensor
                def _(pe):
                    pe.wait_ge(s_in, 64)

                    def step(i, u):
                        on, t, r = tile(i, u, 0, NU, NT)
                        if on:
                            b = r % 2
                            pe.wait_ge(s_row, t + 1)
                            need(pe, s_tt, t - 1)
                            pe.transpose(pt[b][:, 0, :], row[:, b, 0:P], self.identf[:, :])
                            pe.transpose(pt[b][:, 1, :], row[:, b, P:], self.identf[:, :]).then_inc(s_tr, 1)
                        on, t, r = tile(i, u, 1, NU, NT)
                        if on:
                            b = r % 2
                            pe.wait_ge(s_tt, t + 1)
                            need(pe, s_g, t - 1)
                            for ch in range(2):
                                last = pe.matmul(po[b][:, :], rowT[:, b, ch, :], W[:, ch, :], start=ch == 0, stop=ch == 1)
                            last.then_inc(s_mm, 1)
                    steps(pe, NT, NU, 1, step)

    def mix0(self):
        nc, a, H = self.nc, self.a, self.RES
        MH, MD, FF, FC, GT = 8, 32, 1024, 8, 5
        SCALE = MD ** -0.25
        NG, GH = NT // GT, GT * P // 2
        n = self.sem
        names = ("w", "wf", "st", "sd", "row", "tr", "tt", "mm", "qk", "v", "cm", "cmt", "dg", "cmb", "kd", "ek", "cx", "cn", "ct", "ctt", "m", "ms",
                 "qd", "qe", "qr", "qtr", "qt", "y", "h", "st2", "sd2", "frow", "ftr", "ftt", "u", "gel", "fy", "fh")
        S = {x: n("m_" + x) for x in names}
        s = lambda x: S[x]
        with ExitStack() as c:
            sb = lambda name, shape, dt=F32: self.sb(c, "m_" + name, shape, dt)
            pb = lambda name, shape, dt=F32: self.pb(c, "m_" + name, shape, dt)
            Wqkv, Wo = sb("Wqkv", [P, 2, 3 * D]), sb("Wo", [P, 2, D])
            g1, b1, g2, b2, bf = (sb(x, [P, k]) for x, k in (("g1", 2), ("b1", 2), ("g2", 2), ("b2", 2), ("bf", FC)))
            brow = sb("brow", [P, 2, D])
            st, mean, rstd = sb("stats", [P, NT, 6]), sb("mean", [P, NT]), sb("rstd", [P, NT])
            row, rowT = sb("rows", [P, 2, D]), sb("rowT", [P, 2, 2, P])
            QK = sb("QK", [P, NT, 2 * D])
            VX = sb("VX", [P, NT, 2, P + 1])
            CM, cmT, dg, CMB = sb("CM", [P, D]), sb("cmT", [P, 2]), sb("dg", [P, 2, P]), sb("CMB", [P, D])
            KD, EK = sb("KD", [P, 2, D]), sb("EK", [P, 2, D])
            bd = sb("bd", [P, P])
            rd, CN, CT, M = sb("rd", [P, 2]), sb("CN", [P, 2, P]), sb("CT", [P, 2, P]), sb("M", [P, 2, D])
            qm, qs = sb("qm", [P, 2, MH]), sb("qs", [P, 2, MH])
            QD, QE = sb("QD", [P, 2, D]), sb("QE", [P, 2, D])
            flat = VX[:, :, :, :].rearrange("p t c n -> p (t c n)")
            W1 = flat[:, 0:2 * FF].rearrange("p (c f) -> p c f", c=2)
            W2 = flat[:, 2 * FF:2 * FF + FC * D].rearrange("p (c f) -> p c f", c=FC)
            G = QK[:, 0:10, :].rearrange("p t c -> p (t c)").rearrange("p (f n) -> p f n", f=FC)
            hT = QK[:, 10:15, :].rearrange("p t c -> p (t c)")[:, 0:2 * GT * P].rearrange("p (c n) -> p c n", c=2)
            banks = [pb(f"bank{b}", [P, 512]) for b in range(8)]
            pt = [banks[b][:, 0:D].rearrange("p (c n) -> p c n", c=2) for b in range(2)]
            pqk, pv = [banks[2], banks[3]], [banks[4][:, 0:D], banks[5][:, 0:D]]
            pcx = [banks[6][:, 0:P + 1], banks[7][:, 0:P + 1]]
            py = [banks[4][:, 0:D], banks[5][:, 0:D]]
            mh = lambda x: x.rearrange("p (h d) -> p h d", h=MH)
            with nc.Block() as block:

                @block.gpsimd
                def _(pool):
                    v = bd[:, :].rearrange("p (h d) -> p h d", d=MD)
                    pool.affine_select(out=v, in_=self.ones[:, :].rearrange("p (h d) -> p h d", d=MD), compare_op=ALU.is_ge, fill=0.0,
                                       base=0, pattern=[[-MD, P // MD], [0, MD]], channel_multiplier=1)
                    pool.drain()
                    pool.affine_select(out=v, in_=v, compare_op=ALU.is_ge, fill=0.0,
                                       base=MD - 1, pattern=[[MD, P // MD], [0, MD]], channel_multiplier=-1)

                @block.vector
                def _(dve):
                    with dve.Fori(0, NT) as t:
                        dve.bn_stats(st[:, at(t), :], H[:, at(t), :])

            with nc.Fori(0, LAYERS) as layer:
                with nc.Block() as block:

                    @block.gpsimd
                    def _(pool):
                        for edges, bodies in zip(self.placing, BESIDE):
                            with pool.Fori(0, bodies) as j:
                                self.place_edges(pool, edges, layer * bodies + (j + PEEL))

                    @block.sync
                    def _(sp):
                        w = lambda x: a["L0_mix_" + x]
                        for j, x in enumerate(("Wq", "Wk", "Wv")):
                            sp.dma_start(Wqkv[:, :, j * D:(j + 1) * D], w(x)[at(layer), :, :].squeeze(0).rearrange("(c p) f -> p c f", p=P)).then_inc(s("w"), 16)
                        for dst, x in ((g1, "ln1_g"), (b1, "ln1_b"), (g2, "ln2_g"), (b2, "ln2_b"), (bf, "b1")):
                            sp.dma_start(dst[:, :], w(x)[at(layer), :].squeeze(0).rearrange("(c p) -> p c", p=P)).then_inc(s("w"), 16)
                        sp.dma_start(brow[:, 0, :], w("bo")[at(layer), :].squeeze(0).partition_broadcast(P)).then_inc(s("w"), 16)
                        sp.dma_start(brow[:, 1, :], w("b2")[at(layer), :].squeeze(0).partition_broadcast(P)).then_inc(s("w"), 16)
                        sp.dma_start(Wo[:, :, :], w("Wo")[at(layer), :, :].squeeze(0).rearrange("(c p) f -> p c f", p=P)).then_inc(s("w"), 16)
                        sp.wait_ge(s("cx"), NT)
                        sp.dma_start(W1, w("W1")[at(layer), :, :].squeeze(0).rearrange("(c p) f -> p c f", p=P)).then_inc(s("wf"), 16)
                        sp.dma_start(W2, w("W2")[at(layer), :, :].squeeze(0).rearrange("(c p) f -> p c f", p=P)).then_inc(s("wf"), 16)
                    WALL = 16 * 11

                    @block.vector
                    def _(dve):
                        self.finish_stats(dve, st, mean[:, :], rstd[:, :], NT).then_inc(s("st"), 1)
                        dve.memset(CM[:, :], -BIG)
                        dve.memset(VX[:, :, :, P:], 1.0)
                        dve.wait_ge(s("sd"), 1)
                        dve.reciprocal(rstd[:, :], rstd[:, :])
                        dve.drain()

                        dve.wait_ge(s("w"), WALL)
                        def step(i, u):
                            on, t, r = tile(i, u, 0, NU, NT)
                            if on:
                                need(dve, s("tr"), t - 1)
                                dve.tensor_scalar(row[:, r % 2, :], H[:, at(t), :], mean[:, at(t)], rstd[:, at(t)],
                                                  ALU.subtract, ALU.mult).then_inc(s("row"), 1)
                            on, t, r = tile(i, u, 2, NU, NT)
                            if on:
                                dve.wait_ge(s("mm"), t + 1)
                                dve.tensor_copy(VX[:, at(t), :, 0:P], pv[r % 2].rearrange("p (c n) -> p c n", c=2)).then_inc(s("v"), 1)
                                rows = slice(0, TAIL if isinstance(t, int) and t == NT - 1 else P)
                                need(dve, s("cm"), t)
                                dve.wait_ge(s("qk"), t + 1)
                                dve.tensor_tensor(CM[rows, :], CM[rows, :], QK[rows, at(t), D:], ALU.max).then_inc(s("cm"), 1)
                        steps(dve, NT, NU, 2, step)
                        dve.wait_ge(s("cmt"), 1)
                        dve.tensor_reduce(cmT[:, :], pt[0], AX.X, ALU.max)
                        dve.drain()
                        for ch in range(2):
                            last = dve.tensor_scalar(dg[:, ch, :], self.identf[:, :], cmT[:, ch:ch + 1], None, ALU.mult)
                        last.then_inc(s("dg"), 1)
                        dve.wait_ge(s("cmb"), 1)
                        dve.tensor_copy(CMB[:, :], banks[2][:, 0:D])
                        dve.drain()

                        def step(i, u):
                            on, t, r = tile(i, u, 0, NU, NT)
                            if on:
                                need(dve, s("ek"), t - 1)
                                dve.tensor_tensor(KD[:, r % 2, :], QK[:, at(t), D:], CMB[:, :], ALU.subtract).then_inc(s("kd"), 1)
                                dve.tensor_tensor(H[:, at(t), :], H[:, at(t), :], brow[:, 0, :], ALU.add)
                        steps(dve, NT, NU, 0, step)
                        dve.wait_ge(s("cx"), NT)
                        for ch in range(2):
                            dve.reciprocal(rd[:, ch:ch + 1], pcx[ch][:, P:])
                        dve.drain()
                        for ch in range(2):
                            last = dve.scalar_tensor_tensor(out=CN[:, ch, :], in0=pcx[ch][:, 0:P], scalar=rd[:, ch:ch + 1], in1=bd[:, :], op0=ALU.mult, op1=ALU.mult)
                        last.then_inc(s("cn"), 1)
                        dve.wait_ge(s("ctt"), 1)
                        dve.tensor_copy(CT[:, :, :], pt[0]).then_inc(s("ct"), 1)
                        dve.wait_ge(s("m"), 1)
                        dve.tensor_copy(M[:, :, :], banks[2][:, :].rearrange("p (c n) -> p c n", c=2)).then_inc(s("ms"), 1)

                        def step(i, u):
                            on, t, r = tile(i, u, 1, NU, NT)
                            if on:
                                b = r % 2
                                dve.wait_ge(s("qe"), t + 1)
                                dve.tensor_reduce(qs[:, b, :], mh(QE[:, b, :]), AX.X, ALU.add)
                            on0, t0, r0 = tile(i, u, 0, NU, NT)
                            if on0:
                                b0 = r0 % 2
                                need(dve, s("qe"), t0 - 1)
                                dve.tensor_reduce(qm[:, b0, :], mh(QK[:, at(t0), 0:D].squeeze(1)), AX.X, ALU.max)
                            dve.drain()
                            if on:
                                dve.reciprocal(qs[:, b, :], qs[:, b, :])
                            if on0:
                                dve.tensor_tensor(mh(QD[:, b0, :]), mh(QK[:, at(t0), 0:D].squeeze(1)), qm[:, b0, :].unsqueeze(2).to_broadcast([P, MH, MD]), ALU.subtract).then_inc(s("qd"), 1)
                            dve.drain()
                            if on:
                                dve.tensor_tensor(mh(QE[:, b, :]), mh(QE[:, b, :]), qs[:, b, :].unsqueeze(2).to_broadcast([P, MH, MD]), ALU.mult).then_inc(s("qr"), 1)
                            on, t, r = tile(i, u, 3, NU, NT)
                            if on:
                                dve.wait_ge(s("y"), t + 1)
                                dve.tensor_tensor(H[:, at(t), :], H[:, at(t), :], py[r % 2], ALU.add).then_inc(s("h"), 1)
                                dve.drain()
                                dve.bn_stats(st[:, at(t), :], H[:, at(t), :])
                        steps(dve, NT, NU, 3, step)
                        dve.drain()
                        self.finish_stats(dve, st, mean[:, :], rstd[:, :], NT).then_inc(s("st2"), 1)
                        dve.wait_ge(s("sd2"), 1)
                        dve.reciprocal(rstd[:, :], rstd[:, :])
                        dve.drain()

                        def step(i, u):
                            for k in (0, 1):
                                on, g, _ = tile(i, u, k, 1, NG)
                                if on:
                                    for j in range(GT):
                                        t = g * GT + j
                                        if k == 0:
                                            need(dve, s("ftr"), t - 1 if j else t)
                                            dve.tensor_scalar(row[:, j % 2, :], H[:, at(t), :], mean[:, at(t)], rstd[:, at(t)],
                                                              ALU.subtract, ALU.mult).then_inc(s("frow"), 1)
                                            dve.drain()
                                            dve.tensor_tensor(H[:, at(t), :], H[:, at(t), :], brow[:, 1, :], ALU.add)
                                        else:
                                            dve.wait_ge(s("fy"), t + 1)
                                            dve.tensor_tensor(H[:, at(t), :], H[:, at(t), :], py[j % 2], ALU.add).then_inc(s("fh"), 1)
                                            dve.drain()
                                            dve.bn_stats(st[:, at(t), :], H[:, at(t), :])
                        steps(dve, NG, 1, 1, step)

                    @block.scalar
                    def _(act):
                        act.wait_ge(s("st"), 1)
                        act.activation(rstd[:, :], rstd[:, :], ACT.Sqrt, bias=self.eps[:, :]).then_inc(s("sd"), 1)
                        act.wait_ge(s("w"), WALL)

                        def step(i, u):
                            on, t, r = tile(i, u, 0, NU, NT)
                            if on:
                                b = r % 2
                                act.wait_ge(s("tr"), t + 1)
                                need(act, s("mm"), t - 1)
                                for ch in range(2):
                                    last = act.activation(rowT[:, b, ch, :], pt[b][:, ch, :], ACT.Identity, scale=g1[:, ch:ch + 1], bias=b1[:, ch:ch + 1])
                                last.then_inc(s("tt"), 1)
                            on, t, r = tile(i, u, 1, NU, NT)
                            if on:
                                act.wait_ge(s("mm"), t + 1)
                                act.activation(QK[:, at(t), :], pqk[r % 2][:, :], ACT.Copy).then_inc(s("qk"), 1)
                        steps(act, NT, NU, 1, step)

                        def step(i, u):
                            on, t, r = tile(i, u, 0, NU, NT)
                            if on:
                                act.wait_ge(s("kd"), t + 1)
                                need(act, s("cx"), t - 1)
                                act.activation(EK[:, r % 2, :], KD[:, r % 2, :], ACT.Exp, scale=SCALE).then_inc(s("ek"), 1)
                        steps(act, NT, NU, 0, step)

                        def step(i, u):
                            on, t, r = tile(i, u, 0, NU, NT)
                            if on:
                                act.wait_ge(s("qd"), t + 1)
                                need(act, s("qtr"), t - 1)
                                act.activation(QE[:, r % 2, :], QD[:, r % 2, :], ACT.Exp, scale=SCALE).then_inc(s("qe"), 1)
                            on, t, r = tile(i, u, 2, NU, NT)
                            if on:
                                act.wait_ge(s("qtr"), t + 1)
                                need(act, s("y"), t - 1)
                                act.activation(rowT[:, r % 2, :, :], pt[r % 2], ACT.Copy).then_inc(s("qt"), 1)
                        steps(act, NT, NU, 2, step)
                        act.wait_ge(s("st2"), 1)
                        act.activation(rstd[:, :], rstd[:, :], ACT.Sqrt, bias=self.eps[:, :]).then_inc(s("sd2"), 1)

                        def step(i, u):
                            on, g, _ = tile(i, u, 0, 1, NG)
                            if on:
                                need(act, s("u"), g * (2 * FC))
                                for j in range(GT):
                                    t = g * GT + j
                                    act.wait_ge(s("ftr"), t + 1)
                                    for ch in range(2):
                                        last = act.activation(hT[:, ch, j * P:(j + 1) * P], pt[j % 2][:, ch, :], ACT.Identity, scale=g2[:, ch:ch + 1], bias=b2[:, ch:ch + 1])
                                    last.then_inc(s("ftt"), 1)
                                need(act, s("fy"), g * GT)
                                for f in range(FC):
                                    for h in range(2):
                                        act.wait_ge(s("u"), g * (2 * FC) + (2 * f + h + 1))
                                        act.activation(G[:, f, h * GH:(h + 1) * GH], banks[(2, 3, 6, 7)[2 * (f % 2) + h]][:, 0:GH], ACT.Gelu, bias=bf[:, f:f + 1]).then_inc(s("gel"), 1)
                        steps(act, NG, 1, 0, step)

                    @block.tensor
                    def _(pe):
                        pe.wait_ge(s("w"), WALL)

                        def step(i, u):
                            on, t, r = tile(i, u, 0, NU, NT)
                            if on:
                                b = r % 2
                                pe.wait_ge(s("row"), t + 1)
                                need(pe, s("tt"), t - 1)
                                pe.transpose(pt[b][:, 0, :], row[:, b, 0:P], self.identf[:, :])
                                pe.transpose(pt[b][:, 1, :], row[:, b, P:], self.identf[:, :]).then_inc(s("tr"), 1)
                            on, t, r = tile(i, u, 1, NU, NT)
                            if on:
                                b = r % 2
                                pe.wait_ge(s("tt"), t + 1)
                                need(pe, s("qk"), t - 1)
                                need(pe, s("v"), t - 1)
                                for ch in range(2):
                                    pe.matmul(pqk[b][:, :], rowT[:, b, ch, :], Wqkv[:, ch, 0:2 * D], start=ch == 0, stop=ch == 1)
                                for ch in range(2):
                                    last = pe.matmul(pv[b], rowT[:, b, ch, :], Wqkv[:, ch, 2 * D:], start=ch == 0, stop=ch == 1)
                                last.then_inc(s("mm"), 1)
                        steps(pe, NT, NU, 1, step)
                        pe.wait_ge(s("cm"), NT)
                        pe.wait_ge(s("qk"), NT)
                        pe.transpose(pt[0][:, 0, :], CM[:, 0:P], self.identf[:, :])
                        pe.transpose(pt[0][:, 1, :], CM[:, P:], self.identf[:, :]).then_inc(s("cmt"), 1)
                        pe.wait_ge(s("dg"), 1)
                        pe.matmul(banks[2][:, 0:D], self.ones[:, :], dg[:, :, :], start=True, stop=True).then_inc(s("cmb"), 1)

                        def step(i, u):
                            on, t, r = tile(i, u, 0, NU, NT)
                            if on:
                                pe.wait_ge(s("ek"), t + 1)
                                first, final = isinstance(t, int) and t == 0, isinstance(t, int) and t == NT - 1
                                rows = slice(0, TAIL if final else P)
                                for ch in range(2):
                                    last = pe.matmul(pcx[ch], EK[rows, r % 2, ch * P:(ch + 1) * P], VX[rows, at(t), ch, :], start=first, stop=final)
                                last.then_inc(s("cx"), 1)
                        steps(pe, NT, NU, 0, step)
                        pe.wait_ge(s("cn"), 1)
                        for ch in range(2):
                            last = pe.transpose(pt[0][:, ch, :], CN[:, ch, :], self.identf[:, :])
                        last.then_inc(s("ctt"), 1)
                        pe.wait_ge(s("ct"), 1)
                        for ch in range(2):
                            last = pe.matmul(banks[2][:, ch * D:(ch + 1) * D], CT[:, ch, :], Wo[:, ch, :], start=True, stop=True)
                        last.then_inc(s("m"), 1)
                        pe.wait_ge(s("ms"), 1)

                        def step(i, u):
                            on, t, r = tile(i, u, 1, NU, NT)
                            if on:
                                b = r % 2
                                pe.wait_ge(s("qr"), t + 1)
                                need(pe, s("qt"), t - 1)
                                pe.transpose(pt[b][:, 0, :], QE[:, b, 0:P], self.identf[:, :])
                                pe.transpose(pt[b][:, 1, :], QE[:, b, P:], self.identf[:, :]).then_inc(s("qtr"), 1)
                            on, t, r = tile(i, u, 2, NU, NT)
                            if on:
                                b = r % 2
                                pe.wait_ge(s("qt"), t + 1)
                                need(pe, s("h"), t - 1)
                                for ch in range(2):
                                    last = pe.matmul(py[b], rowT[:, b, ch, :], M[:, ch, :], start=ch == 0, stop=ch == 1)
                                last.then_inc(s("y"), 1)
                        steps(pe, NT, NU, 2, step)
                        pe.wait_ge(s("h"), NT)
                        pe.wait_ge(s("qt"), NT)
                        pe.wait_ge(s("wf"), 32)

                        def step(i, u):
                            on, g, _ = tile(i, u, 0, 1, NG)
                            if on:
                                for j in range(GT):
                                    t = g * GT + j
                                    pe.wait_ge(s("frow"), t + 1)
                                    need(pe, s("ftt"), t - 1 if j else t)
                                    pe.transpose(pt[j % 2][:, 0, :], row[:, j % 2, 0:P], self.identf[:, :])
                                    pe.transpose(pt[j % 2][:, 1, :], row[:, j % 2, P:], self.identf[:, :]).then_inc(s("ftr"), 1)
                            on, g1_, _ = tile(i, u, 1, 1, NG)
                            if on:
                                pe.wait_ge(s("gel"), (g1_ + 1) * (2 * FC))
                                for j in range(GT):
                                    t = g1_ * GT + j
                                    need(pe, s("fh"), t - 1 if j else t)
                                    for f in range(FC):
                                        last = pe.matmul(py[j % 2], G[:, f, j * P:(j + 1) * P], W2[:, f, :], start=f == 0, stop=f == FC - 1)
                                    last.then_inc(s("fy"), 1)
                            on, g, _ = tile(i, u, 0, 1, NG)
                            if on:
                                pe.wait_ge(s("ftt"), (g + 1) * GT)
                                for f in range(FC):
                                    for h in range(2):
                                        need(pe, s("gel"), g * (2 * FC) + (2 * f + h - 3))
                                        for ch in range(2):
                                            last = pe.matmul(banks[(2, 3, 6, 7)[2 * (f % 2) + h]][:, 0:GH], W1[:, ch, f * P:(f + 1) * P], hT[:, ch, h * GH:(h + 1) * GH],
                                                             start=ch == 0, stop=ch == 1)
                                        last.then_inc(s("u"), 1)
                        steps(pe, NG, 1, 1, step)

                with nc.Block() as block:

                    @block.gpsimd
                    def _(pool):
                        for x in names:
                            pool.sem_clear(S[x])

            with nc.Block() as block:

                @block.gpsimd
                def _(pool):
                    for s in self.placing[1][4]:
                        pool.wait_ge(s, 16 * (EC // U))

    def norm_rows(self, which):
        nc, XN, RES = self.nc, self.XN, self.RES
        s_st, s_sd = self.sem(which + "_st"), self.sem(which + "_sd")
        with ExitStack() as c:
            st = self.sb(c, which + "_stats", [P, NT, 6])
            mean, rstd = self.sb(c, which + "_mean", [P, NT]), self.sb(c, which + "_rstd", [P, NT])
            with nc.Block() as block:

                @block.vector
                def _(dve):
                    with dve.Fori(0, NT) as t:
                        dve.bn_stats(st[:, at(t), :], RES[:, at(t), :])
                    dve.drain()
                    self.finish_stats(dve, st, mean[:, :], rstd[:, :], NT).then_inc(s_st, 1)
                    dve.wait_ge(s_sd, 1)
                    dve.reciprocal(rstd[:, :], rstd[:, :])
                    dve.drain()
                    with dve.Fori(0, NT) as t:
                        dve.tensor_scalar(XN[:, at(t), :], RES[:, at(t), :], mean[:, at(t)], rstd[:, at(t)], ALU.subtract, ALU.mult)

                @block.scalar
                def _(act):
                    act.wait_ge(s_st, 1)
                    act.activation(rstd[:, :], rstd[:, :], ACT.Sqrt, bias=self.eps[:, :]).then_inc(s_sd, 1)

    def route(self, ctx, xs_tab):
        nc, a, XN = self.nc, self.a, self.XN
        n = self.sem
        self.SLOT = SLOT = self.sb(ctx, "SLOT", [P, NT, 2], I32)
        self.GATE = GATE = self.sb(ctx, "GATE", [P, NT, 2])
        self.XTILE = XTILE = self.sb(ctx, "XTILE", [1, XT], I32)
        s_in, s_row, s_tr, s_tt, s_mm, s_lg, s_d, s_e, s_oh, s_pf, s_z, s_slot, s_cp, s_turn = (n(f"r_{x}") for x in (
            "in", "row", "tr", "tt", "mm", "lg", "d", "e", "oh", "pf", "z", "slot", "cp", "turn"))
        s_sc = self.soft_sems("r_sc", NU)
        with ExitStack() as c:
            sb = lambda name, shape, dt=F32: self.sb(c, "r_" + name, shape, dt)
            pb = lambda name, shape, dt=F32: self.pb(c, "r_" + name, shape, dt)
            gw, gb = sb("gw", [P, 2, NX]), sb("gb", [P, NX])
            row, rowT = sb("rows", [P, 2, D]), sb("rowT", [P, 2, 2, P])
            LG, TMP, FIRST = sb("LG", [P, NT, NX]), sb("TMP", [P, NT, NX]), sb("FIRST", [P, NT, NX])
            OH1, OH2, OH = sb("OH1", [P, NT, NX]), sb("OH2", [P, NT, NX]), sb("OH", [P, NT, NX])
            m1, m2, ix, sf = (sb(x, [P, NT]) for x in ("m1", "m2", "ix", "sf"))
            TOT, CUM = sb("TOT", [P, NX, NT]), sb("CUM", [P, NX, NT])
            te, ti, tb = sb("te", [P, NX]), sb("ti", [P, NX], I32), sb("tb", [P, NX])
            xt = sb("xt", [1, XT])
            zero = sb("zero", [P, 8, D])
            srow, sidx = sb("srow", [P, NU, D]), sb("sidx", [P, NU, 2], I32)
            pt = [pb(f"pt{b}", [P, 2, P]) for b in range(2)]
            pl = [pb(f"pl{b}", [P, NX]) for b in range(2)]
            ppf, ptot = pb("ppf", [P, NT, NX]), pb("ptot", [P, NT, NX])
            wide = lambda x: x.unsqueeze(2).to_broadcast([P, NT, NX])
            iota_e = self.iota_t[:, 0:NX].unsqueeze(1).to_broadcast([P, NT, NX])
            with nc.Block() as block:

                @block.sync
                def _(sp):
                    sp.dma_start(gw[:, :, :], a["L0_ffn_gate_w"].rearrange("(c p) f -> p c f", p=P)).then_inc(s_in, 16)
                    sp.dma_start(gb[:, :], a["L0_ffn_gate_b"].partition_broadcast(P)).then_inc(s_in, 16)
                    sp.wait_ge(s_z, 1)
                    for j in range(XT // 8):
                        sp.dma_start(xs_tab.rearrange("(p t) d -> p t d", p=P)[:, j * 8:(j + 1) * 8, :], zero[:, :, :]).then_inc(s_z, 16)

                @block.vector
                def _(dve):
                    dve.memset(zero[:, :, :], 0.0).then_inc(s_z, 1)
                    dve.memset(xt[:, :], 0.0)
                    dve.wait_ge(s_in, 32)

                    def step(i, u):
                        on, t, r = tile(i, u, 0, NU, NT)
                        if on:
                            need(dve, s_tr, t - 1)
                            dve.tensor_copy(row[:, r % 2, :], XN[:, at(t), :]).then_inc(s_row, 1)
                        on, t, r = tile(i, u, 2, NU, NT)
                        if on:
                            dve.wait_ge(s_mm, t + 1)
                            dve.tensor_tensor(LG[:, at(t), :], pl[r % 2][:, :], gb[:, :], ALU.add).then_inc(s_lg, 1)
                    steps(dve, NT, NU, 2, step)
                    dve.drain()
                    for m, oh in ((m1, OH1), (m2, OH2)):
                        dve.tensor_reduce(m[:, :], LG[:, :, :], AX.X, ALU.max)
                        dve.drain()
                        dve.tensor_tensor(TMP[:, :, :], LG[:, :, :], wide(m[:, :]), ALU.is_lt)
                        dve.drain()
                        dve.scalar_tensor_tensor(out=FIRST[:, :, :], in0=TMP[:, :, :], scalar=float(NX), in1=iota_e, op0=ALU.mult, op1=ALU.add)
                        dve.drain()
                        dve.tensor_reduce(ix[:, :], FIRST[:, :, :], AX.X, ALU.min)
                        dve.drain()
                        dve.tensor_tensor(oh[:, :, :], iota_e, wide(ix[:, :]), ALU.is_equal)
                        dve.drain()
                        dve.scalar_tensor_tensor(out=LG[:, :, :], in0=oh[:, :, :], scalar=-BIG, in1=LG[:, :, :], op0=ALU.mult, op1=ALU.add)
                        dve.drain()
                        dve.tensor_scalar(oh[:, NT - 1, :], oh[:, NT - 1, :], self.lower[:, TAIL:TAIL + 1], None, ALU.mult)
                        dve.drain()
                    dve.tensor_tensor(m2[:, :], m2[:, :], m1[:, :], ALU.subtract).then_inc(s_d, 1)
                    dve.tensor_tensor(OH[:, :, :], OH1[:, :, :], OH2[:, :, :], ALU.add).then_inc(s_oh, 1)
                    dve.wait_ge(s_e, 1)
                    dve.tensor_scalar(m1[:, :], m2[:, :], 1.0, None, ALU.add)
                    dve.drain()
                    dve.reciprocal(m1[:, :], m1[:, :])
                    dve.drain()
                    dve.tensor_copy(GATE[:, :, 0], m1[:, :])
                    dve.tensor_tensor(GATE[:, :, 1], m1[:, :], m2[:, :], ALU.mult)
                    dve.wait_ge(s_pf, 1)
                    dve.tensor_copy(TOT[:, :, :], ptot[:, :, :].rearrange("p t e -> p e t"))
                    dve.drain()
                    for e in range(NX):
                        dve.tensor_tensor_scan(CUM[:, e, :], TOT[:, e, :], self.zeros[:, 0:NT], 0.0, ALU.add, ALU.add)
                    dve.drain()
                    dve.tensor_scalar(te[:, :], CUM[:, :, NT - 1], float(P - 1), None, ALU.add)
                    dve.drain()
                    dve.tensor_copy(ti[:, :], te[:, :])
                    dve.drain()
                    dve.tensor_scalar(ti[:, :], ti[:, :], 7, None, ALU.arith_shift_right)
                    dve.drain()
                    dve.tensor_copy(te[:, :], ti[:, :])
                    dve.drain()
                    dve.tensor_tensor_scan(tb[:, :], te[:, :], self.zeros[:, 0:NX], 0.0, ALU.add, ALU.add)
                    dve.drain()
                    dve.tensor_tensor(tb[:, :], tb[:, :], te[:, :], ALU.subtract)
                    dve.tensor_tensor(CUM[:, :, :], CUM[:, :, :], TOT[:, :, :], ALU.subtract)
                    dve.drain()
                    for e in range(1, NX):
                        dve.scalar_tensor_tensor(out=xt[:, :], in0=self.iota_t[0:1, 0:XT], scalar=tb[0:1, e:e + 1], in1=xt[:, :], op0=ALU.is_ge, op1=ALU.add)
                        dve.drain()
                    dve.tensor_copy(XTILE[:, :], xt[:, :])
                    dve.tensor_scalar(tb[:, :], tb[:, :], float(P), None, ALU.mult)
                    dve.tensor_tensor(TMP[:, :, :], ppf[:, :, :], CUM[:, :, :].rearrange("p e t -> p t e"), ALU.add)
                    dve.drain()
                    dve.tensor_tensor(TMP[:, :, :], TMP[:, :, :], tb[:, :].unsqueeze(1).to_broadcast([P, NT, NX]), ALU.add)
                    dve.drain()
                    for j, oh in enumerate((OH1, OH2)):
                        dve.tensor_tensor(FIRST[:, :, :], TMP[:, :, :], oh[:, :, :], ALU.mult)
                        dve.drain()
                        dve.tensor_reduce(sf[:, :], FIRST[:, :, :], AX.X, ALU.add)
                        dve.drain()
                        dve.tensor_copy(SLOT[:, :, j], sf[:, :])
                    dve.drain()
                    dve.sem_inc(s_slot, 1)

                @block.scalar
                def _(act):
                    def step(i, u):
                        on, t, r = tile(i, u, 0, NU, NT)
                        if on:
                            act.wait_ge(s_tr, t + 1)
                            need(act, s_mm, t - 1)
                            act.activation(rowT[:, r % 2, :, :], pt[r % 2][:, :, :], ACT.Copy).then_inc(s_tt, 1)
                    steps(act, NT, NU, 0, step)
                    act.wait_ge(s_d, 1)
                    act.activation(m2[:, :], m2[:, :], ACT.Exp).then_inc(s_e, 1)

                @block.tensor
                def _(pe):
                    pe.wait_ge(s_in, 32)

                    def step(i, u):
                        on, t, r = tile(i, u, 0, NU, NT)
                        if on:
                            b = r % 2
                            pe.wait_ge(s_row, t + 1)
                            need(pe, s_tt, t - 1)
                            pe.transpose(pt[b][:, 0, :], row[:, b, 0:P], self.identf[:, :])
                            pe.transpose(pt[b][:, 1, :], row[:, b, P:], self.identf[:, :]).then_inc(s_tr, 1)
                        on, t, r = tile(i, u, 1, NU, NT)
                        if on:
                            b = r % 2
                            pe.wait_ge(s_tt, t + 1)
                            need(pe, s_lg, t - 1)
                            for ch in range(2):
                                last = pe.matmul(pl[b][:, :], rowT[:, b, ch, :], gw[:, ch, :], start=ch == 0, stop=ch == 1)
                            last.then_inc(s_mm, 1)
                    steps(pe, NT, NU, 1, step)
                    pe.wait_ge(s_oh, 1)
                    pe.matmul(ppf[:, :, :], self.lower[:, :], OH[:, :, :], start=True, stop=True)
                    pe.matmul(ptot[:, :, :], self.ones[:, :], OH[:, :, :], start=True, stop=True).then_inc(s_pf, 1)

                @block.gpsimd
                def _(pool):
                    pool.wait_ge(s_slot, 1)
                    pool.wait_ge(s_z, 1 + 16 * (XT // 8))

                    def step(i, u):
                        on, t, r = tile(i, u, 0, NU, NT)
                        if on:
                            rows = TAIL if isinstance(t, int) and t == NT - 1 else P
                            need(pool, s_sc[r], i * 32)
                            pool.tensor_copy(srow[:, r, :], XN[:, at(t), :]).then_inc(s_cp, 1)
                            pool.tensor_copy(sidx[:, r, :], SLOT[:, at(t), :].squeeze(1)).then_inc(s_cp, 1)
                            pool.wait_ge(s_cp, t * 2 + 2)
                            for j in range(2):
                                pool.sem_inc(s_turn, 1)
                                pool.indirect_dma_start(xs_tab, bass.IndirectOffsetOnAxis(sidx[0:rows, r, j:j + 1], 0), srow[0:rows, r, :], None).then_inc(s_sc[r], 16)
                    steps(pool, NT, NU, 0, step)
                    for r in range(NU):
                        pool.wait_ge(s_sc[r], 32 * ((NT + NU - 1 - r) // NU))

    def experts(self, xs_tab, ys_tab):
        nc, a, XTILE = self.nc, self.a, self.XTILE
        n = self.sem
        HC = HX // P
        s_x, s_w, s_w3 = [n(f"e_x{i}") for i in range(4)], [n(f"e_w{i}") for i in range(4)], [n(f"e_w3{i}") for i in range(4)]
        s_out = [n(f"e_out{i}") for i in range(2)]
        s_tr, s_tt, s_h, s_sl, s_hid, s_htr, s_ht, s_y, s_ys = (n(f"e_{x}") for x in ("tr", "tt", "h", "sl", "hid", "htr", "ht", "y", "ys"))
        XU = 4
        with ExitStack() as c:
            sb = lambda name, shape, dt=F32: self.sb(c, "e_" + name, shape, dt)
            pb = lambda name, shape, dt=F32: self.pb(c, "e_" + name, shape, dt)
            XS, xT = sb("XS", [P, XU, D]), sb("xT", [P, 2, 2, P])
            W1, W2, W3 = sb("W1", [P, XU, 2, HX]), sb("W2", [P, XU, 2, HX]), sb("W3", [P, XU, HC, D])
            sl, hid, hidT, ys = sb("sl", [P, 2, HX]), sb("hid", [P, 2, HX]), sb("hidT", [P, 2, HC, P]), sb("ys", [P, 2, D])
            pt = pb("pt", [P, 2, P])
            ph1, ph2 = [pb(f"ph1{b}", [P, HX]) for b in range(2)], [pb(f"ph2{b}", [P, HX]) for b in range(2)]
            pht = pb("pht", [P, HC, P])
            py = [pb(f"py{b}", [P, D]) for b in range(2)]
            with nc.Block() as block:

                @block.sync
                def _(sp):
                    regs = [sp.alloc_register(f"e_x{j}") for j in range(XU)]
                    ex = [None]

                    def step(i, u):
                        if u % XU == 0 and (not isinstance(i, int) or i < XT // XU):
                            sp.load(regs, XTILE[0:1, ds(i * XU, XU)])
                            ex[0] = [sp.snap(g, min_val=0, max_val=NX - 1) for g in regs]
                        on, t, r = tile(i, u, 0, XU, XT)
                        if on:
                            e = ex[0][r]
                            need(sp, s_tr, t - 3)
                            sp.dma_start(XS[:, r, :], xs_tab[ds(t * P, P), :]).then_inc(s_x[r], 16)
                            need(sp, s_h, t - 3)
                            sp.dma_start(W1[:, r, :, :], a["L0_ffn_w1"][at(e), :, :].squeeze(0).rearrange("(c p) f -> p c f", p=P)).then_inc(s_w[r], 16)
                            sp.dma_start(W2[:, r, :, :], a["L0_ffn_w2"][at(e), :, :].squeeze(0).rearrange("(c p) f -> p c f", p=P)).then_inc(s_w[r], 16)
                            need(sp, s_y, t - 3)
                            sp.dma_start(W3[:, r, :, :], a["L0_ffn_w3"][at(e), :, :].squeeze(0).rearrange("(c p) f -> p c f", p=P)).then_inc(s_w3[r], 16)
                    steps(sp, XT, XU, 0, step)

                @block.gpsimd
                def _(pool):
                    if self.placing:
                        self.last_edges(pool)

                @block.vector
                def _(dve):
                    def step(i, u):
                        on, t, r = tile(i, u, 0, XU, XT)
                        if on:
                            b = r % 2
                            dve.wait_ge(s_sl, t + 1)
                            need(dve, s_htr, t - 1)
                            dve.tensor_tensor(hid[:, b, :], sl[:, b, :], ph2[b][:, :], ALU.mult).then_inc(s_hid, 1)
                        on, t, r = tile(i, u, 3, XU, XT)
                        if on:
                            b = r % 2
                            dve.wait_ge(s_y, t + 1)
                            need(dve, s_out[b], 16 * uses(i, u, 3, XU, 2))
                            dve.tensor_copy(ys[:, b, :], py[b][:, :]).then_inc(s_ys, 1)
                    steps(dve, XT, XU, 3, step)

                @block.scalar
                def _(act):
                    def step(i, u):
                        on, t, r = tile(i, u, 0, XU, XT)
                        if on:
                            act.wait_ge(s_tr, t + 1)
                            need(act, s_h, t - 1)
                            act.activation(xT[:, r % 2, :, :], pt[:, :, :], ACT.Copy).then_inc(s_tt, 1)
                        on, t, r = tile(i, u, 1, XU, XT)
                        if on:
                            act.wait_ge(s_h, t + 1)
                            need(act, s_hid, t - 1)
                            act.activation(sl[:, r % 2, :], ph1[r % 2][:, :], ACT.Silu).then_inc(s_sl, 1)
                        on, t, r = tile(i, u, 2, XU, XT)
                        if on:
                            act.wait_ge(s_htr, t + 1)
                            need(act, s_y, t - 1)
                            act.activation(hidT[:, r % 2, :, :], pht[:, :, :], ACT.Copy).then_inc(s_ht, 1)
                        on, t, r = tile(i, u, 4, XU, XT)
                        if on:
                            act.wait_ge(s_ys, t + 1)
                            act.dma_start(ys_tab[ds(t * P, P), :], ys[:, r % 2, :]).then_inc(s_out[r % 2], 16)
                    steps(act, XT, XU, 4, step)
                    for b in range(2):
                        act.wait_ge(s_out[b], 16 * XT // 2)

                @block.tensor
                def _(pe):
                    def step(i, u):
                        on, t, r = tile(i, u, 0, XU, XT)
                        if on:
                            pe.wait_ge(s_x[r], i * 16 + 16)
                            need(pe, s_tt, t)
                            pe.transpose(pt[:, 0, :], XS[:, r, 0:P], self.identf[:, :])
                            pe.transpose(pt[:, 1, :], XS[:, r, P:], self.identf[:, :]).then_inc(s_tr, 1)
                        on, t, r = tile(i, u, 1, XU, XT)
                        if on:
                            b = r % 2
                            pe.wait_ge(s_tt, t + 1)
                            pe.wait_ge(s_w[r], i * 32 + 32 * (1 + (u - 1) // XU))
                            need(pe, s_hid, t - 1)
                            for W, ph in ((W1, ph1), (W2, ph2)):
                                for ch in range(2):
                                    last = pe.matmul(ph[b][:, :], xT[:, b, ch, :], W[:, r, ch, :], start=ch == 0, stop=ch == 1)
                            last.then_inc(s_h, 1)
                        on, t, r = tile(i, u, 2, XU, XT)
                        if on:
                            pe.wait_ge(s_hid, t + 1)
                            need(pe, s_ht, t)
                            for f in range(HC):
                                last = pe.transpose(pht[:, f, :], hid[:, r % 2, f * P:(f + 1) * P], self.identf[:, :])
                            last.then_inc(s_htr, 1)
                        on, t, r = tile(i, u, 3, XU, XT)
                        if on:
                            b = r % 2
                            pe.wait_ge(s_ht, t + 1)
                            pe.wait_ge(s_w3[r], i * 16 + 16 * (1 + (u - 3) // XU))
                            need(pe, s_ys, t - 1)
                            for f in range(HC):
                                last = pe.matmul(py[b][:, :], hidT[:, b, f, :], W3[:, r, f, :], start=f == 0, stop=f == HC - 1)
                            last.then_inc(s_y, 1)
                    steps(pe, XT, XU, 3, step)

    def combine(self, ys_tab):
        nc, RES, SLOT, GATE = self.nc, self.RES, self.SLOT, self.GATE
        n = self.sem
        s_used, s_cp, s_turn = n("c_used"), n("c_cp"), n("c_turn")
        s_got = self.soft_sems("c_got", 4)
        with ExitStack() as c:
            Y, idx = self.sb(c, "c_Y", [P, 4, 2, D]), self.sb(c, "c_idx", [P, 4, 2], I32)
            with nc.Block() as block:

                @block.gpsimd
                def _(pool):
                    def step(i, u):
                        on, t, r = tile(i, u, 0, NU, NT)
                        if on:
                            need(pool, s_used, t - 3)
                            need(pool, s_got[r], i * 32)
                            pool.tensor_copy(idx[:, r, :], SLOT[:, at(t), :].squeeze(1)).then_inc(s_cp, 1)
                            pool.wait_ge(s_cp, t + 1)
                            for j in range(2):
                                pool.sem_inc(s_turn, 1)
                                pool.indirect_dma_start(Y[:, r, j, :], None, ys_tab, bass.IndirectOffsetOnAxis(idx[:, r, j:j + 1], 0)).then_inc(s_got[r], 16)
                    steps(pool, NT, NU, 0, step)

                @block.vector
                def _(dve):
                    def step(i, u):
                        on, t, r = tile(i, u, 0, NU, NT)
                        if on:
                            dve.wait_ge(s_got[r], i * 32 + 32)
                            for j in range(2):
                                last = dve.scalar_tensor_tensor(out=RES[:, at(t), :], in0=Y[:, r, j, :], scalar=GATE[:, at(t), j], in1=RES[:, at(t), :], op0=ALU.mult, op1=ALU.add)
                                if j:
                                    last.then_inc(s_used, 1)
                                dve.drain()
                    steps(dve, NT, NU, 0, step)


    def batch_norm(self, HB, tabs):
        nc, a, XN = self.nc, self.a, self.XN
        n = self.sem
        s_in, s_sum, s_mean, s_sq, s_var, s_sd, s_row, s_tr, s_tt, s_mm, s_f = (n(f"b_{x}") for x in (
            "in", "sum", "mean", "sq", "var", "sd", "row", "tr", "tt", "mm", "f"))
        s_out = [n(f"b_out{i}") for i in range(2)]
        with ExitStack() as c:
            sb = lambda name, shape, dt=F32: self.sb(c, "b_" + name, shape, dt)
            pb = lambda name, shape, dt=F32: self.pb(c, "b_" + name, shape, dt)
            W, vec, bias = sb("W", [P, 2, 2 * D]), sb("vec", [P, 2, D]), sb("bias", [P, 2, D])
            mean, var, sq = sb("mean", [P, D]), sb("var", [P, D]), sb("sq", [P, 2, D])
            row, rowT, fo = sb("rows", [P, 2, D]), sb("rowT", [P, 2, 2, P]), sb("fo", [P, 2, 2, D])
            pt = [pb(f"pt{b}", [P, 2, P]) for b in range(2)]
            pf = [pb(f"pf{b}", [P, 2 * D]) for b in range(2)]
            psum, pvar = pb("psum", [P, D]), pb("pvar", [P, D])
            with nc.Block() as block:

                @block.sync
                def _(sp):
                    for j, x in enumerate(("in", "out")):
                        sp.dma_start(W[:, :, j * D:(j + 1) * D], a[f"L1_gnn_W_{x}"].rearrange("(c p) f -> p c f", p=P)).then_inc(s_in, 16)
                        sp.dma_start(bias[:, j, :], a[f"L1_gnn_b_{x}"].partition_broadcast(P)).then_inc(s_in, 16)
                    for j, x in enumerate(("gamma", "beta")):
                        sp.dma_start(vec[:, j, :], a[f"L1_gnn_{x}"].partition_broadcast(P)).then_inc(s_in, 16)

                    def step(i, u):
                        on, t, r = tile(i, u, 1, NU, NT)
                        if on:
                            sp.wait_ge(s_f, t + 1)
                            for j in range(2):
                                sp.dma_start(tabs[j][ds(t * P, P), :], fo[:, r % 2, j, :]).then_inc(s_out[r % 2], 16)
                    steps(sp, NT, NU, 1, step)
                    sp.wait_ge(s_out[0], 32 * (NT - NT // 2))
                    sp.wait_ge(s_out[1], 32 * (NT // 2))

                @block.vector
                def _(dve):
                    dve.wait_ge(s_in, 96)
                    dve.wait_ge(s_sum, 1)
                    dve.tensor_scalar(mean[:, :], psum[:, :], 1.0 / N, None, ALU.mult)
                    dve.drain()

                    def step(i, u):
                        on, t, r = tile(i, u, 0, NU, NT)
                        if on:
                            need(dve, s_sq, t - 1)
                            dve.tensor_tensor(HB[:, at(t), :], XN[:, at(t), :], mean[:, :], ALU.subtract)
                            dve.drain()
                            dve.tensor_tensor(sq[:, r % 2, :], HB[:, at(t), :], HB[:, at(t), :], ALU.mult).then_inc(s_mean, 1)
                    steps(dve, NT, NU, 0, step)
                    dve.wait_ge(s_sd, 1)
                    dve.reciprocal(var[:, :], var[:, :])
                    dve.drain()
                    dve.tensor_tensor(var[:, :], var[:, :], vec[:, 0, :], ALU.mult)
                    dve.drain()

                    def step(i, u):
                        on, t, r = tile(i, u, 0, NU, NT)
                        if on:
                            dve.tensor_tensor(HB[:, at(t), :], HB[:, at(t), :], var[:, :], ALU.mult)
                            dve.drain()
                            need(dve, s_tr, t - 1)
                            dve.tensor_tensor(row[:, r % 2, :], HB[:, at(t), :], vec[:, 1, :], ALU.add).then_inc(s_row, 1)
                            dve.drain()
                            dve.tensor_copy(HB[:, at(t), :], row[:, r % 2, :])
                        on, t, r = tile(i, u, 2, NU, NT)
                        if on:
                            b = r % 2
                            dve.wait_ge(s_mm, t + 1)
                            need(dve, s_out[b], 32 * uses(i, u, 2, NU, 2))
                            dve.tensor_tensor(fo[:, b, :, :], pf[b][:, :].rearrange("p (j d) -> p j d", j=2), bias[:, :, :], ALU.add).then_inc(s_f, 1)
                            dve.drain()
                    steps(dve, NT, NU, 2, step)

                @block.scalar
                def _(act):
                    act.wait_ge(s_var, 1)
                    act.activation(var[:, :], pvar[:, :], ACT.Sqrt, scale=1.0 / N, bias=self.eps[:, :]).then_inc(s_sd, 1)

                    def step(i, u):
                        on, t, r = tile(i, u, 0, NU, NT)
                        if on:
                            act.wait_ge(s_tr, t + 1)
                            need(act, s_mm, t - 1)
                            act.activation(rowT[:, r % 2, :, :], pt[r % 2][:, :, :], ACT.Copy).then_inc(s_tt, 1)
                    steps(act, NT, NU, 0, step)

                @block.tensor
                def _(pe):
                    for t in (0, NT - 1):
                        if t:
                            with pe.Fori(1, NT - 1) as i:
                                pe.matmul(psum[:, :], self.ones[:, :], XN[:, at(i), :], start=False, stop=False)
                        rows = slice(0, TAIL if t else P)
                        last = pe.matmul(psum[:, :], self.ones[rows, :], XN[rows, t, :], start=t == 0, stop=t == NT - 1)
                    last.then_inc(s_sum, 1)

                    def step(i, u):
                        on, t, r = tile(i, u, 0, NU, NT)
                        if on:
                            first, final = isinstance(t, int) and t == 0, isinstance(t, int) and t == NT - 1
                            rows = slice(0, TAIL if final else P)
                            pe.wait_ge(s_mean, t + 1)
                            last = pe.matmul(pvar[:, :], self.ones[rows, :], sq[rows, r % 2, :], start=first, stop=final)
                            last.then_inc(s_sq, 1)
                            if final:
                                pe.wait_ge(s_sq, NT)
                                pe.sem_inc(s_var, 1)
                    steps(pe, NT, NU, 0, step)
                    pe.wait_ge(s_in, 96)

                    def step(i, u):
                        on, t, r = tile(i, u, 0, NU, NT)
                        if on:
                            b = r % 2
                            pe.wait_ge(s_row, t + 1)
                            need(pe, s_tt, t - 1)
                            pe.transpose(pt[b][:, 0, :], row[:, b, 0:P], self.identf[:, :])
                            pe.transpose(pt[b][:, 1, :], row[:, b, P:], self.identf[:, :]).then_inc(s_tr, 1)
                        on, t, r = tile(i, u, 1, NU, NT)
                        if on:
                            b = r % 2
                            pe.wait_ge(s_tt, t + 1)
                            need(pe, s_f, t - 1)
                            for ch in range(2):
                                last = pe.matmul(pf[b][:, :], rowT[:, b, ch, :], W[:, ch, :], start=ch == 0, stop=ch == 1)
                            last.then_inc(s_mm, 1)
                    steps(pe, NT, NU, 1, step)

    def edge_sums(self, w, slots, col, blk_tab, tab, ACC, Beside):
        nc = self.nc
        n = self.sem
        s_in, s_idx, s_turn, s_oh, s_pv, s_acc = (n(f"{w}_{x}") for x in ("in", "idx", "turn", "oh", "pv", "acc"))
        s_got = self.soft_sems(w + "_got", U)
        LB = (NTL // U - 1) // NT
        assert 1 + LB * NT == NTL // U
        with ExitStack() as c:
            SL = self.sb(c, w + "_SL", [P, NTL, 4])
            idx = self.sb(c, w + "_idx", [P, 2, U // 2], I32)
            FG, oh = self.sb(c, w + "_FG", [P, U, D]), self.sb(c, w + "_oh", [P, U, P])
            pf = [self.pb(c, f"{w}_pf{b}", [P, D]) for b in range(4)]
            L = Beside(self, c, LB)
            with nc.Block() as block:

                @block.sync
                def _(sp):
                    sp.dma_start(SL[:, :, :], slots.rearrange("(p t) c -> p t c", p=P)).then_inc(s_in, 16)
                    L.load(sp)

                @block.gpsimd
                def _(pool):
                    L.mask(pool)

                    def step(i, u):
                        on, t, r = tile(i, u, 0, U, NTL)
                        if on:
                            need(pool, s_pv, t - (U - 1))
                            if r % (U // 2) == 0:
                                pool.wait_ge(s_idx, i * 2 + (1 + r // (U // 2)))
                            pool.sem_inc(s_turn, 1)
                            pool.indirect_dma_start(FG[:, r, :], None, tab, bass.IndirectOffsetOnAxis(idx[:, r // (U // 2), ds(r % (U // 2), 1)], 0)).then_inc(s_got[r], 16)
                    steps(pool, NTL, U, 0, step)

                @block.vector
                def _(dve):
                    dve.memset(ACC[:, :, :], 0.0)
                    L.set_up(dve)
                    dve.wait_ge(s_in, 16)
                    dve.drain()
                    regs = [dve.alloc_register(f"{w}_dblk{j}") for j in range(U)]
                    blk = [None]

                    def step(i, u):
                        if u % U == 0:
                            blk[0] = self.load_blocks(dve, regs, blk_tab, i + u // U, 2)
                        on, t, r = tile(i, u, 0, U, NTL)
                        if on:
                            need(dve, s_pv, t - (U - 1))
                            dve.tensor_scalar(oh[:, r, :], self.iota_t[:, 0:P], SL[:, at(t), 1], SL[:, at(t), col], ALU.is_equal, ALU.mult).then_inc(s_oh, 1)
                        on, t, r = tile(i, u, 2, U, NTL)
                        if on:
                            k = blk[0][u % U]
                            dve.wait_ge(s_pv, t + 1)
                            need(dve, s_acc, t)
                            dve.tensor_tensor(ACC[:, at(k), :], ACC[:, at(k), :], pf[r % 4][:, :], ALU.add).then_inc(s_acc, 1)
                    self.steps_beside(dve, LB, 2, step, L.on_dve)
                    L.finish_dve(dve)

                @block.scalar
                def _(act):
                    act.wait_ge(s_in, 16)
                    for h in range(2):
                        self.refill(act, 0, h, s_got, s_idx, idx, SL)
                    with act.Fori(0, NT) as T:
                        for q in range(LB):
                            for h in range(2):
                                self.refill(act, T * LB + (q + 1), h, s_got, s_idx, idx, SL)
                            L.on_act(act, T, q)

                @block.tensor
                def _(pe):
                    def step(i, u):
                        on, t, r = tile(i, u, 0, U, NTL)
                        if on:
                            pe.wait_ge(s_oh, t + 1)
                            pe.wait_ge(s_got[r], i * 16 + 16)
                            need(pe, s_acc, t - 3)
                            pe.matmul(pf[r % 4][:, :], oh[:, r, :], FG[:, r, :], start=True, stop=True).then_inc(s_pv, 1)
                    L.ready(pe)
                    self.steps_beside(pe, LB, 0, step, L.on_pe)
                    L.finish_pe(pe)

    def steps_beside(self, eng, LB, lag, step, other):
        for u in range(U):
            step(0, u)
        with eng.Fori(0, NT) as T:
            for q in range(LB):
                for u in range(U):
                    step(T * LB + (q + 1), u)
                    other(eng, T, q, u)
        for u in range(lag):
            step(NTL // U, u)

    def gates(self, HB, AIN, AOUT):
        nc, a, XN, RES = self.nc, self.a, self.XN, self.RES
        n = self.sem
        s_in, s_row, s_tr, s_tt, s_mm, s_z, s_gt, s_dn = (n(f"g_{x}") for x in ("in", "row", "tr", "tt", "mm", "z", "gt", "dn"))
        with ExitStack() as c:
            sb = lambda name, shape, dt=F32: self.sb(c, "g_" + name, shape, dt)
            pb = lambda name, shape, dt=F32: self.pb(c, "g_" + name, shape, dt)
            W = sb("W", [P, 2, 2 * D])
            row, rowT = sb("rows", [P, 2, D]), sb("rowT", [P, 2, 2, P])
            z, g = sb("z", [P, 2, 2 * D]), sb("gates", [P, 2, 2 * D])
            pt = [pb(f"pt{b}", [P, 2, P]) for b in range(2)]
            pg = [pb(f"pg{b}", [P, 2 * D]) for b in range(2)]
            with nc.Block() as block:

                @block.sync
                def _(sp):
                    sp.dma_start(W[:, :, :], a["L1_gnn_W_x2i"][D:, :].rearrange("(c p) f -> p c f", p=P)).then_inc(s_in, 16)

                @block.vector
                def _(dve):
                    def step(i, u):
                        on, t, r = tile(i, u, 0, NU, NT)
                        if on:
                            need(dve, s_tr, t - 1)
                            dve.tensor_copy(row[:, r % 2, :], AOUT[:, at(t), :]).then_inc(s_row, 1)
                        on, t, r = tile(i, u, 2, NU, NT)
                        if on:
                            b = r % 2
                            dve.wait_ge(s_mm, t + 1)
                            need(dve, s_gt, t - 1)
                            dve.tensor_tensor(z[:, b, 0:D], AIN[:, at(t), :], pg[b][:, 0:D], ALU.add)
                            dve.tensor_tensor(z[:, b, D:], XN[:, at(t), :], pg[b][:, D:], ALU.add).then_inc(s_z, 1)
                        on, t, r = tile(i, u, 3, NU, NT)
                        if on:
                            b = r % 2
                            dve.wait_ge(s_gt, t + 1)
                            dve.tensor_tensor(HB[:, at(t), :], HB[:, at(t), :], g[:, b, D:], ALU.subtract)
                            dve.tensor_tensor(RES[:, at(t), :], RES[:, at(t), :], g[:, b, D:], ALU.add)
                            dve.drain()
                            dve.tensor_tensor(HB[:, at(t), :], HB[:, at(t), :], g[:, b, 0:D], ALU.mult).then_inc(s_dn, 1)
                            dve.drain()
                            dve.tensor_tensor(RES[:, at(t), :], RES[:, at(t), :], HB[:, at(t), :], ALU.add)
                    steps(dve, NT, NU, 3, step)

                @block.scalar
                def _(act):
                    def step(i, u):
                        on, t, r = tile(i, u, 0, NU, NT)
                        if on:
                            act.wait_ge(s_tr, t + 1)
                            need(act, s_mm, t - 1)
                            act.activation(rowT[:, r % 2, :, :], pt[r % 2][:, :, :], ACT.Copy).then_inc(s_tt, 1)
                        on, t, r = tile(i, u, 2, NU, NT)
                        if on:
                            b = r % 2
                            act.wait_ge(s_z, t + 1)
                            need(act, s_dn, t - 1)
                            act.activation(g[:, b, 0:D], z[:, b, 0:D], ACT.Sigmoid)
                            act.activation(g[:, b, D:], z[:, b, D:], ACT.Tanh).then_inc(s_gt, 1)
                    steps(act, NT, NU, 2, step)

                @block.tensor
                def _(pe):
                    pe.wait_ge(s_in, 16)

                    def step(i, u):
                        on, t, r = tile(i, u, 0, NU, NT)
                        if on:
                            b = r % 2
                            pe.wait_ge(s_row, t + 1)
                            need(pe, s_tt, t - 1)
                            pe.transpose(pt[b][:, 0, :], row[:, b, 0:P], self.identf[:, :])
                            pe.transpose(pt[b][:, 1, :], row[:, b, P:], self.identf[:, :]).then_inc(s_tr, 1)
                        on, t, r = tile(i, u, 1, NU, NT)
                        if on:
                            b = r % 2
                            pe.wait_ge(s_tt, t + 1)
                            need(pe, s_z, t - 1)
                            for ch in range(2):
                                last = pe.matmul(pg[b][:, :], rowT[:, b, ch, :], W[:, ch, :], start=ch == 0, stop=ch == 1)
                            last.then_inc(s_mm, 1)
                    steps(pe, NT, NU, 1, step)

    def last_ffn(self, w_tab, out):
        nc, a, XN, RES = self.nc, self.a, self.XN, self.RES
        FF, FC, GT = 1024, 8, 5
        NG, GH = NT // GT, GT * P // 2
        KEEP = max(1, N // 2) - 1
        n = self.sem
        s_in, s_row, s_tr, s_tt, s_u, s_gel, s_y, s_yr, s_res, s_out = (n(f"f_{x}") for x in ("in", "row", "tr", "tt", "u", "gel", "y", "yr", "res", "out"))
        s_wr, s_w, s_st, s_ld, s_gm, s_gt, s_g1, s_gb, s_cd, s_pf = (n(f"k_{x}") for x in ("wr", "w", "st", "ld", "gm", "gt", "g1", "gb", "cd", "pf"))
        with ExitStack() as c:
            sb = lambda name, shape, dt=F32: self.sb(c, "f_" + name, shape, dt)
            pb = lambda name, shape, dt=F32: self.pb(c, "f_" + name, shape, dt)
            W1, W2, bf, brow = sb("W1", [P, 2, FF]), sb("W2", [P, FC, D]), sb("bf", [P, FC]), sb("brow", [1, D])
            row, hT, G1 = sb("rows", [P, 2, D]), sb("hT", [P, 2, GT * P]), sb("G1", [P, FC, GT * P])
            Y, WSEL = sb("Y", [P, NT, D]), sb("WSEL", [P, NT])
            wr, br, prod = sb("wr", [P, D]), sb("br", [P, 1]), sb("prod", [P, 4, D])
            w, wc, off = sb("w", [P, NT]), sb("wc", [P, NT]), sb("off", [P, 1])
            ROW, HIT = sb("ROW", [P, NT * P]), sb("HIT", [P, NT * P])
            G, GA, GK, gm, g1 = sb("G", [P, NT]), sb("GA", [P, NT]), sb("GK", [P, NT]), sb("gm", [P, 1]), sb("g1", [1, 1])
            gs, cand, pre, cum, left = sb("gs", [P, 1]), sb("cand", [P, NT]), sb("pre", [P, NT]), sb("cum", [P, NT]), sb("left", [P, 1])
            pt = [pb(f"pt{b}", [P, 2, P]) for b in range(2)]
            pu = [pb(f"pu{b}", [P, GH]) for b in range(4)]
            py = [pb(f"py{b}", [P, D]) for b in range(2)]
            pgm, pgb, ppf = pt[0][0:1, 0, :], pt[1][:, 0, 0:1], pu[0][:, 0:2 * NT]
            with nc.Block() as block:

                @block.sync
                def _(sp):
                    sp.dma_start(W1[:, :, :], a["L1_ffn_w1"].rearrange("(c p) f -> p c f", p=P)).then_inc(s_in, 16)
                    sp.dma_start(W2[:, :, :], a["L1_ffn_w2"].rearrange("(c p) f -> p c f", p=P)).then_inc(s_in, 16)
                    sp.dma_start(bf[:, :], a["L1_ffn_b1"].rearrange("(c p) -> p c", p=P)).then_inc(s_in, 16)
                    sp.dma_start(brow[:, :], a["L1_ffn_b2"].partition_broadcast(1)).then_inc(s_in, 16)
                    sp.dma_start(wr[:, :], a["L1_ffn_wr"].rearrange("d o -> (d o)").partition_broadcast(P)).then_inc(s_wr, 16)
                    sp.dma_start(br[:, :], a["L1_ffn_br"].partition_broadcast(P)).then_inc(s_wr, 16)
                    sp.wait_ge(s_w, 1)
                    sp.dma_start(w_tab.rearrange("(t p) -> p t", p=P), wc[:, :]).then_inc(s_st, 16)
                    sp.wait_ge(s_st, 16)
                    sp.dma_start(ROW[:, :], w_tab.partition_broadcast(P)).then_inc(s_ld, 16)
                    for g in range(NG):
                        sp.wait_ge(s_res, (g + 1) * GT)
                        k = GT if g < NG - 1 else GT - 1
                        sp.dma_start(out[g * GT * P:(g * GT + k) * P, :].rearrange("(t p) d -> p t d", p=P), RES[:, g * GT:g * GT + k, :]).then_inc(s_out, 16)
                    sp.dma_start(out[(NT - 1) * P:N, :], RES[0:TAIL, NT - 1, :]).then_inc(s_out, 16)
                    sp.wait_ge(s_out, 16 * (NG + 1))

                @block.vector
                def _(dve):
                    dve.wait_ge(s_wr, 32)
                    with dve.Fori(0, NT) as t:
                        dve.tensor_tensor(RES[:, at(t), :], RES[:, at(t), :], XN[:, at(t), :], ALU.add)
                        dve.tensor_tensor(prod[:, 0, :], XN[:, at(t), :], wr[:, :], ALU.mult)
                        dve.drain()
                        dve.tensor_reduce(w[:, at(t)], prod[:, 0, :], AX.X, ALU.add)
                        dve.drain()
                    dve.tensor_scalar(w[:, :], w[:, :], br[:, :], None, ALU.add)
                    dve.tensor_scalar(off[:, :], self.lower[:, TAIL:TAIL + 1], BIG, -BIG, ALU.mult, ALU.add)
                    dve.drain()
                    dve.tensor_copy(wc[:, :], w[:, :])
                    dve.drain()
                    dve.tensor_scalar(wc[:, NT - 1:], wc[:, NT - 1:], self.lower[:, TAIL:TAIL + 1], off[:, :], ALU.mult, ALU.add)
                    dve.drain()
                    dve.sem_inc(s_w, 1)
                    dve.wait_ge(s_ld, 16)
                    for t in range(NT):
                        dve.tensor_scalar(HIT[:, :], ROW[:, :], wc[:, t:t + 1], None, ALU.is_gt, ALU.add, accum_out=G[:, t:t + 1])
                        dve.drain()
                    dve.tensor_scalar(GA[:, :], G[:, :], float(KEEP), None, ALU.is_lt)
                    dve.tensor_scalar(GK[:, :], G[:, :], 1.0, None, ALU.add)
                    dve.drain()
                    dve.tensor_tensor(GK[:, :], GK[:, :], GA[:, :], ALU.mult)
                    dve.drain()
                    dve.tensor_reduce(gm[:, :], GK[:, :], AX.X, ALU.max).then_inc(s_gm, 1)
                    dve.wait_ge(s_gt, 1)
                    dve.tensor_reduce(g1[:, :], pgm, AX.X, ALU.max).then_inc(s_g1, 1)
                    dve.wait_ge(s_gb, 1)
                    dve.tensor_scalar(gs[:, :], pgb, -1.0, None, ALU.add)
                    dve.drain()
                    dve.tensor_scalar(left[:, :], gs[:, :], -1.0, float(KEEP), ALU.mult, ALU.add)
                    dve.tensor_scalar(cand[:, :], G[:, :], gs[:, :], None, ALU.is_equal).then_inc(s_cd, 1)
                    dve.tensor_scalar(GA[:, :], G[:, :], gs[:, :], None, ALU.is_lt)
                    dve.wait_ge(s_pf, 1)
                    dve.tensor_copy(pre[:, :], ppf[:, NT:2 * NT])
                    dve.drain()
                    dve.tensor_tensor_scan(cum[:, :], pre[:, :], self.zeros[:, 0:NT], 0.0, ALU.add, ALU.add)
                    dve.drain()
                    dve.tensor_tensor(cum[:, :], cum[:, :], pre[:, :], ALU.subtract)
                    dve.drain()
                    dve.tensor_tensor(cum[:, :], cum[:, :], ppf[:, 0:NT], ALU.add)
                    dve.drain()
                    dve.scalar_tensor_tensor(out=cum[:, :], in0=cum[:, :], scalar=left[:, :], in1=cand[:, :], op0=ALU.is_lt, op1=ALU.mult)
                    dve.drain()
                    dve.tensor_tensor(GA[:, :], GA[:, :], cum[:, :], ALU.add)
                    dve.drain()
                    dve.tensor_tensor(WSEL[:, :], GA[:, :], w[:, :], ALU.mult)
                    dve.wait_ge(s_yr, NT)
                    dve.drain()
                    with dve.Fori(0, NT) as t:
                        dve.scalar_tensor_tensor(out=RES[:, at(t), :], in0=Y[:, at(t), :], scalar=WSEL[:, at(t)], in1=RES[:, at(t), :],
                                                 op0=ALU.mult, op1=ALU.add).then_inc(s_res, 1)

                @block.scalar
                def _(act):
                    act.wait_ge(s_in, 64)

                    def step(i, u):
                        on, g, _ = tile(i, u, 0, 1, NG)
                        if on:
                            need(act, s_u, g * (2 * FC))
                            for j in range(GT + 1):
                                if j < GT:
                                    need(act, s_tr, g * GT + (j - 1) if j else g * GT)
                                    act.activation(row[:, j % 2, :], XN[:, at(g * GT + j), :], ACT.Copy).then_inc(s_row, 1)
                                if j:
                                    act.wait_ge(s_tr, g * GT + j)
                                    act.activation(hT[:, :, (j - 1) * P:j * P], pt[(j - 1) % 2][:, :, :], ACT.Copy).then_inc(s_tt, 1)
                        on, gy, _ = tile(i, u, 1, 1, NG)
                        if on:
                            for j in range(GT):
                                act.wait_ge(s_y, gy * GT + (j + 1))
                                act.activation(Y[:, at(gy * GT + j), :], py[j % 2][:, :], ACT.Copy).then_inc(s_yr, 1)
                        if tile(i, u, 0, 1, NG)[0]:
                            for f in range(FC):
                                for h in range(2):
                                    act.wait_ge(s_u, g * (2 * FC) + (2 * f + h + 1))
                                    act.activation(G1[:, f, h * GH:(h + 1) * GH], pu[2 * (f % 2) + h][:, :], ACT.Gelu_apprx_tanh, bias=bf[:, f:f + 1]).then_inc(s_gel, 1)
                    steps(act, NG, 1, 1, step)

                @block.tensor
                def _(pe):
                    pe.wait_ge(s_in, 64)

                    def step(i, u):
                        on, g, _ = tile(i, u, 0, 1, NG)
                        if on:
                            for j in range(GT):
                                t = g * GT + j
                                pe.wait_ge(s_row, t + 1)
                                need(pe, s_tt, t - 1 if j else t)
                                pe.transpose(pt[j % 2][:, 0, :], row[:, j % 2, 0:P], self.identf[:, :])
                                pe.transpose(pt[j % 2][:, 1, :], row[:, j % 2, P:], self.identf[:, :]).then_inc(s_tr, 1)
                        on, gy, _ = tile(i, u, 1, 1, NG)
                        if on:
                            pe.wait_ge(s_gel, (gy + 1) * (2 * FC))
                            for j in range(GT):
                                t = gy * GT + j
                                need(pe, s_yr,  t - 1 if j else t)
                                pe.matmul(py[j % 2][:, :], self.ones[0:1, :], brow[:, :], start=True, stop=False)
                                for f in range(FC):
                                    last = pe.matmul(py[j % 2][:, :], G1[:, f, j * P:(j + 1) * P], W2[:, f, :], start=False, stop=f == FC - 1)
                                last.then_inc(s_y, 1)
                        on, g, _ = tile(i, u, 0, 1, NG)
                        if on:
                            pe.wait_ge(s_tt, (g + 1) * GT)
                            for f in range(FC):
                                for h in range(2):
                                    need(pe, s_gel, g * (2 * FC) + (2 * f + h - 3))
                                    for ch in range(2):
                                        last = pe.matmul(pu[2 * (f % 2) + h][:, :], W1[:, ch, f * P:(f + 1) * P], hT[:, ch, h * GH:(h + 1) * GH],
                                                         start=ch == 0, stop=ch == 1)
                                    last.then_inc(s_u, 1)
                    steps(pe, NG, 1, 1, step)
                    pe.wait_ge(s_yr, NT)
                    pe.wait_ge(s_gm, 1)
                    pe.transpose(pgm, gm[:, :], self.identf[:, :]).then_inc(s_gt, 1)
                    pe.wait_ge(s_g1, 1)
                    pe.matmul(pgb, self.ones[0:1, :], g1[:, :], start=True, stop=True).then_inc(s_gb, 1)
                    pe.wait_ge(s_cd, 1)
                    pe.matmul(ppf[:, 0:NT], self.lower[:, :], cand[:, :], start=True, stop=True)
                    pe.matmul(ppf[:, NT:2 * NT], self.ones[:, :], cand[:, :], start=True, stop=True).then_inc(s_pf, 1)

    def run(self, out):
        a = self.a
        self.k_tab, self.v_tab = self.dram("k_tab", [NT * P, D]), self.dram("v_tab", [NT * P, D])
        by_dst, by_src = self.dram("by_dst", [P * NTL, 4]), self.dram("by_src", [P * NTL, 4])
        self.stage(self.constants)
        self.blk_dst = self.sb(self.ctx, "blk_dst", [1, NTL + 2 * U], I32)
        self.blk_src = self.sb(self.ctx, "blk_src", [1, NTL + 2 * U], I32)
        self.XN = self.sb(self.ctx, "XN", [P, NT, D])
        self.RES = self.sb(self.ctx, "RES", [P, NT, D])
        with ExitStack() as by_source:
            self.stage(self.norm_x)
            with ExitStack() as by_node:
                self.stage(self.bucket, by_source, "bs", a["src"], a["dst"], [a["edge_weight_n2"]], by_src, self.blk_src)
                self.stage(self.bucket, by_node, "bd", a["dst"], a["src"], [a["edge_type_64"], a["edge_weight"]], by_dst, self.blk_dst)
                self.stage(self.mix0)
            with ExitStack() as att:
                self.QS = self.sb(att, "QS", [P, NT, 3, D], BF16)
                self.VS = self.sb(att, "VS", [P, NT, D])
                self.stage(self.project)
                with ExitStack() as slots:
                    self.stage(self.att_scores, slots, by_dst)
                    self.ACC = self.QS[:, :, :, :].rearrange("p t j d -> p (t j d)").bitcast(F32)[:, 0:NT * (D + HEADS)].rearrange("p (t d) -> p t d", t=NT)
                    self.stage(self.att_sums)
                self.stage(self.att_out)
            xs_tab, ys_tab = self.dram("xs_tab", [XT * P, D]), self.dram("ys_tab", [XT * P, D])
            self.stage(self.norm_rows, "n1")
            with ExitStack() as moe:
                self.stage(self.route, moe, xs_tab)
                self.stage(self.experts, xs_tab, ys_tab)
                self.stage(self.combine, ys_tab)
        with ExitStack() as l1:
            HB = self.sb(l1, "HB", [P, NT, D])
            AIN, AOUT = self.sb(l1, "AIN", [P, NT, D]), self.sb(l1, "AOUT", [P, NT, D])
            self.HB, self.AIN, self.M2 = HB, AIN, self.sb(l1, "M2", [P, 2, D])
            fi_tab, fo_tab = self.dram("fi_tab", [NT * P, D]), self.dram("fo_tab", [NT * P, D])
            self.stage(self.norm_rows, "n2")
            self.stage(self.batch_norm, HB, (fi_tab, fo_tab))
            self.stage(self.edge_sums, "ei", by_dst, 3, self.blk_dst, fi_tab, AIN, LinAtt)
            self.stage(self.edge_sums, "eo", by_src, 2, self.blk_src, fo_tab, AOUT, GateIn)
            self.stage(self.gates, HB, AIN, AOUT)
        self.stage(self.norm_rows, "n3")
        w_tab = self.dram("w_tab", [NT * P])
        self.stage(self.last_ffn, w_tab, out)



def build(nc, a, out):
    k = Kernel(nc, a)
    with k.ctx, nc.allow_non_contiguous_dma(reason="small vectors, one element per partition"):
        k.run(out)


def kernel(**inputs):
    import numpy as np
    import concourse.bacc as bacc
    from concourse.bass_utils import run_bass_kernel_spmd

    arrays = {k: np.ascontiguousarray(v) for k, v in inputs.items() if k != "L1_ffn_attention_mask"}
    for x in ("Wqkv", "Wout"):
        arrays[f"L1_mix_{x}T"] = np.ascontiguousarray(arrays[f"L1_mix_{x}"].T)
    nc = bacc.Bacc("TRN2", target_bir_lowering=False, num_devices=1)
    a = {k: nc.dram_tensor(f"in_{k}", v.shape, mybir.dt.from_np(v.dtype), kind="ExternalInput").ap() for k, v in arrays.items()}
    out = nc.dram_tensor("out_0_dram", (N, D), F32, kind="ExternalOutput").ap()
    build(nc, a, out)
    r = run_bass_kernel_spmd(nc, [{f"in_{k}": v for k, v in arrays.items()}], core_ids=[0])
    return r.results[0]["out_0_dram"]
```
